# Optimizing a Trainium2 kernel written in Bass

```python
import numpy as np
import jax
import jax.numpy as jnp

def _softmax(x, axis=-1):
    return jax.nn.softmax(x, axis=axis)

def _gelu(x):
    return jax.nn.gelu(x, approximate=True)

def _silu(x):
    return jax.nn.silu(x)

def _sigmoid(x):
    return jax.nn.sigmoid(x)

def _layernorm(x, axis=-1, eps=1e-05):
    m = jnp.mean(x, axis=axis, keepdims=True)
    v = jnp.var(x, axis=axis, keepdims=True)
    return (x - m) / jnp.sqrt(v + eps)

def _scatter_add(tgt, idx, src, axis=0):
    return tgt.at[idx].add(src)

def _segment_sum(src, seg, n):
    return jax.ops.segment_sum(src, seg, n)
kernel_name = 'mk_prb_d2_jaxref_r8_f5e472'

def setup_inputs(seed: int=0):
    np.random.seed(seed)
    _w = jnp.asarray

    def _L0_attn_setup():
        import jax, jax.numpy as jnp
        import numpy as np
        D = 128
        FF = 512
        EPS = 1e-06

        def _linear(x, w, b):
            return jnp.einsum('bld,fd->blf', x, w) + b

        def _rmsnorm(x, g):
            xf = x.astype(jnp.float32)
            out = xf * jax.lax.rsqrt(jnp.mean(xf * xf, axis=-1, keepdims=True) + EPS)
            return out.astype(x.dtype) * g

        def _silu(x):
            return x * jax.nn.sigmoid(x)
        key = jax.random.key(seed)
        ks = jax.random.split(key, 20)
        sd = 1.0 / np.sqrt(D)
        sf = 1.0 / np.sqrt(FF)
        inp = {'x': jax.random.normal(ks[0], (4, 512, D), jnp.float32), 'w_ln_z': jax.random.uniform(ks[1], (D, D), jnp.float32, -sd, sd), 'b_ln_z': jax.random.uniform(ks[2], (D,), jnp.float32, -sd, sd), 'w_dt': jax.random.uniform(ks[3], (D, D), jnp.float32, -sd, sd), 'b_dt': jax.random.uniform(ks[4], (D,), jnp.float32, -sd, sd), 'w_y': jax.random.uniform(ks[5], (D, D), jnp.float32, -sd, sd), 'b_y': jax.random.uniform(ks[6], (D,), jnp.float32, -sd, sd), 'w_yact': jax.random.uniform(ks[7], (D, D), jnp.float32, -sd, sd), 'b_yact': jax.random.uniform(ks[8], (D,), jnp.float32, -sd, sd), 'h0': jax.random.normal(ks[9], (D,), jnp.float32), 'w_fc': jax.random.uniform(ks[10], (FF, D), jnp.float32, -sd, sd), 'b_fc': jax.random.uniform(ks[11], (FF,), jnp.float32, -sd, sd), 'w_fcact': jax.random.uniform(ks[12], (FF, D), jnp.float32, -sd, sd), 'b_fcact': jax.random.uniform(ks[13], (FF,), jnp.float32, -sd, sd), 'w_out': jax.random.uniform(ks[14], (D, FF), jnp.float32, -sf, sf), 'b_out': jax.random.uniform(ks[15], (D,), jnp.float32, -sf, sf), 'g_sio': jnp.ones((D,), jnp.float32), 'g_ffn': jnp.ones((D,), jnp.float32)}
        return inp
    _L0_attn_in = _L0_attn_setup()

    def _L0_ffn_setup():
        import jax, jax.numpy as jnp
        import numpy as np
        FEATURES = 128
        D_IN = 128

        def fp8_gemm_optimized(x, input_scale, kernel, kernel_scale):
            s_in = input_scale[0]
            s_k = kernel_scale[0]
            x_q = (x.astype(jnp.float32) / s_in).astype(jnp.float8_e4m3fn)
            k_q = (kernel.astype(jnp.float32) / s_k).astype(jnp.float8_e4m3fn)
            y = jnp.dot(x_q.astype(jnp.float32), k_q.astype(jnp.float32), preferred_element_type=jnp.float32)
            return y * (s_in * s_k)
        key = jax.random.key(seed)
        kx, kk, kb = jax.random.split(key, 3)
        x = jax.random.normal(kx, (4, 1024, D_IN), dtype=jnp.float32)
        limit = np.sqrt(6.0 / (D_IN + FEATURES)).astype(np.float32)
        kernel = jax.random.uniform(kk, (D_IN, FEATURES), dtype=jnp.float32, minval=-limit, maxval=limit).astype(jnp.bfloat16)
        input_scale = jnp.ones((1,), dtype=jnp.float32)
        kernel_scale = jnp.ones((1,), dtype=jnp.float32)
        bias = jnp.zeros((FEATURES,), dtype=jnp.bfloat16)
        return {'x': x, 'kernel': kernel, 'input_scale': input_scale, 'kernel_scale': kernel_scale, 'bias': bias}
    _L0_ffn_in = _L0_ffn_setup()

    def _L1_attn_setup():
        import jax, jax.numpy as jnp
        import numpy as np
        N_HEAD = 16
        PAGE_SIZE = 32
        ROPE_THETA = 10000.0

        def _rope_tables(T, D, dtype):
            inv = 1.0 / ROPE_THETA ** (np.arange(0, D, 2, dtype=np.float32) / D)
            ang = np.outer(np.arange(T, dtype=np.float32), inv)
            return (jnp.asarray(np.cos(ang), dtype), jnp.asarray(np.sin(ang), dtype))

        def _apply_rope(x, cos, sin):
            x1 = x[..., 0::2]
            x2 = x[..., 1::2]
            c = cos[None, :, None, :]
            s = sin[None, :, None, :]
            out = jnp.stack([x1 * c - x2 * s, x1 * s + x2 * c], axis=-1)
            return out.reshape(x.shape)
        key = jax.random.key(seed)
        ks = jax.random.split(key, 6)
        B, T, E = (2, 256, 128)
        L = E // 2
        sc = lambda fan: 1.0 / np.sqrt(fan)
        return {'x': jax.random.normal(ks[0], (B, T, E), jnp.float32), 'wq': jax.random.normal(ks[1], (E, E), jnp.float32) * sc(E), 'w_down': jax.random.normal(ks[2], (E, L), jnp.float32) * sc(E), 'wk_up': jax.random.normal(ks[3], (L, E), jnp.float32) * sc(L), 'wv_up': jax.random.normal(ks[4], (L, E), jnp.float32) * sc(L), 'wo': jax.random.normal(ks[5], (E, E), jnp.float32) * sc(E)}
    _L1_attn_in = _L1_attn_setup()

    def _L1_ffn_setup():
        import jax, jax.numpy as jnp
        import numpy as np
        NUM_EXPERTS = 8
        HIDDEN = 128
        FFN = 512
        BATCH = 2
        SEQ = 256
        key = jax.random.key(seed)
        k_x, k_g, k_u, k_d = jax.random.split(key, 4)
        scale_in = 1.0 / np.sqrt(HIDDEN)
        scale_mid = 1.0 / np.sqrt(FFN)
        return {'hidden_states': jax.random.normal(k_x, (BATCH, SEQ, HIDDEN), dtype=jnp.float32), 'Wg': jax.random.normal(k_g, (NUM_EXPERTS, HIDDEN, FFN), dtype=jnp.float32) * scale_in, 'Wu': jax.random.normal(k_u, (NUM_EXPERTS, HIDDEN, FFN), dtype=jnp.float32) * scale_in, 'Wd': jax.random.normal(k_d, (NUM_EXPERTS, FFN, HIDDEN), dtype=jnp.float32) * scale_mid}
    _L1_ffn_in = _L1_ffn_setup()
    _d = {'L0_attn_x': _L0_attn_in['x'], 'L0_attn_w_ln_z': _L0_attn_in['w_ln_z'], 'L0_attn_b_ln_z': _L0_attn_in['b_ln_z'], 'L0_attn_w_dt': _L0_attn_in['w_dt'], 'L0_attn_b_dt': _L0_attn_in['b_dt'], 'L0_attn_w_y': _L0_attn_in['w_y'], 'L0_attn_b_y': _L0_attn_in['b_y'], 'L0_attn_w_yact': _L0_attn_in['w_yact'], 'L0_attn_b_yact': _L0_attn_in['b_yact'], 'L0_attn_h0': _L0_attn_in['h0'], 'L0_attn_w_fc': _L0_attn_in['w_fc'], 'L0_attn_b_fc': _L0_attn_in['b_fc'], 'L0_attn_w_fcact': _L0_attn_in['w_fcact'], 'L0_attn_b_fcact': _L0_attn_in['b_fcact'], 'L0_attn_w_out': _L0_attn_in['w_out'], 'L0_attn_b_out': _L0_attn_in['b_out'], 'L0_attn_g_sio': _L0_attn_in['g_sio'], 'L0_attn_g_ffn': _L0_attn_in['g_ffn'], 'L0_ffn_kernel': _L0_ffn_in['kernel'], 'L0_ffn_input_scale': _L0_ffn_in['input_scale'], 'L0_ffn_kernel_scale': _L0_ffn_in['kernel_scale'], 'L0_ffn_bias': _L0_ffn_in['bias'], 'L1_attn_wq': _L1_attn_in['wq'], 'L1_attn_w_down': _L1_attn_in['w_down'], 'L1_attn_wk_up': _L1_attn_in['wk_up'], 'L1_attn_wv_up': _L1_attn_in['wv_up'], 'L1_attn_wo': _L1_attn_in['wo'], 'L1_ffn_Wg': _L1_ffn_in['Wg'], 'L1_ffn_Wu': _L1_ffn_in['Wu'], 'L1_ffn_Wd': _L1_ffn_in['Wd']}
    _x0 = _d['L0_attn_x']
    _d['L0_attn_x'] = jax.random.normal(jax.random.fold_in(jax.random.key(seed), 1), (4, 1024, 128), dtype=_x0.dtype)
    del _x0
    return _d

def reference(L0_attn_x, L0_attn_w_ln_z, L0_attn_b_ln_z, L0_attn_w_dt, L0_attn_b_dt, L0_attn_w_y, L0_attn_b_y, L0_attn_w_yact, L0_attn_b_yact, L0_attn_h0, L0_attn_w_fc, L0_attn_b_fc, L0_attn_w_fcact, L0_attn_b_fcact, L0_attn_w_out, L0_attn_b_out, L0_attn_g_sio, L0_attn_g_ffn, L0_ffn_kernel, L0_ffn_input_scale, L0_ffn_kernel_scale, L0_ffn_bias, L1_attn_wq, L1_attn_w_down, L1_attn_wk_up, L1_attn_wv_up, L1_attn_wo, L1_ffn_Wg, L1_ffn_Wu, L1_ffn_Wd):

    def _L0_attn_ref(x, w_ln_z, b_ln_z, w_dt, b_dt, w_y, b_y, w_yact, b_yact, h0, w_fc, b_fc, w_fcact, b_fcact, w_out, b_out, g_sio, g_ffn):
        import jax, jax.numpy as jnp
        import numpy as np
        D = 128
        FF = 512
        EPS = 1e-06

        def _linear(x, w, b):
            return jnp.einsum('bld,fd->blf', x, w) + b

        def _rmsnorm(x, g):
            xf = x.astype(jnp.float32)
            out = xf * jax.lax.rsqrt(jnp.mean(xf * xf, axis=-1, keepdims=True) + EPS)
            return out.astype(x.dtype) * g

        def _silu(x):
            return x * jax.nn.sigmoid(x)
        xn = _rmsnorm(x, g_sio)
        ln_z = -jax.nn.softplus(-_linear(xn, w_ln_z, b_ln_z))
        dt = _linear(xn, w_dt, b_dt)
        ln_da = -jax.nn.softplus(-dt)
        ln_o_da = -jax.nn.softplus(dt)
        ln_o_da_cumsum = jnp.cumsum(ln_o_da, axis=1)
        lcse = jax.lax.cumlogsumexp(ln_z + ln_da - ln_o_da_cumsum, axis=1)
        h_inner = jnp.exp(lcse + ln_o_da_cumsum)
        h_cross = jnp.exp(ln_o_da_cumsum) * h0[None, None, :]
        h = h_inner + h_cross
        y = _linear(h, w_y, b_y) * _silu(_linear(xn, w_yact, b_yact))
        x = x + y
        xn2 = _rmsnorm(x, g_ffn)
        hid = _linear(xn2, w_fc, b_fc) * _silu(_linear(xn2, w_fcact, b_fcact))
        return x + _linear(hid, w_out, b_out)

    def _L0_ffn_ref(x, kernel, input_scale, kernel_scale, bias):
        import jax, jax.numpy as jnp
        import numpy as np
        FEATURES = 128
        D_IN = 128

        def fp8_gemm_optimized(x, input_scale, kernel, kernel_scale):
            s_in = input_scale[0]
            s_k = kernel_scale[0]
            x_q = (x.astype(jnp.float32) / s_in).astype(jnp.float8_e4m3fn)
            k_q = (kernel.astype(jnp.float32) / s_k).astype(jnp.float8_e4m3fn)
            y = jnp.dot(x_q.astype(jnp.float32), k_q.astype(jnp.float32), preferred_element_type=jnp.float32)
            return y * (s_in * s_k)
        dtype = jnp.bfloat16
        x = x.astype(dtype)
        orig_shape = x.shape
        x2 = x.reshape(-1, x.shape[-1])
        y = fp8_gemm_optimized(x2, input_scale, kernel, kernel_scale)
        y = y.astype(dtype) + bias
        return y.reshape(orig_shape[:-1] + (FEATURES,))

    def _L1_attn_ref(x, wq, w_down, wk_up, wv_up, wo):
        import jax, jax.numpy as jnp
        import numpy as np
        N_HEAD = 16
        PAGE_SIZE = 32
        ROPE_THETA = 10000.0

        def _rope_tables(T, D, dtype):
            inv = 1.0 / ROPE_THETA ** (np.arange(0, D, 2, dtype=np.float32) / D)
            ang = np.outer(np.arange(T, dtype=np.float32), inv)
            return (jnp.asarray(np.cos(ang), dtype), jnp.asarray(np.sin(ang), dtype))

        def _apply_rope(x, cos, sin):
            x1 = x[..., 0::2]
            x2 = x[..., 1::2]
            c = cos[None, :, None, :]
            s = sin[None, :, None, :]
            out = jnp.stack([x1 * c - x2 * s, x1 * s + x2 * c], axis=-1)
            return out.reshape(x.shape)
        B, T, E = x.shape
        H = N_HEAD
        D = E // H
        q = (x @ wq).reshape(B, T, H, D)
        lat = x @ w_down
        k = (lat @ wk_up).reshape(B, T, H, D)
        v = (lat @ wv_up).reshape(B, T, H, D)
        cos, sin = _rope_tables(T, D, x.dtype)
        q = _apply_rope(q, cos, sin)
        k = _apply_rope(k, cos, sin)
        scale = 1.0 / jnp.sqrt(jnp.asarray(D, x.dtype))
        scores = jnp.einsum('bqhd,bkhd->bhqk', q, k) * scale
        pages = jnp.arange(T) // PAGE_SIZE
        allowed = pages[None, :] <= pages[:, None]
        scores = jnp.where(allowed[None, None], scores, jnp.finfo(scores.dtype).min)
        attn = jax.nn.softmax(scores, axis=-1)
        out = jnp.einsum('bhqk,bkhd->bqhd', attn, v).reshape(B, T, E)
        return out @ wo

    def _L1_ffn_ref(hidden_states, Wg, Wu, Wd):
        import jax, jax.numpy as jnp
        import numpy as np
        NUM_EXPERTS = 8
        HIDDEN = 128
        FFN = 512
        BATCH = 2
        SEQ = 256
        B, S, H = hidden_states.shape
        x = hidden_states.reshape(-1, H)

        def expert_step(acc, w):
            wg, wu, wd = w
            h = jax.nn.silu(x @ wg) * (x @ wu)
            return (acc + h @ wd, None)
        acc, _ = jax.lax.scan(expert_step, jnp.zeros_like(x), (Wg, Wu, Wd))
        return acc.reshape(B, S, H)
    x = L0_attn_x
    xn = _layernorm(x, axis=-1)
    x = x + _L0_attn_ref(xn, L0_attn_w_ln_z, L0_attn_b_ln_z, L0_attn_w_dt, L0_attn_b_dt, L0_attn_w_y, L0_attn_b_y, L0_attn_w_yact, L0_attn_b_yact, L0_attn_h0, L0_attn_w_fc, L0_attn_b_fc, L0_attn_w_fcact, L0_attn_b_fcact, L0_attn_w_out, L0_attn_b_out, L0_attn_g_sio, L0_attn_g_ffn) + _L0_ffn_ref(xn, L0_ffn_kernel, L0_ffn_input_scale, L0_ffn_kernel_scale, L0_ffn_bias)
    xn = _layernorm(x, axis=-1)
    x = x + _L1_attn_ref(xn, L1_attn_wq, L1_attn_w_down, L1_attn_wk_up, L1_attn_wv_up, L1_attn_wo) + _L1_ffn_ref(xn, L1_ffn_Wg, L1_ffn_Wu, L1_ffn_Wd)
    return x

_drawn_inputs = setup_inputs


def setup_inputs(seed=0):
    import zlib

    import numpy as np

    out = dict(_drawn_inputs(seed))
    spreads = {'L0_attn_g_sio': (1.0, 0.6), 'L0_attn_g_ffn': (1.0, 0.6), 'L0_ffn_bias': (0.0, 0.1)}
    factors = {'L0_attn_w_ln_z': 6.695,
     'L0_attn_b_ln_z': 64.0,
     'L0_attn_w_dt': 8.0,
     'L0_attn_b_dt': 64.0,
     'L0_attn_b_y': 6.076,
     'L0_attn_b_yact': 8.0,
     'L0_attn_h0': 8.0,
     'L0_attn_b_fc': 8.0,
     'L0_attn_b_fcact': 8.0,
     'L0_attn_b_out': 4.178}
    for name, (base, spread) in spreads.items():
        noise = np.random.default_rng([zlib.crc32(name.encode()), seed]).standard_normal(out[name].shape)
        drawn = base * np.exp(spread * noise) if base else spread * noise
        out[name] = jnp.asarray(drawn.astype(out[name].dtype))
    for name, factor in factors.items():
        out[name] = (out[name] * factor).astype(out[name].dtype)
    return out
```

```python
from contextlib import ExitStack

import numpy as np

import concourse.bass as bass
from concourse import mybir

F32 = mybir.dt.float32
F16 = mybir.dt.float16
BF16 = mybir.dt.bfloat16
U32 = mybir.dt.uint32
ALU = mybir.AluOpType
ACT = mybir.ActivationFunctionType
AX = mybir.AxisListType

P = 128
B, T = 4, 1024
NT = T // P
HT = NT // 2
HALF = T // 2
FF0 = 4
NE, FE = 8, 4
SLOTS = NE * FE * 2
LAT = 64
H, D = 16, 8
G = 4
NG = H // G
PAGE = 32
LN_EPS, RMS_EPS = 1e-5, 1e-6
SCALE = float(1.0 / np.sqrt(np.float32(D)))

MASK_ROW, MAX_ROW = 32, 96
S_ROWS, ST_ROWS = 96, 98
BIG = 60000.0

W_Z, W_DT, W_Y, W_YACT, W_FC, W_FCACT, W_OUT, NW0 = 0, 1, 2, 3, 4, 8, 12, 16
(V_BZ, V_BDT, V_NBDT, V_BY, V_BYACT, V_H0, V_GSIO, V_GFFN, V_BOUT, V_SIN, V_SK, V_RIN, V_RK, V_SC,
 V_BFC, V_BFCACT) = [*range(14), 14, 18]
NV = 22

PE_SLOT = {("xrT", 0): 5, ("xrT", 1): 6, ("z", 0): 7, ("z", 1): 8, ("dt", 0): 9, ("dt", 1): 10,
           ("yact", 0): 11, ("yact", 1): 12, ("qT", 0): 13, ("qT", 1): 14, ("y8", 0): 15, ("y8", 1): 16,
           ("y", 0): 17, ("y", 1): 18, ("ynat", 0): 19, ("ynat", 1): 20, ("xr2T", 0): 24, ("xr2T", 1): 25}
for _i in range(2 * FF0):
    PE_SLOT["fcact", _i] = 26 + 2 * _i
    PE_SLOT["fc", _i] = 27 + 2 * _i
PE_SLOT |= {("out", 0): 43, ("out", 1): 44, ("onat", 0): 45, ("onat", 1): 46, ("xT", 0): 50, ("xT", 1): 51,
            ("lat", 0): 52, ("lat", 1): 53, ("k", 0): 54, ("ks", 0): 55, ("k", 1): 56, ("ks", 1): 57,
            ("q", 0): 58, ("qs", 0): 59, ("q", 1): 60, ("qs", 1): 61, ("v", 0): 62, ("v", 1): 63}
AT_SLOT = {s: use for use, s in PE_SLOT.items()}
FRONT_USES = len(PE_SLOT)

S_USES = [[(0, 0, 128, 0), (2, 0, 384, 128)], [(1, 0, 256, 0), (5, 512, 256, 256)],
          [(4, 512, 128, 0), (6, 512, 384, 128)], [(3, 0, 512, 0)], [(4, 0, 512, 0)], [(5, 0, 512, 0)],
          [(6, 0, 512, 0)], [(7, 0, 512, 0)], [(7, 512, 512, 0)]]
NS = G * len(S_USES)
SETS = [[0], [1, 7], [2, 6], [3, 5], [4]]


def columns(j):
    return T - P * j


PACKS = []
for _p, _js in enumerate(SETS):
    if _p < 4:
        for _h in range(G):
            PACKS.append((_p, _h, [(_h, j, sum(columns(i) for i in _js[:n])) for n, j in enumerate(_js)]))
    else:
        for _h in range(0, G, 2):
            PACKS.append((_p, _h // 2, [(_h, 4, 0), (_h + 1, 4, columns(4))]))
NPACK = len(PACKS)
WHERE = {(h, j): (place, col) for _, place, items in PACKS for h, j, col in items}
PV_AFTER = {5: 0, 9: 1, 13: 2, 17: 3}

S_BEHIND = [3, 2] * 7 + [1, 0, 0, 0]
OUT_BEHIND = 3
assert sum(S_BEHIND) == NS

ATT_USES = (NS + 2) * NG + 2 * NG
CYCLE = ATT_USES + 2 + FRONT_USES + 2
assert CYCLE % 2 == 0 and FRONT_USES % 2 == 0 and ATT_USES % 2 == 0


def front_at(n, use):
    order = sorted(PE_SLOT.values()).index(PE_SLOT[use])
    return (0, order) if isinstance(n, int) and n == 0 else (n, order - (2 + FRONT_USES))


def rope_tables():
    inv = 1.0 / 10000.0 ** (np.arange(0, D, 2, dtype=np.float32) / D)
    ang = np.outer(np.arange(T, dtype=np.float32), inv)
    rows = np.arange(P) % D // 2
    return (np.ascontiguousarray(np.cos(ang).astype(np.float32).T[rows]),
            np.ascontiguousarray(np.sin(ang).astype(np.float32).T[rows]))


def mask_rows():
    page = np.arange(T) // PAGE
    rows = np.arange(T // PAGE)[:, None]
    q = np.where(page[None] == rows, BIG, 0.0).astype(np.float16)
    k = np.where(page[None] > rows, -BIG, 0.0).astype(np.float16)
    return q, k


def build(nc, x, w_ln_z, b_ln_z, w_dt, b_dt, w_y, b_y, w_yact, b_yact, h0, w_fc, b_fc, w_fcact, b_fcact,
          w_out, b_out, g_sio, g_ffn, k8, s_in, s_k, bias8, wq, w_down, wk_up, wv_up, wo, Wg, Wu, Wd,
          c_ident, c_cos, c_sin, c_maskq, c_maskk, out):
    with ExitStack() as ctx:
        def sb(name, shape, dt=F32):
            return ctx.enter_context(nc.sbuf_tensor(name, shape, dt))

        def ps(name, shape, dt=F32):
            return ctx.enter_context(nc.psum_tensor(name, shape, dt))

        sem = {}
        for name in (
            "consts_loaded w0_loaded w1_loaded x_loaded w_staged0 w_staged1 w_staged2 w_staged3 qk_loaded0 qk_loaded1 "
            "max_loaded0 max_loaded1 handed_over stored batch_done "
            "half_made zeros_made prep_dve turned0 turned1 split0 w0_hi w0_lo w1_hi w1_lo vecs_ready kq_ready wf_hi wf_lo "
            "ring_full0 ring_full1 ring_free0 ring_free1 "
            "stats1 ln1_ready pool_steps xn_ready xr_ready xb_ready amax_ready sc_ready quant_steps rows_counted q_ready "
            "xrT_hi xrT_lo sz_ready sdt_ready b_ready h_ready h_hi h_lo yact_ready qT_ready y8_steps yT_ready "
            "x1_ready stats2 r2_ready xr2_ready xr2T_hi xr2T_lo fcact_ready hid_ready hid_hi hid_lo oT_ready "
            "x1o_ready x2_ready stats3 ln2_ready xn2_ready xT_hi xT_lo lat_hi lat_lo rope1 rope2 rot_ready "
            "k_hi k_lo q_hi q_lo v_ready "
            "max_steps maxrow_ready st_full exp_done pv_done po_ready po_turned rden_ready att_ready attT_hi attT_lo "
            "gate_full up_full silu_ready h32_ready e_hi e_lo down_done acc_full fT_ready y_ready"
        ).split():
            sem[name] = ctx.enter_context(nc.semaphore(name))
        ring_full = [sem["ring_full0"], sem["ring_full1"]]
        ring_free = [sem["ring_free0"], sem["ring_free1"]]
        qk_loaded = [sem["qk_loaded0"], sem["qk_loaded1"]]
        max_loaded = [sem["max_loaded0"], sem["max_loaded1"]]
        w_staged = [sem[f"w_staged{i}"] for i in range(4)]

        wf = sb("wf", [P, 3 * NE, 2, 512], F16)
        w0 = sb("w0", [P, 2, NW0, P], F16)
        w1 = sb("w1", [P, 2, 448], F16)
        w1u = sb("w1u", [LAT, 2, 384], F16)
        WQ, WQS, WDN, WO = slice(0, 128), slice(128, 256), slice(256, 320), slice(320, 448)
        WK, WKS, WV = slice(0, 128), slice(128, 256), slice(256, 384)
        vec = sb("vec", [P, NV])
        ident = sb("ident", [P, P])
        ident16 = sb("ident16", [P, P], F16)
        identb = sb("identb", [P, P], BF16)
        neg_half, ln_eps, rms_eps = (sb(name, [P, NT]) for name in ("neg_half", "ln_eps", "rms_eps"))
        k8q = sb("k8q", [P, P], BF16)
        bias_bc = sb("bias_bc", [P, P], BF16)
        cos = sb("cos", [P, T])
        sin = sb("sin", [P, T])

        probs = sb("probs", [P, 2, G, T])
        sz, sdt, a_dec, sy = (probs[:, 0, i, :] for i in range(4))
        hid = probs[:, 0, :, :].bitcast(F16)
        h32 = [probs[:, 1, 0, 0:512], probs[:, 1, 0, 512:1024], probs[:, 1, 1, 0:512], probs[:, 1, 1, 512:1024]]
        e_hi = [probs[:, 1, 2, :].bitcast(F16)[:, 512 * i:512 * i + 512] for i in range(4)]
        e_lo = [probs[:, 1, 3, :].bitcast(F16)[:, 512 * i:512 * i + 512] for i in range(4)]
        stage = [probs[:, 1, i, 0:512] for i in range(4)]
        w0nat = probs[:, 0, 0:2, :].rearrange("p a b -> p (a b)").rearrange("p (n m) -> p n m", m=P)
        w1nat = probs[:, 0, 2, 0:448]
        w1unat = probs[0:LAT, 0, 3, 0:384]

        x_nat = sb("x_nat", [P, NT, P])
        xn = sb("xn", [P, NT, P])
        xr = sb("xr", [P, NT, P])
        x1 = sb("x1", [P, NT, P])
        x2 = sb("x2", [P, NT, P])
        x2_keep = sb("x2_keep", [P, NT, P])
        y8 = sb("y8", [P, NT, P], BF16)
        xrT = sb("xrT", [P, 2, T], F16)
        xT = sb("xT", [P, 2, T], F16)
        exT = sb("exT", [P, 2, T], F16)
        tmp = sb("tmp", [P, 2, 512])
        misc = sb("misc", [P, 2, 512])
        qb = misc[:, 0, :].bitcast(BF16).rearrange("p (t d) -> p t d", d=P)
        qT = misc[:, 1, :].bitcast(BF16)
        hid32 = [misc[:, i, :] for i in range(2)]
        gated = sb("gated", [P, 2, 512])
        latT = gated[0:LAT].rearrange("p a b -> p (a b)").bitcast(F16).rearrange("p (s t) -> p s t", s=2)
        sg = sb("sg", [P, 2, 512])
        qh = sb("qh", [P, 2, T], F16)
        kh = sb("kh", [P, 2, T], F16)
        v1 = sb("v1", [P, NT, H, D + 1])
        QO = [sb(f"qo{i}", [P, G, T], F16) for i in range(2)]
        KO = [sb(f"ko{i}", [P, G, T], F16) for i in range(2)]
        mx = [sb(f"mx{i}", [P, G, 12]) for i in range(2)]
        mhl = sb("mhl", [P, 2, G * NT], F16)
        maxrow = sb("maxrow", [G * NT, 2, P], F16)
        rden = sb("rden", [P, HT, G])
        raw6 = sb("raw6", [P, NT, 6])
        mv = sb("mv", [P, NT, 2])
        st = sb("st", [P, 6, NT])
        amax = sb("amax", [P, NT])
        sc_tok = sb("sc_tok", [P, NT])
        h_hl = xrT
        hT = sdt
        yT = a_dec
        att = x1
        attT = xrT
        po = xn[:, :, :].rearrange("p a b -> p (a b)")
        fT = po
        oT = po

        pair = [ps(f"pair{i}", [P, T]) for i in range(2)]
        acc = [ps(f"acc{i}", [P, HALF]) for i in range(2)]
        ring = [ps(f"ring{i}", [P, HALF]) for i in range(2)]
        ring16 = [r[:].bitcast(F16) for r in ring]
        ringb = [r[:].bitcast(BF16) for r in ring]

        HC = [slice(0, HALF), slice(HALF, T)]

        def tiles(c):
            return slice(HT * c, HT * c + HT)

        def ring_no(pos):
            n, off = pos
            return n * (CYCLE // 2) + (off + FRONT_USES) // 2 if not (isinstance(n, int) and n == 0 and off >= 0 and False) else 0

        def parity(pos):
            return pos[1] % 2

        def before(pos):
            return ring_no(pos)

        def front_pos(n, use):
            order = sorted(PE_SLOT.values()).index(PE_SLOT[use])
            if isinstance(n, int) and n == 0:
                return (0, order - FRONT_USES)
            return (n - 1, ATT_USES + 2 + order)

        def s_pos(b, g, u):
            if g == 0:
                return (b, u)
            base = (NS + 2) * g + 2 * (g - 2 if g >= 2 else 0)
            if g >= 2:
                base += 2 if u >= out_index() else 0
            return (b, base + u)

        def out_index():
            return sum(S_BEHIND[:OUT_BEHIND + 1])

        def o_pos(b, g, c):
            if g == NG - 1:
                return (b, ATT_USES - 2 + c)
            if g == NG - 2:
                return (b, ATT_USES - 4 + c)
            return (b, (NS + 2) * (g + 2) + 2 * g + out_index() + c)

        def attT_pos(b, c):
            return (b, ATT_USES + c)

        def fin_pos(b, c):
            return (b, ATT_USES + 2 + (FRONT_USES if not (isinstance(b, int) and b == B - 1) else 0) + c)

        def wait_full(eng, pos):
            eng.wait_ge(ring_full[parity(pos)], before(pos) + 1)

        def wait_free(eng, pos):
            if not (isinstance(pos[0], int) and pos[0] == 0 and pos[1] + FRONT_USES < 2):
                eng.wait_ge(ring_free[parity(pos)], before(pos))

        block = ctx.enter_context(nc.Block())

        @block.sync
        def _(sp):
            def load_x(n):
                sp.dma_start(x_nat[:], x[bass.ds(n, 1)].rearrange("b (t p) d -> p (b t) d", p=P)
                             ).then_inc(sem["x_loaded"], 16)

            load_x(0)
            for w, at in ((w_ln_z, W_Z), (w_dt, W_DT), (w_y, W_Y), (w_yact, W_YACT)):
                sp.dma_start(w0nat[:, at, :], w).then_inc(sem["w0_loaded"], 16)
            sp.dma_start(w0nat[:, W_FC:W_FC + 4, :], w_fc.rearrange("(f p) d -> p f d", p=P)).then_inc(sem["w0_loaded"], 16)
            sp.dma_start(w0nat[:, W_FCACT:W_FCACT + 4, :], w_fcact.rearrange("(f p) d -> p f d", p=P)).then_inc(sem["w0_loaded"], 16)
            sp.dma_start(w0nat[:, W_OUT:W_OUT + 4, :], w_out.rearrange("d (f p) -> d f p", p=P)).then_inc(sem["w0_loaded"], 16)
            for dst, src in ((w1nat[:, WQ], wq), (w1nat[:, WDN], w_down), (w1nat[:, WO], wo),
                             (w1unat[:, WK], wk_up), (w1unat[:, WV], wv_up)):
                sp.dma_start(dst, src).then_inc(sem["w1_loaded"], 16)
            sp.wait_ge(sem["zeros_made"], 1)
            for i in range(2):
                for h in range(G):
                    sp.dma_start(QO[i][MASK_ROW:MASK_ROW + T // PAGE, h, :], c_maskq).then_inc(sem["consts_loaded"], 16)
                    sp.dma_start(KO[i][MASK_ROW:MASK_ROW + T // PAGE, h, :], c_maskk).then_inc(sem["consts_loaded"], 16)
            for u in range(3 * NE):
                e, kind = u // 3, u % 3
                if u >= 4:
                    sp.wait_ge(sem["wf_lo"], u - 3)
                if kind < 2:
                    sp.dma_start(stage[u % 4], (Wg if kind == 0 else Wu)[e]).then_inc(w_staged[u % 4], 16)
                else:
                    sp.dma_start(stage[u % 4].rearrange("p (f h) -> p f h", h=P), Wd[e].rearrange("(f p) h -> p f h", p=P)
                                 ).then_inc(w_staged[u % 4], 16)

            def scatter(b, g):
                i = g % 2
                for h in range(G):
                    rows = slice(D * (G * g + h), D * (G * g + h) + D)
                    for at, (qs, ks) in enumerate(((0, 0), (0, 1), (1, 0))):
                        sp.dma_start(KO[i][D * at:D * at + D, h, :], kh[rows, ks, :]).then_inc(qk_loaded[i], 16)
                        sp.dma_start(QO[i][D * at:D * at + D, h, :], qh[rows, qs, :]).then_inc(qk_loaded[i], 16)

            def put_max(b, g):
                sp.wait_ge(sem["maxrow_ready"], 2 * NG * b + 2 * g + 2)
                for s in range(2):
                    sp.dma_start(QO[g % 2][MAX_ROW + s:MAX_ROW + s + 1, :, :], maxrow[:, s, :]).then_inc(max_loaded[g % 2], 16)

            def batch(b, more):
                for name in ("k_hi", "k_lo", "q_hi", "q_lo"):
                    sp.wait_ge(sem[name], 2 * b + 2)
                scatter(b, 0)
                scatter(b, 1)
                for name in ("xT_hi", "xT_lo"):
                    sp.wait_ge(sem[name], 2 * b + 2)
                sp.wait_ge(sem["x2_ready"], 2 * b + 2)
                sp.dma_start(exT[:], xT[:]).then_inc(sem["handed_over"], 16)
                sp.dma_start(x2_keep[:], x2[:]).then_inc(sem["handed_over"], 16)
                if more:
                    load_x(b + 1)
                put_max(b, 0)
                put_max(b, 1)
                for g in range(2, NG):
                    sp.wait_ge(sem["st_full"], NPACK * (NG * b + g - 1))
                    scatter(b, g)
                    put_max(b, g)
                for c in range(2):
                    sp.wait_ge(sem["y_ready"], 2 * b + c + 1)
                    sp.dma_start(out[bass.ds(b, 1)].rearrange("b (t p) d -> p (b t) d", p=P)[:, tiles(c), :],
                                 x2_keep[:, tiles(c), :]).then_inc(sem["stored"], 16)
                sp.wait_ge(sem["stored"], 32 * b + 32)
                sp.sem_inc(sem["batch_done"], 1)

            with sp.Fori(0, B - 1) as b:
                batch(b, True)
            batch(B - 1, False)

        STEPS = 10

        @block.gpsimd
        def _(pool):
            nc.gpsimd.memset(ln_eps[:], LN_EPS)
            nc.gpsimd.memset(rms_eps[:], RMS_EPS)
            nc.gpsimd.memset(neg_half[:], -0.5).then_inc(sem["half_made"], 1)
            pool.wait_ge(sem["half_made"], 1)

            for src, at in ((b_ln_z, V_BZ), (b_dt, V_BDT), (b_y, V_BY), (b_yact, V_BYACT), (h0, V_H0),
                            (g_sio, V_GSIO), (g_ffn, V_GFFN), (b_out, V_BOUT)):
                pool.dma_start(vec[:, at:at + 1], src.rearrange("(p o) -> p o", o=1)).then_inc(sem["vecs_ready"], 16)
            with nc.allow_non_contiguous_dma(reason="512 numbers, an element to a partition"):
                pool.dma_start(vec[:, V_BFC:V_BFC + 4], b_fc.rearrange("(f p) -> p f", p=P)).then_inc(sem["vecs_ready"], 16)
                pool.dma_start(vec[:, V_BFCACT:V_BFCACT + 4], b_fcact.rearrange("(f p) -> p f", p=P)).then_inc(sem["vecs_ready"], 16)
            for src, at in ((s_in, V_SIN), (s_k, V_SK)):
                pool.dma_start(vec[:, at:at + 1], src.rearrange("(o p) -> o p", o=1).to_broadcast([P, 1])).then_inc(sem["vecs_ready"], 16)
            pool.dma_start(bias_bc[:], bias8.rearrange("(o p) -> o p", o=1).to_broadcast([P, P])).then_inc(sem["vecs_ready"], 16)
            pool.dma_start(k8q[:], k8).then_inc(sem["vecs_ready"], 16)
            pool.dma_start(ident[:], c_ident).then_inc(sem["vecs_ready"], 16)
            pool.dma_start(cos[:], c_cos).then_inc(sem["vecs_ready"], 16)
            pool.dma_start(sin[:], c_sin).then_inc(sem["vecs_ready"], 16)

            def chain(n, first):
                count = [first]

                def link(ins):
                    ins.then_inc(sem["pool_steps"], 1)
                    count[0] += 1
                    pool.wait_ge(sem["pool_steps"], STEPS * n + count[0])
                return link

            MEAN, VAR = mv[:, :, 0], mv[:, :, 1]

            def rstd1(n):
                pool.wait_ge(sem["stats1"], n + 1)
                link = chain(n, 0)
                link(nc.gpsimd.tensor_tensor(st[:, 0, :], VAR, ln_eps[:], ALU.add))
                link(nc.gpsimd.tensor_tensor(st[:, 1, :], st[:, 0, :], neg_half[:], ALU.pow))
                link(nc.gpsimd.tensor_tensor(st[:, 2, :], st[:, 1, :], st[:, 1, :], ALU.mult))
                link(nc.gpsimd.tensor_tensor(st[:, 3, :], st[:, 2, :], VAR, ALU.mult))
                link(nc.gpsimd.tensor_tensor(st[:, 2, :], st[:, 3, :], rms_eps[:], ALU.add))
                link(nc.gpsimd.tensor_tensor(st[:, 3, :], st[:, 2, :], neg_half[:], ALU.pow))
                nc.gpsimd.tensor_tensor(st[:, 2, :], st[:, 3, :], st[:, 1, :], ALU.mult).then_inc(sem["ln1_ready"], 1)

            def rstd2(n):
                pool.wait_ge(sem["stats2"], n + 1)
                link = chain(n, 6)
                link(nc.gpsimd.tensor_tensor(st[:, 3, :], MEAN, MEAN, ALU.mult))
                link(nc.gpsimd.tensor_tensor(st[:, 4, :], st[:, 3, :], VAR, ALU.add))
                link(nc.gpsimd.tensor_tensor(st[:, 3, :], st[:, 4, :], rms_eps[:], ALU.add))
                nc.gpsimd.tensor_tensor(st[:, 4, :], st[:, 3, :], neg_half[:], ALU.pow).then_inc(sem["r2_ready"], 1)

            def rstd3(n):
                pool.wait_ge(sem["stats3"], n + 1)
                link = chain(n, 9)
                link(nc.gpsimd.tensor_tensor(st[:, 3, :], VAR, ln_eps[:], ALU.add))
                nc.gpsimd.tensor_tensor(st[:, 5, :], st[:, 3, :], neg_half[:], ALU.pow).then_inc(sem["ln2_ready"], 1)

            def front(n, s):
                if s == 2:
                    rstd1(n)
                if s == 22:
                    rstd2(n)
                if s == 47:
                    rstd3(n)
                use = AT_SLOT.get(s - 1)
                if use and use[0] == "fc":
                    i = use[1]
                    f, c = i // 2, i % 2
                    pool.wait_ge(sem["hid_hi"], 2 * FF0 * n + i + 1)
                    nc.gpsimd.tensor_tensor(hid[:, f, T + HALF * c:T + HALF * c + HALF], hid32[i % 2],
                                            hid[:, f, HALF * c:HALF * c + HALF], ALU.subtract).then_inc(sem["hid_lo"], 1)

            def expert_lo(b, s):
                pool.wait_ge(sem["e_hi"], SLOTS * b + s + 1)
                nc.gpsimd.tensor_tensor(e_lo[s % 4], h32[s % 4], e_hi[s % 4], ALU.subtract).then_inc(sem["e_lo"], 1)

            def experts(b, more):
                for s in range(SLOTS + 1):
                    if s:
                        expert_lo(b, s - 1)
                    if more and s < SLOTS:
                        front(b + 1, s)

            for s in range(SLOTS):
                front(0, s)
            with pool.Fori(0, B - 1) as b:
                experts(b, True)
            experts(B - 1, False)

        @block.tensor
        def _(pe):
            def three(o, whi, wlo, xhi, xlo, start, stop, inc=None):
                nc.tensor.matmul(o, whi, xhi, start=start, stop=False)
                nc.tensor.matmul(o, whi, xlo, start=False, stop=False)
                mm = nc.tensor.matmul(o, wlo, xhi, start=False, stop=stop)
                if inc is not None:
                    mm.then_inc(inc, 1)

            def turn(pos, src, c, idt, dst=None):
                wait_free(pe, pos)
                r = ring[parity(pos)] if dst is None else dst[parity(pos)]
                for t in range(HT):
                    mm = nc.tensor.transpose(r[:, P * t:P * t + P], src(HT * c + t), idt)
                mm.then_inc(ring_full[parity(pos)], 1)

            def product(pos, w, at, xs, c, rows=P, m=P):
                wait_free(pe, pos)
                three(ring[parity(pos)][0:m, :], w[0:rows, 0, at], w[0:rows, 1, at], xs[0:rows, 0, HC[c]],
                      xs[0:rows, 1, HC[c]], True, True, ring_full[parity(pos)])

            pe.wait_ge(sem["w0_loaded"], 7 * 16)
            pe.wait_ge(sem["vecs_ready"], VECS)
            for i in range(4):
                for j in range(4):
                    mm = nc.tensor.transpose(pair[i // 2][:, 512 * (i % 2) + P * j:512 * (i % 2) + P * j + P],
                                             w0nat[:, 4 * i + j, :], ident[:])
                mm.then_inc(sem["turned0"], 1)

            def w0block(at):
                return w0[:, :, at, :]

            def front(n, s):
                use = AT_SLOT.get(s)
                if use is None:
                    return
                name, c = use
                pos = front_pos(n, use)
                if name == "xrT":
                    if c == 0:
                        pe.wait_ge(sem["xr_ready"], n + 1)
                    turn(pos, lambda t: xr[:, t, :], c, ident[:])
                elif name in ("z", "dt", "yact"):
                    if name == "z":
                        if c == 0:
                            pe.wait_ge(sem["w0_hi"], 4)
                            pe.wait_ge(sem["w0_lo"], 4)
                        pe.wait_ge(sem["xrT_lo"], 2 * n + c + 1)
                    product(pos, w0block({"z": W_Z, "dt": W_DT, "yact": W_YACT}[name]), slice(0, P), xrT, c)
                elif name == "qT":
                    pe.wait_ge(sem["q_ready"], 2 * n + c + 1)
                    turn(pos, lambda t: qb[:, t, :], c, identb[:], ringb)
                elif name == "y8":
                    if c == 0:
                        pe.wait_ge(sem["kq_ready"], 1)
                    pe.wait_ge(sem["qT_ready"], 2 * n + c + 1)
                    wait_free(pe, pos)
                    for t in range(HT):
                        at = HALF * c + P * t
                        mm = nc.tensor.matmul(ring[parity(pos)][:, P * t:P * t + P], qT[:, at:at + P], k8q[:],
                                              start=True, stop=True)
                    mm.then_inc(ring_full[parity(pos)], 1)
                elif name == "y":
                    if c == 0:
                        pe.wait_ge(sem["h_lo"], n + 1)
                    product(pos, w0block(W_Y), slice(0, P), h_hl, c)
                elif name == "ynat":
                    pe.wait_ge(sem["yT_ready"], 2 * n + c + 1)
                    turn(pos, lambda t: yT[:, P * t:P * t + P], c, ident[:])
                elif name == "xr2T":
                    if c == 0:
                        pe.wait_ge(sem["xr2_ready"], n + 1)
                    turn(pos, lambda t: xr[:, t, :], c, ident[:])
                elif name in ("fcact", "fc"):
                    if name == "fcact" and c < 2:
                        pe.wait_ge(sem["xr2T_lo"], 2 * n + c + 1)
                    product(pos, w0block((W_FCACT if name == "fcact" else W_FC) + c // 2), slice(0, P), xrT, c % 2)
                elif name == "out":
                    pe.wait_ge(sem["hid_lo"], 2 * FF0 * n + 2 * FF0 - 1 + c)
                    wait_free(pe, pos)
                    for f in range(FF0):
                        three(ring[parity(pos)][:], w0[:, 0, W_OUT + f, :], w0[:, 1, W_OUT + f, :],
                              hid[:, f, HALF * c:HALF * c + HALF], hid[:, f, T + HALF * c:T + HALF * c + HALF],
                              f == 0, f == FF0 - 1, ring_full[parity(pos)] if f == FF0 - 1 else None)
                elif name == "onat":
                    pe.wait_ge(sem["oT_ready"], 2 * n + c + 1)
                    turn(pos, lambda t: oT[:, P * t:P * t + P], c, ident[:])
                elif name == "xT":
                    if c == 0:
                        pe.wait_ge(sem["xn2_ready"], n + 1)
                    turn(pos, lambda t: xr[:, t, :], c, ident[:])
                elif name == "lat":
                    if c == 0:
                        pe.wait_ge(sem["w1_hi"], 2)
                        pe.wait_ge(sem["w1_lo"], 2)
                    pe.wait_ge(sem["xT_lo"], 2 * n + c + 1)
                    product(pos, w1, WDN, xT, c, m=LAT)
                elif name in ("k", "ks"):
                    pe.wait_ge(sem["lat_lo"], 2 * n + c + 1)
                    product(pos, w1u, WK if name == "k" else WKS, latT, c, rows=LAT)
                elif name in ("q", "qs"):
                    product(pos, w1, WQ if name == "q" else WQS, xT, c)
                elif name == "v":
                    wait_free(pe, pos)
                    for t in range(HT):
                        at = slice(HALF * c + P * t, HALF * c + P * t + P)
                        three(ring[parity(pos)][:, P * t:P * t + P], latT[:, 0, at], latT[:, 1, at],
                              w1u[:, 0, WV], w1u[:, 1, WV], True, True,
                              ring_full[parity(pos)] if t == HT - 1 else None)

            def scores(b, g, u):
                pos = s_pos(b, g, u)
                h, pieces = u // len(S_USES), S_USES[u % len(S_USES)]
                if u == 0:
                    pe.wait_ge(qk_loaded[g % 2], 16 * 6 * G * (NG // 2 * b + g // 2 + 1))
                wait_free(pe, pos)
                for i, k0, kn, col in pieces:
                    mm = nc.tensor.matmul(ring[parity(pos)][:, col:col + kn], QO[g % 2][0:S_ROWS, h, P * i:P * i + P],
                                          KO[g % 2][0:S_ROWS, h, k0:k0 + kn], start=True, stop=True)
                mm.then_inc(ring_full[parity(pos)], 1)

            def maxima(b, g):
                pe.wait_ge(sem["max_steps"], 3 * (NG * b + g + 1))
                for s in range(2):
                    pos = s_pos(b, g, NS + s)
                    wait_free(pe, pos)
                    nc.tensor.transpose(ring16[parity(pos)][0:G * NT, 0:P], mhl[:, s, :], ident16[:]
                                        ).then_inc(ring_full[parity(pos)], 1)

            def pack(b, g, k):
                no = NPACK * (NG * b + g) + k
                if k == 0:
                    pe.wait_ge(max_loaded[g % 2], 32 * (NG // 2 * b + g // 2 + 1))
                if g > 0 or k >= 2:
                    pe.wait_ge(sem["exp_done"], no - 1)
                for h, j, col in PACKS[k][2]:
                    q0 = P * j
                    while q0 < T:
                        at = col + q0 - P * j
                        n = min(T - q0, HALF - at % HALF)
                        mm = nc.tensor.matmul(pair[k % 2][:, at:at + n], KO[g % 2][0:ST_ROWS, h, P * j:P * j + P],
                                              QO[g % 2][0:ST_ROWS, h, q0:q0 + n], start=True, stop=True)
                        q0 += n
                mm.then_inc(sem["st_full"], 1)

            def times_v(b, g, p):
                last = max(k for k in range(NPACK) if PACKS[k][0] == p)
                pe.wait_ge(sem["exp_done"], NPACK * (NG * b + g) + last + 1)
                if p == 0:
                    if g > 0:
                        pe.wait_ge(sem["po_ready"], 2 * (NG * b + g))
                    else:
                        pe.wait_ge(sem["v_ready"], 2 * b + 2)
                buf = (len(SETS) * g + p) % 2
                for j in SETS[p]:
                    for c in range(2):
                        q0 = max(HALF * c, P * j)
                        if q0 >= HALF * c + HALF:
                            continue
                        n = HALF * c + HALF - q0
                        for h in range(G):
                            place, col = WHERE[h, j]
                            at = col + q0 - P * j
                            mm = nc.tensor.matmul(acc[c][32 * h:32 * h + D + 1, q0 - HALF * c:HALF],
                                                  v1[:, j, G * g + h, :], probs[:, buf, place, at:at + n],
                                                  start=(j == 0), stop=(j == (3 if c == 0 else 4)))
                mm.then_inc(sem["pv_done"], 1)

            def output(b, g):
                for c in range(2):
                    pos = o_pos(b, g, c)
                    pe.wait_ge(sem["po_ready"], 2 * (NG * b + g) + c + 1)
                    turn(pos, lambda t: po[:, P * t:P * t + P], c, ident[:])

            def attention(b):
                for u in range(NS):
                    scores(b, 0, u)
                maxima(b, 0)
                for g in range(NG):
                    u = 0
                    for k in range(NPACK):
                        pack(b, g, k)
                        if g + 1 < NG:
                            for _ in range(S_BEHIND[k]):
                                scores(b, g + 1, u)
                                u += 1
                        if k == OUT_BEHIND and 0 < g < NG:
                            output(b, g - 1)
                        if k in PV_AFTER:
                            times_v(b, g, PV_AFTER[k])
                    if g + 1 < NG:
                        maxima(b, g + 1)
                    times_v(b, g, len(SETS) - 1)
                output(b, NG - 1)
                pe.wait_ge(sem["att_ready"], 2 * NG * (b + 1))
                for c in range(2):
                    turn(attT_pos(b, c), lambda t: att[:, t, :], c, ident[:])
                for c in range(2):
                    pe.wait_ge(sem["attT_lo"], 2 * b + c + 1)
                    three(acc[c][:], w1[:, 0, WO], w1[:, 1, WO], attT[:, 0, HC[c]], attT[:, 1, HC[c]], True, False)

            def unit(s):
                return s // (2 * FE), s // 2 % FE, s % 2

            def gate_up(b, s):
                e, f, c = unit(s)
                if s == 0:
                    pe.wait_ge(sem["handed_over"], 32 * (b + 1))
                    pe.wait_ge(sem["wf_lo"], 3 * NE)
                ws = slice(P * f, P * f + P)
                for k, (name, freed) in enumerate((("gate_full", "silu_ready"), ("up_full", "h32_ready"))):
                    if s >= 2:
                        pe.wait_ge(sem[freed], SLOTS * b + s - 1)
                    three(pair[k][:, HC[s % 2]], wf[:, 3 * e + k, 0, ws], wf[:, 3 * e + k, 1, ws],
                          exT[:, 0, HC[c]], exT[:, 1, HC[c]], True, True, sem[name])

            def down(b, s):
                e, f, c = unit(s)
                pe.wait_ge(sem["e_lo"], SLOTS * b + s + 1)
                ws = slice(P * f, P * f + P)
                three(acc[c][:], wf[:, 3 * e + 2, 0, ws], wf[:, 3 * e + 2, 1, ws], e_hi[s % 4], e_lo[s % 4],
                      False, s >= SLOTS - 2, sem["down_done"])

            def experts(b, more):
                for s in range(SLOTS + LAG):
                    if s < SLOTS:
                        gate_up(b, s)
                        if more:
                            front(b + 1, s)
                    if s >= LAG:
                        down(b, s - LAG)
                for c in range(2):
                    pe.wait_ge(sem["fT_ready"], 2 * b + c + 1)
                    turn(fin_pos(b, c), lambda t: fT[:, P * t:P * t + P], c, ident[:])

            for s in range(SLOTS):
                front(0, s)
            with pe.Fori(0, B - 1) as b:
                attention(b)
                experts(b, True)
            attention(B - 1)
            experts(B - 1, False)

        @block.scalar
        def _(act):
            for i in range(4):
                act.wait_ge(sem["turned0"], i + 1)
                nc.scalar.activation(w0[:, 0, 4 * i:4 * i + 4, :].rearrange("p a b -> p (a b)"),
                                     pair[i // 2][:, HC[i % 2]], ACT.Copy).then_inc(sem["w0_hi"], 1)
            act.wait_ge(sem["w1_loaded"], 5 * 16)
            act.wait_ge(sem["prep_dve"], PREP_W1)
            nc.scalar.activation(w1[:, 0, :], w1nat, ACT.Copy).then_inc(sem["w1_hi"], 1)
            nc.scalar.activation(w1u[:, 0, :], w1unat, ACT.Copy).then_inc(sem["w1_hi"], 1)

            def hi_of(n, use, dst, name, scale=1.0, rows=P):
                pos = front_pos(n, use)
                wait_full(act, pos)
                nc.scalar.activation(dst[0:rows, 0, HC[use[1]]], ring[parity(pos)][0:rows, :], ACT.Copy,
                                     scale=scale).then_inc(sem[name], 1)

            def front(n, s):
                use = AT_SLOT.get(s)
                name, c = use or (None, 0)
                pos = front_pos(n, use) if use else None
                if name == "xrT":
                    hi_of(n, use, xrT, "xrT_hi", vec[:, V_GSIO:V_GSIO + 1])
                elif name == "z":
                    wait_full(act, pos)
                    nc.scalar.activation(sz[:, HC[c]], ring[parity(pos)][:], ACT.Sigmoid,
                                         bias=vec[:, V_BZ:V_BZ + 1]).then_inc(ring_free[parity(pos)], 1)
                elif name == "dt":
                    wait_full(act, pos)
                    nc.scalar.activation(sdt[:, HC[c]], ring[parity(pos)][:], ACT.Sigmoid,
                                         bias=vec[:, V_BDT:V_BDT + 1]).then_inc(sem["sdt_ready"], 1)
                    if isinstance(n, int) and n == 0 and c == 0:
                        act.wait_ge(sem["prep_dve"], PREP_VEC)
                    nc.scalar.activation(a_dec[:, HC[c]], ring[parity(pos)][:], ACT.Sigmoid, scale=-1.0,
                                         bias=vec[:, V_NBDT:V_NBDT + 1]).then_inc(ring_free[parity(pos)], 1)
                elif name == "yact":
                    wait_full(act, pos)
                    nc.scalar.activation(sy[:, HC[c]], ring[parity(pos)][:], ACT.Silu,
                                         bias=vec[:, V_BYACT:V_BYACT + 1]).then_inc(ring_free[parity(pos)], 1)
                elif name == "qT":
                    wait_full(act, pos)
                    nc.scalar.activation(qT[:, HC[c]], ringb[parity(pos)][:, 0:HALF], ACT.Copy).then_inc(sem["qT_ready"], 1)
                    act.wait_ge(sem["qT_ready"], 2 * n + c + 1)
                    act.sem_inc(ring_free[parity(pos)], 1)
                elif name == "xr2T":
                    hi_of(n, use, xrT, "xr2T_hi", vec[:, V_GFFN:V_GFFN + 1])
                elif name == "fcact":
                    i = c
                    if i >= 2:
                        act.wait_ge(sem["hid_ready"], 2 * FF0 * n + i - 1)
                    wait_full(act, pos)
                    nc.scalar.activation(gated[:, i % 2, :], ring[parity(pos)][:], ACT.Silu,
                                         bias=vec[:, V_BFCACT + i // 2:V_BFCACT + i // 2 + 1]).then_inc(ring_free[parity(pos)], 1)
                elif name == "fc":
                    i = c
                    act.wait_ge(sem["hid_ready"], 2 * FF0 * n + i + 1)
                    nc.scalar.activation(hid[:, i // 2, HALF * (i % 2):HALF * (i % 2) + HALF], hid32[i % 2],
                                         ACT.Copy).then_inc(sem["hid_hi"], 1)
                elif name == "out":
                    wait_full(act, pos)
                    nc.scalar.activation(oT[:, HC[c]], ring[parity(pos)][:], ACT.Identity,
                                         bias=vec[:, V_BOUT:V_BOUT + 1]).then_inc(sem["oT_ready"], 1)
                    act.wait_ge(sem["oT_ready"], 2 * n + c + 1)
                    act.sem_inc(ring_free[parity(pos)], 1)
                elif name == "xT":
                    hi_of(n, use, xT, "xT_hi")
                elif name == "lat":
                    hi_of(n, use, latT, "lat_hi", rows=LAT)
                elif name in ("ks", "qs"):
                    which, dst = ("k_hi", kh) if name == "ks" else ("q_hi", qh)
                    act.wait_ge(sem["rot_ready"], 4 * n + (0 if name == "ks" else 2) + c + 1)
                    nc.scalar.activation(dst[:, 0, HC[c]], tmp[:, 0, :], ACT.Copy).then_inc(sem[which], 1)
                elif name == "v":
                    wait_full(act, pos)
                    nc.scalar.activation(v1[:, tiles(c), :, 0:D],
                                         ring[parity(pos)][:].rearrange("p (t h d) -> p t h d", t=HT, h=H),
                                         ACT.Copy).then_inc(sem["v_ready"], 1)
                    act.wait_ge(sem["v_ready"], 2 * n + c + 1)
                    act.sem_inc(ring_free[parity(pos)], 1)
                if s == 13:
                    act.wait_ge(sem["h_ready"], n + 1)
                    nc.scalar.activation(h_hl[:, 0, :], hT, ACT.Copy).then_inc(sem["h_hi"], 1)

            def weights(u):
                act.wait_ge(w_staged[u % 4], 16 * (u // 4 + 1))
                nc.scalar.activation(wf[:, u, 0, :], stage[u % 4], ACT.Copy).then_inc(sem["wf_hi"], 1)

            def attention(b):
                for g in range(NG):
                    for k in range(NPACK):
                        p, place, items = PACKS[k]
                        n = sum(columns(j) for _, j, _ in items)
                        buf = (len(SETS) * g + p) % 2
                        if place == 0 and (g > 0 or p >= 2):
                            act.wait_ge(sem["pv_done"], len(SETS) * (NG * b + g) + p - 1)
                        act.wait_ge(sem["st_full"], NPACK * (NG * b + g) + k + 1)
                        nc.scalar.activation(probs[:, buf, place, 0:n], pair[k % 2][:, 0:n], ACT.Exp,
                                             scale=SCALE).then_inc(sem["exp_done"], 1)
                    act.wait_ge(sem["pv_done"], len(SETS) * (NG * b + g + 1))
                    if g > 0:
                        act.wait_ge(sem["po_turned"], 2 * (NG * b + g))
                    for c in range(2):
                        nc.scalar.activation(po[:, HC[c]], acc[c][:], ACT.Copy).then_inc(sem["po_ready"], 1)
                for c in range(2):
                    pos = attT_pos(b, c)
                    wait_full(act, pos)
                    nc.scalar.activation(attT[:, 0, HC[c]], ring[parity(pos)][:], ACT.Copy).then_inc(sem["attT_hi"], 1)

            def expert_silu(b, s):
                if s >= 2:
                    act.wait_ge(sem["h32_ready"], SLOTS * b + s - 1)
                act.wait_ge(sem["gate_full"], SLOTS * b + s + 1)
                nc.scalar.activation(sg[:, s % 2, :], pair[0][:, HC[s % 2]], ACT.Silu).then_inc(sem["silu_ready"], 1)

            def expert_hi(b, s):
                if s >= 4:
                    act.wait_ge(sem["down_done"], SLOTS * b + s - 3)
                act.wait_ge(sem["h32_ready"], SLOTS * b + s + 1)
                nc.scalar.activation(e_hi[s % 4], h32[s % 4], ACT.Copy).then_inc(sem["e_hi"], 1)

            def experts(b, more):
                for s in range(SLOTS + 1):
                    if s < SLOTS:
                        expert_silu(b, s)
                    if s:
                        expert_hi(b, s - 1)
                    if more and s < SLOTS:
                        front(b + 1, s)
                for c in range(2):
                    act.wait_ge(sem["down_done"], SLOTS * b + SLOTS - 1 + c)
                    nc.scalar.activation(fT[:, HC[c]], acc[c][:], ACT.Copy).then_inc(sem["fT_ready"], 1)

            for s in range(SLOTS):
                front(0, s)
                if s % 2 == 0 and s // 2 < 3 * NE:
                    weights(s // 2)
            with act.Fori(0, B - 1) as b:
                attention(b)
                experts(b, True)
            attention(B - 1)
            experts(B - 1, False)

        @block.vector
        def _(dve):
            for i in range(2):
                for z in (QO[i], KO[i]):
                    nc.vector.memset(z[:].rearrange("p a b -> p (a b)").bitcast(U32), 0)
            for z in acc:
                mm = nc.vector.memset(z[:], 0.0)
            mm.then_inc(sem["zeros_made"], 1)
            dve.wait_ge(sem["zeros_made"], 1)
            for i in range(2):
                nc.vector.memset(KO[i][MAX_ROW:MAX_ROW + 2, :, :].rearrange("p a b -> p (a b)"), 1.0)
            nc.vector.memset(v1[:, :, :, D:D + 1], 1.0).then_inc(sem["prep_dve"], 1)

            count = [1]

            def link(ins):
                ins.then_inc(sem["prep_dve"], 1)
                count[0] += 1
                dve.wait_ge(sem["prep_dve"], count[0])

            dve.wait_ge(sem["vecs_ready"], VECS)
            col = lambda i: vec[:, i:i + 1]
            nc.vector.tensor_copy(ident16[:], ident[:])
            nc.vector.tensor_copy(identb[:], ident[:])
            nc.vector.tensor_scalar(col(V_NBDT), col(V_BDT), -1.0, None, ALU.mult)
            nc.vector.reciprocal(col(V_RIN), col(V_SIN))
            nc.vector.reciprocal(col(V_RK), col(V_SK))
            link(nc.vector.tensor_tensor(col(V_SC), col(V_SIN), col(V_SK), ALU.mult))
            assert count[0] == PREP_VEC

            def swap(dst, src):
                d = dst.rearrange("p (i two) -> p i two", two=2)
                s = src.rearrange("p (i two) -> p i two", two=2)
                nc.vector.tensor_scalar(d[:, :, 0:1], s[:, :, 1:2], -1.0, None, ALU.mult)
                return nc.vector.tensor_copy(d[:, :, 1:2], s[:, :, 0:1])

            dve.wait_ge(sem["w1_loaded"], 5 * 16)
            swap(w1nat[:, WQS], w1nat[:, WQ])
            link(swap(w1unat[:, WKS], w1unat[:, WK]))
            assert count[0] == PREP_W1

            for i in range(4):
                dve.wait_ge(sem["w0_hi"], i + 1)
                nc.vector.tensor_tensor(w0[:, 1, 4 * i:4 * i + 4, :].rearrange("p a b -> p (a b)"), pair[i // 2][:, HC[i % 2]],
                                        w0[:, 0, 4 * i:4 * i + 4, :].rearrange("p a b -> p (a b)"),
                                        ALU.subtract).then_inc(sem["w0_lo"], 1)
            dve.wait_ge(sem["w1_hi"], 2)
            nc.vector.tensor_tensor(w1[:, 1, :], w1nat, w1[:, 0, :], ALU.subtract).then_inc(sem["w1_lo"], 1)
            nc.vector.tensor_tensor(w1u[:, 1, :], w1unat, w1u[:, 0, :], ALU.subtract).then_inc(sem["w1_lo"], 1)

            def quantise(dst, src, rcp, shape, step, flag=None):
                v, m = (tmp[:, i, 0:shape[0] * shape[1]] for i in range(2))
                v3 = v.rearrange("p (a b) -> p a b", b=shape[1])
                m3 = m.rearrange("p (a b) -> p a b", b=shape[1])
                step(nc.vector.tensor_scalar(v3, src, rcp, None, ALU.mult))
                step(nc.vector.tensor_scalar(m.bitcast(U32), v.bitcast(U32), 0x7F800000, None, ALU.bitwise_and))
                step(nc.vector.tensor_scalar(m, m, 2.0 ** -6, 1.5 * 2.0 ** 20, ALU.max, ALU.mult))
                step(nc.vector.tensor_tensor(v, v, m, ALU.add))
                return nc.vector.tensor_tensor(dst, v3, m3, ALU.subtract)

            k3 = k8q[:].rearrange("p (a b) -> p a b", a=1)
            dve.wait_ge(sem["prep_dve"], count[0])
            big = tmp[:, 1, 256:384]
            link(nc.vector.tensor_scalar(big, k8q[:], col(V_RK), None, ALU.mult))
            link(nc.vector.tensor_scalar(tmp[:, 1, 384:512].bitcast(U32), big.bitcast(U32), 0x7FFFFFFF, None, ALU.bitwise_and))
            link(nc.vector.tensor_scalar(big, tmp[:, 1, 384:512], 464.0, 3e38, ALU.is_gt, ALU.mult))
            link(nc.vector.tensor_scalar(big, big, 3e38, 0.0, ALU.mult, ALU.mult))
            link(quantise(k3, k3, col(V_RK), (1, P), link))
            nc.vector.tensor_tensor(k8q[:], k8q[:], big, ALU.add).then_inc(sem["kq_ready"], 1)

            def lo_of(n, use, dst, hi, name, scale=1.0, rows=P):
                pos = front_pos(n, use)
                c = use[1]
                dve.wait_ge(sem[hi], 2 * n + c + 1)
                wait_full(dve, pos)
                nc.vector.scalar_tensor_tensor(dst[0:rows, 1, HC[c]], ring[parity(pos)][0:rows, :], scale,
                                               dst[0:rows, 0, HC[c]], ALU.mult, ALU.subtract).then_inc(sem[name], 1)
                release(pos, name, 2 * n + c + 1)

            def release(pos, name, value):
                dve.wait_ge(sem[name], value)
                dve.sem_inc(ring_free[parity(pos)], 1)

            def row_stats(src, ts, name=None):
                for t in ts:
                    ins = nc.vector.bn_stats(raw6[:, t, :], src[:, t, :])
                ins.then_inc(sem["quant_steps"], 1)

            QSTEPS = 8 + 6

            def aggregate(name, n, k):
                dve.wait_ge(sem["quant_steps"], QSTEPS * n + k)
                dve.sem_inc(sem["rows_counted"], 1)
                for t in range(NT):
                    ins = nc.vector.bn_aggr(mv[:, t, :], raw6[:, t, :])
                ins.then_inc(sem[name], 1)

            def front(n, s):
                use = AT_SLOT.get(s)
                name, c = use or (None, 0)
                pos = front_pos(n, use) if use else None
                if s == 0:
                    dve.wait_ge(sem["x_loaded"], 16 * n + 16)
                    row_stats(x_nat, range(0, 4))
                if s == 1:
                    row_stats(x_nat, range(4, 8))
                if s == 2:
                    aggregate("stats1", n, 2)
                if s == 3:
                    dve.wait_ge(sem["ln1_ready"], n + 1)
                    for t in range(NT):
                        ins = nc.vector.tensor_scalar(xn[:, t, :], x_nat[:, t, :], mv[:, t, 0:1], st[:, 1, t:t + 1],
                                                      ALU.subtract, ALU.mult)
                    ins.then_inc(sem["xn_ready"], 1)
                if s == 4:
                    for t in range(NT):
                        ins = nc.vector.tensor_scalar(xr[:, t, :], x_nat[:, t, :], mv[:, t, 0:1], st[:, 2, t:t + 1],
                                                      ALU.subtract, ALU.mult)
                    ins.then_inc(sem["xr_ready"], 1)
                if name == "xrT":
                    lo_of(n, use, xrT, "xrT_hi", "xrT_lo", vec[:, V_GSIO:V_GSIO + 1])
                if s == 5:
                    dve.wait_ge(sem["xn_ready"], n + 1)
                    nc.vector.tensor_copy(qb[:], xn[:]).then_inc(sem["xb_ready"], 1)
                if s == 6:
                    dve.wait_ge(sem["xb_ready"], n + 1)
                    nc.vector.tensor_reduce(amax[:], qb[:], AX.X, ALU.max, apply_absolute_value=True).then_inc(sem["amax_ready"], 1)
                if s in (7, 9):
                    half = (s - 7) // 2
                    k = [2 + 4 * half]

                    def step(ins):
                        ins.then_inc(sem["quant_steps"], 1)
                        k[0] += 1
                        dve.wait_ge(sem["quant_steps"], QSTEPS * n + k[0])
                    quantise(qb[:, tiles(half), :], qb[:, tiles(half), :], col(V_RIN), (HT, P), step).then_inc(sem["q_ready"], 1)
                if s == 8:
                    dve.wait_ge(sem["amax_ready"], n + 1)
                    dve.wait_ge(sem["q_ready"], 2 * n + 1)
                    nc.vector.tensor_scalar(amax[:], amax[:], col(V_RIN), 464.0, ALU.mult, ALU.is_gt).then_inc(sem["sc_ready"], 1)
                    dve.wait_ge(sem["sc_ready"], 3 * n + 1)
                    nc.vector.tensor_scalar(amax[:], amax[:], 3e38, 3e38, ALU.mult, ALU.mult).then_inc(sem["sc_ready"], 1)
                    dve.wait_ge(sem["sc_ready"], 3 * n + 2)
                    nc.vector.tensor_scalar(sc_tok[:], amax[:], 0.0, col(V_SC), ALU.mult, ALU.add).then_inc(sem["sc_ready"], 1)
                if s in (10, 11):
                    half = s - 10
                    dve.wait_ge(sem["sdt_ready"], 2 * n + half + 1)
                    nc.vector.tensor_tensor(sz[:, HC[half]], sz[:, HC[half]], sdt[:, HC[half]], ALU.mult).then_inc(sem["b_ready"], 1)
                if s == 12:
                    dve.wait_ge(sem["b_ready"], 2 * n + 2)
                    dve.wait_ge(ring_free[parity(front_pos(n, ("dt", 1)))], before(front_pos(n, ("dt", 1))) + 1)
                    nc.vector.tensor_tensor_scan(hT, a_dec, sz, col(V_H0), ALU.mult, ALU.add).then_inc(sem["h_ready"], 1)
                if s == 14:
                    dve.wait_ge(sem["h_hi"], n + 1)
                    nc.vector.tensor_tensor(h_hl[:, 1, :], hT, h_hl[:, 0, :], ALU.subtract).then_inc(sem["h_lo"], 1)
                if name == "y8":
                    wait_full(dve, pos)
                    dve.wait_ge(sem["sc_ready"], 3 * n + 3)
                    for t in range(HT):
                        ins = nc.vector.tensor_scalar(y8[:, HT * c + t, :], ring[parity(pos)][:, P * t:P * t + P],
                                                      sc_tok[:, HT * c + t:HT * c + t + 1], None, ALU.mult)
                    ins.then_inc(sem["y8_steps"], 1)
                    release(pos, "y8_steps", 4 * n + 2 * c + 1)
                    nc.vector.tensor_tensor(y8[:, tiles(c), :], y8[:, tiles(c), :],
                                            bias_bc[:].rearrange("p (o d) -> p o d", o=1).to_broadcast([P, HT, P]),
                                            ALU.add).then_inc(sem["y8_steps"], 1)
                if name == "y":
                    wait_full(dve, pos)
                    dve.wait_ge(ring_free[parity(front_pos(n, ("yact", c)))], before(front_pos(n, ("yact", c))) + 1)
                    nc.vector.scalar_tensor_tensor(yT[:, HC[c]], ring[parity(pos)][:], col(V_BY), sy[:, HC[c]],
                                                   ALU.add, ALU.mult).then_inc(sem["yT_ready"], 1)
                    release(pos, "yT_ready", 2 * n + c + 1)
                if name == "ynat":
                    wait_full(dve, pos)
                    nc.vector.tensor_tensor(x1[:, tiles(c), :], ring[parity(pos)][:].rearrange("p (t d) -> p t d", d=P),
                                            xn[:, tiles(c), :], ALU.add).then_inc(sem["x1_ready"], 1)
                    release(pos, "x1_ready", 2 * n + c + 1)
                    row_stats(x1, range(HT * c, HT * c + HT))
                if s == 21:
                    aggregate("stats2", n, 12)
                if s == 23:
                    dve.wait_ge(sem["r2_ready"], n + 1)
                    for t in range(NT):
                        ins = nc.vector.tensor_scalar(xr[:, t, :], x1[:, t, :], st[:, 4, t:t + 1], None, ALU.mult)
                    ins.then_inc(sem["xr2_ready"], 1)
                if name == "xr2T":
                    lo_of(n, use, xrT, "xr2T_hi", "xr2T_lo", vec[:, V_GFFN:V_GFFN + 1])
                if name == "fc":
                    i = c
                    if i >= 2:
                        dve.wait_ge(sem["hid_lo"], 2 * FF0 * n + i - 1)
                    other = front_pos(n, ("fcact", i))
                    dve.wait_ge(ring_free[parity(other)], before(other) + 1)
                    wait_full(dve, pos)
                    nc.vector.scalar_tensor_tensor(hid32[i % 2], ring[parity(pos)][:], vec[:, V_BFC + i // 2:V_BFC + i // 2 + 1],
                                                   gated[:, i % 2, :], ALU.add, ALU.mult).then_inc(sem["hid_ready"], 1)
                    release(pos, "hid_ready", 2 * FF0 * n + i + 1)
                if name == "onat":
                    wait_full(dve, pos)
                    nc.vector.tensor_tensor(x2[:, tiles(c), :], ring[parity(pos)][:].rearrange("p (t d) -> p t d", d=P),
                                            x1[:, tiles(c), :], ALU.add).then_inc(sem["x1o_ready"], 1)
                    release(pos, "x1o_ready", 4 * n + 2 * c + 1)
                    nc.vector.tensor_tensor(x2[:, tiles(c), :], x2[:, tiles(c), :], x_nat[:, tiles(c), :],
                                            ALU.add).then_inc(sem["x1o_ready"], 1)
                    dve.wait_ge(sem["x1o_ready"], 4 * n + 2 * c + 2)
                    dve.wait_ge(sem["y8_steps"], 4 * n + 2 * c + 2)
                    nc.vector.tensor_tensor(x2[:, tiles(c), :], x2[:, tiles(c), :], y8[:, tiles(c), :],
                                            ALU.add).then_inc(sem["x2_ready"], 1)
                    dve.wait_ge(sem["x2_ready"], 2 * n + c + 1)
                    row_stats(x2, range(HT * c, HT * c + HT))
                if s == 47:
                    aggregate("stats3", n, 14)
                if s == 48:
                    dve.wait_ge(sem["ln2_ready"], n + 1)
                    for t in range(NT):
                        ins = nc.vector.tensor_scalar(xr[:, t, :], x2[:, t, :], mv[:, t, 0:1], st[:, 5, t:t + 1],
                                                      ALU.subtract, ALU.mult)
                    ins.then_inc(sem["xn2_ready"], 1)
                if name == "xT":
                    lo_of(n, use, xT, "xT_hi", "xT_lo")
                if name == "lat":
                    lo_of(n, use, latT, "lat_hi", "lat_lo", rows=LAT)
                if name in ("k", "q"):
                    j = 4 * n + (0 if name == "k" else 2) + c
                    wait_full(dve, pos)
                    if j_before(name, c):
                        dve.wait_ge(sem[j_before(name, c)[0]], 2 * n + j_before(name, c)[1])
                    nc.vector.tensor_tensor(tmp[:, 0, :], ring[parity(pos)][:], cos[:, HC[c]], ALU.mult).then_inc(sem["rope1"], 1)
                    release(pos, "rope1", j + 1)
                if name in ("ks", "qs"):
                    j = 4 * n + (0 if name == "ks" else 2) + c
                    wait_full(dve, pos)
                    nc.vector.tensor_tensor(tmp[:, 1, :], ring[parity(pos)][:], sin[:, HC[c]], ALU.mult).then_inc(sem["rope2"], 1)
                    release(pos, "rope2", j + 1)
                    nc.vector.tensor_tensor(tmp[:, 0, :], tmp[:, 0, :], tmp[:, 1, :], ALU.add).then_inc(sem["rot_ready"], 1)
                    hi, lo, dst = ("k_hi", "k_lo", kh) if name == "ks" else ("q_hi", "q_lo", qh)
                    dve.wait_ge(sem[hi], 2 * n + c + 1)
                    nc.vector.tensor_tensor(dst[:, 1, HC[c]], tmp[:, 0, :], dst[:, 0, HC[c]], ALU.subtract).then_inc(sem[lo], 1)

            def j_before(name, c):
                return {("k", 0): None, ("k", 1): ("k_lo", 1), ("q", 0): ("k_lo", 2), ("q", 1): ("q_lo", 1)}[name, c]

            def weights(u):
                dve.wait_ge(sem["wf_hi"], u + 1)
                nc.vector.tensor_tensor(wf[:, u, 1, :], stage[u % 4], wf[:, u, 0, :], ALU.subtract).then_inc(sem["wf_lo"], 1)

            def scores(b, g, u):
                pos = s_pos(b, g, u)
                h, m = u // len(S_USES), mx[g % 2]
                pieces = S_USES[u % len(S_USES)]
                wait_full(dve, pos)
                if len(pieces) == 2 and pieces[0][2] == pieces[1][2]:
                    (i0, _, n, _), (i1, k1, _, _) = pieces
                    cols = (i0, i1 + (4 if k1 else 0))
                    ins = nc.vector.tensor_reduce(m[:, h, cols[0]:cols[1] + 1:cols[1] - cols[0]],
                                                  ring[parity(pos)][:].rearrange("p (a k) -> p a k", k=n), AX.X, ALU.max)
                else:
                    for i, k0, n, at in pieces:
                        to = i + (4 if k0 else 0)
                        ins = nc.vector.tensor_reduce(m[:, h, to:to + 1], ring[parity(pos)][:, at:at + n], AX.X, ALU.max)
                ins.then_inc(ring_free[parity(pos)], 1)

            def maxima(b, g):
                m = mx[g % 2]
                done = 3 * (NG * b + g)
                for u in (NS - 2, NS - 1):
                    pos = s_pos(b, g, u)
                    dve.wait_ge(ring_free[parity(pos)], before(pos) + 1)
                nc.vector.tensor_tensor(m[:, :, 4:8], m[:, :, 4:8], m[:, :, 8:12], ALU.max).then_inc(sem["max_steps"], 1)
                dve.wait_ge(sem["max_steps"], done + 1)
                parts = [mhl[:, s, :].rearrange("p (h i) -> p h i", h=G) for s in range(2)]
                nc.vector.tensor_scalar(parts[0], m[:, :, 0:8], -1.0, None, ALU.mult).then_inc(sem["max_steps"], 1)
                dve.wait_ge(sem["max_steps"], done + 2)
                nc.vector.scalar_tensor_tensor(parts[1], m[:, :, 0:8], -1.0, parts[0], ALU.mult, ALU.subtract
                                               ).then_inc(sem["max_steps"], 1)
                for s in range(2):
                    pos = s_pos(b, g, NS + s)
                    wait_full(dve, pos)
                    if s == 0 and g > 0:
                        dve.wait_ge(max_loaded[(g - 1) % 2], 32 * (NG // 2 * b + (g - 1) // 2 + 1))
                    nc.vector.tensor_copy(maxrow[:, s, :], ring16[parity(pos)][0:G * NT, 0:P]).then_inc(sem["maxrow_ready"], 1)
                    release(pos, "maxrow_ready", 2 * (NG * b + g) + s + 1)

            def output(b, g):
                for c in range(2):
                    pos = o_pos(b, g, c)
                    no = 2 * (NG * b + g) + c
                    r = ring[parity(pos)][:].rearrange("p (t h r) -> p t h r", t=HT, h=G)
                    wait_full(dve, pos)
                    nc.vector.reciprocal(rden[:], r[:, :, :, D]).then_inc(sem["rden_ready"], 1)
                    dve.wait_ge(sem["rden_ready"], no + 1)
                    nc.vector.tensor_tensor(att[:, tiles(c), 32 * g:32 * g + 32].rearrange("p t (h d) -> p t h d", h=G),
                                            r[:, :, :, 0:D],
                                            rden[:].rearrange("p t (h o) -> p t h o", o=1).to_broadcast([P, HT, G, D]),
                                            ALU.mult).then_inc(sem["att_ready"], 1)
                    dve.wait_ge(sem["att_ready"], no + 1)
                    dve.sem_inc(ring_free[parity(pos)], 1)
                    dve.sem_inc(sem["po_turned"], 1)

            def attention(b):
                for u in range(NS):
                    scores(b, 0, u)
                maxima(b, 0)
                for g in range(NG):
                    u = 0
                    for k in range(NPACK):
                        if g + 1 < NG:
                            for _ in range(S_BEHIND[k]):
                                scores(b, g + 1, u)
                                u += 1
                        if k == OUT_BEHIND and g > 0:
                            output(b, g - 1)
                    if g + 1 < NG:
                        maxima(b, g + 1)
                output(b, NG - 1)
                for c in range(2):
                    pos = attT_pos(b, c)
                    dve.wait_ge(sem["attT_hi"], 2 * b + c + 1)
                    nc.vector.tensor_tensor(attT[:, 1, HC[c]], ring[parity(pos)][:], attT[:, 0, HC[c]], ALU.subtract
                                            ).then_inc(sem["attT_lo"], 1)
                    release(pos, "attT_lo", 2 * b + c + 1)

            def expert_gated(b, s):
                if s >= 4:
                    dve.wait_ge(sem["e_lo"], SLOTS * b + s - 3)
                dve.wait_ge(sem["silu_ready"], SLOTS * b + s + 1)
                dve.wait_ge(sem["up_full"], SLOTS * b + s + 1)
                nc.vector.tensor_tensor(h32[s % 4], pair[1][:, HC[s % 2]], sg[:, s % 2, :], ALU.mult).then_inc(sem["h32_ready"], 1)

            def experts(b, more):
                for s in range(SLOTS):
                    expert_gated(b, s)
                    if more:
                        front(b + 1, s)
                dve.wait_ge(sem["handed_over"], 32 * (b + 1))
                for c in range(2):
                    pos = fin_pos(b, c)
                    wait_full(dve, pos)
                    nc.vector.tensor_tensor(x2_keep[:, tiles(c), :], ring[parity(pos)][:].rearrange("p (t d) -> p t d", d=P),
                                            x2_keep[:, tiles(c), :], ALU.add).then_inc(sem["y_ready"], 1)
                    release(pos, "y_ready", 2 * b + c + 1)

            for s in range(SLOTS):
                front(0, s)
                if s % 2 == 0 and s // 2 < 3 * NE:
                    weights(s // 2)
            with dve.Fori(0, B - 1) as b:
                attention(b)
                experts(b, True)
            attention(B - 1)
            experts(B - 1, False)


VECS = 16 * 17
PREP_VEC, PREP_W1 = 2, 3
LAG = 3

NAMES = ["L0_attn_x", "L0_attn_w_ln_z", "L0_attn_b_ln_z", "L0_attn_w_dt", "L0_attn_b_dt", "L0_attn_w_y", "L0_attn_b_y",
         "L0_attn_w_yact", "L0_attn_b_yact", "L0_attn_h0", "L0_attn_w_fc", "L0_attn_b_fc", "L0_attn_w_fcact",
         "L0_attn_b_fcact", "L0_attn_w_out", "L0_attn_b_out", "L0_attn_g_sio", "L0_attn_g_ffn", "L0_ffn_kernel",
         "L0_ffn_input_scale", "L0_ffn_kernel_scale", "L0_ffn_bias", "L1_attn_wq", "L1_attn_w_down", "L1_attn_wk_up",
         "L1_attn_wv_up", "L1_attn_wo", "L1_ffn_Wg", "L1_ffn_Wu", "L1_ffn_Wd"]


def kernel(**inputs):
    import concourse.bacc as bacc
    from concourse.bass_utils import run_bass_kernel_spmd

    nc = bacc.Bacc("TRN2", target_bir_lowering=False, num_devices=1)
    cos, sin = rope_tables()
    maskq, maskk = mask_rows()
    arrays = {f"in_{n}": np.ascontiguousarray(inputs[n]) for n in NAMES}
    arrays |= {"c_ident": np.eye(P, dtype=np.float32), "c_cos": cos, "c_sin": sin, "c_maskq": maskq, "c_maskk": maskk}
    args = [nc.dram_tensor(n, a.shape, mybir.dt.from_np(a.dtype), kind="ExternalInput").ap() for n, a in arrays.items()]
    y = nc.dram_tensor("y", (B, T, P), F32, kind="ExternalOutput").ap()
    build(nc, *args, y)
    r = run_bass_kernel_spmd(nc, [arrays], core_ids=[0])
    return r.results[0]["y"]
```

```python
from contextlib import ExitStack

import numpy as np

import concourse.bass as bass
from concourse import mybir

F32 = mybir.dt.float32
F16 = mybir.dt.float16
BF16 = mybir.dt.bfloat16
U32 = mybir.dt.uint32
ALU = mybir.AluOpType
ACT = mybir.ActivationFunctionType
AX = mybir.AxisListType

P = 128
B, T = 4, 1024
NT = T // P
HT = NT // 2
HALF = T // 2
FF0 = 4
NE, FE = 8, 4
SLOTS = NE * FE * 2
LAT = 64
H, D = 16, 8
G = 4
NG = H // G
PAGE = 32
LN_EPS, RMS_EPS = 1e-5, 1e-6
SCALE = float(1.0 / np.sqrt(np.float32(D)))

FIXED_ROW, MASK_ROW, MAX_ROW = 3 * D, 32, 96
S_ROWS, ST_ROWS = 96, 98
BIG = 60000.0

W_Z, W_DT, W_Y, W_YACT, W_FC, W_FCACT, W_OUT, NW0 = 0, 1, 2, 3, 4, 8, 12, 16
(V_BZ, V_BDT, V_BY, V_BYACT, V_H0, V_GSIO, V_GFFN, V_BOUT, V_SIN, V_SK, V_BFC) = range(11)
V_BFCACT, NV_IN = V_BFC + FF0, V_BFC + 2 * FF0
V_NBDT, V_RIN, V_RK, V_SC, NV = (NV_IN + i for i in range(5))

STATS1, RSTD1, XR, XN, XB, AMAX, QUANT0 = 0, 1, 3, 5, 6, 6, 7
B_IN, SCAN, SCALES, H_LO = 9, 10, 10, 12
STATS2, RSTD2, QUANT1, XR2, FC = 15, 16, 16, 18, 20
STATS3, RSTD3, XN2 = 33, 34, 36
FIRST_S0 = 46
PE_USES = {4: [("xrT", 0), ("xrT", 1)], 5: [("z", 0), ("z", 1)], 8: [("dt", 0), ("dt", 1)],
           9: [("yact", 0), ("yact", 1)], 10: [("qT", 0)], 11: [("y8", 0)], 13: [("y", 0), ("y", 1)],
           14: [("ynat", 0), ("ynat", 1)], 18: [("qT", 1)], 19: [("xr2T", 0), ("xr2T", 1)]}
for _i in range(2 * FF0):
    PE_USES[FC + _i] = [("fcact", _i), ("fc", _i)]
PE_USES[FC] = [("y8", 1)] + PE_USES[FC]
PE_USES |= {29: [("out", 0)], 30: [("out", 1)], 31: [("onat", 0)], 32: [("onat", 1)],
            37: [("xT", 0), ("xT", 1)], 38: [("lat", 0), ("lat", 1)], 39: [("k", 0), ("ks", 0)],
            40: [("k", 1), ("ks", 1)], 41: [("q", 0), ("qs", 0)], 42: [("q", 1), ("qs", 1)], 43: [("v", 0)], 44: [("v", 1)]}
S0_SLOTS = {s: 2 for s in range(FIRST_S0, SLOTS)}
S_USES = [[(0, 0, 128, 0), (2, 0, 384, 128)], [(1, 0, 256, 0), (5, 512, 256, 256)],
          [(4, 512, 128, 0), (6, 512, 384, 128)], [(3, 0, 512, 0)], [(4, 0, 512, 0)], [(5, 0, 512, 0)],
          [(6, 0, 512, 0)], [(7, 0, 512, 0)], [(7, 512, 512, 0)]]
NS = G * len(S_USES)
assert sum(S0_SLOTS.values()) == NS
SETS = [[0], [1, 7], [2, 6], [3, 5], [4]]


def columns(j):
    return T - P * j


PACKS = []
for _p, _js in enumerate(SETS):
    if _p < 4:
        for _h in range(G):
            PACKS.append((_p, _h, [(_h, j, sum(columns(i) for i in _js[:n])) for n, j in enumerate(_js)]))
    else:
        for _h in range(0, G, 2):
            PACKS.append((_p, _h // 2, [(_h, 4, 0), (_h + 1, 4, columns(4))]))
NPACK = len(PACKS)
WHERE = {(h, j): (place, col) for _, place, items in PACKS for h, j, col in items}
PIECES = [[(j, c) for j in js for c in range(2) if P * j < HALF * (c + 1)] for js in SETS]
PV_BEHIND = {4 * p + 5 + i: [(0, p, i)] for p in range(3) for i in range(len(PIECES[p]))}
PV_BEHIND[16], PV_BEHIND[17] = [(0, 3, 0)], [(0, 3, 1), (0, 3, 2)]
PV_BEHIND[0] = [(1, 4, 0)]
assert [len(pieces) for pieces in PIECES] == [2, 3, 3, 3, 1]

S_BEFORE = 4
S_BEHIND = [2]*16 + [0, 0]
OUT_BEHIND, MAX_BEHIND, PO_BEHIND, FIN_BEHIND = 4, 16, 1, 2
EARLY = 2
LAG = 3
UNITS_BEHIND = {s: (2 * s - 4, 2 * s - 3) for s in range(2, 12)} | {s: (s - 10,) for s in range(30, 34)}
assert S_BEFORE + sum(S_BEHIND) == NS

FRONT = [use for s in sorted(PE_USES) for use in PE_USES[s]]
S0 = [("s", 0, u) for u in range(NS)]
MAX0 = [("s", 0, NS), ("s", 0, NS + 1)]
FIN = [("fin", 0), ("fin", 1)]


def attention_order(fin):
    order = []
    for g in range(NG):
        u = S_BEFORE
        if g + 1 < NG:
            order += [("s", g + 1, v) for v in range(u)]
        for k in range(NPACK):
            if g + 1 < NG:
                order += [("s", g + 1, v) for v in range(u, u + S_BEHIND[k])]
                u += S_BEHIND[k]
            if k == OUT_BEHIND and g > 0:
                order += [("o", g - 1, 0), ("o", g - 1, 1)]
            if k == FIN_BEHIND and g == 0 and fin:
                order += FIN
            if k == MAX_BEHIND and g + 1 < NG:
                order += [("s", g + 1, NS), ("s", g + 1, NS + 1)]
    return order + [("o", NG - 1, 0), ("o", NG - 1, 1), ("attT", 0), ("attT", 1)]


BEFORE = FRONT + S0 + MAX0 + attention_order(False)
CYCLE = FRONT + S0 + MAX0 + attention_order(True)
LAST = FIN
assert len(BEFORE) % 2 == 0 and len(CYCLE) % 2 == 0
READER = {"xrT": ("xrT_lo", 2), "z": ("sz_ready", 2), "dt": ("a_ready", 2), "yact": ("yact_ready", 2),
          "qT": ("qT_ready", 2), "y8": ("y8_read", 2), "y": ("yT_ready", 2), "ynat": ("x1_ready", 2),
          "xr2T": ("xr2T_lo", 2), "fcact": ("fcact_ready", 2 * FF0), "fc": ("hid_ready", 2 * FF0),
          "out": ("oT_ready", 2), "onat": ("onat_read", 2), "xT": ("xT_lo", 2), "lat": ("lat_lo", 2),
          "k": ("rope1", 4), "ks": ("rope2", 4), "q": ("rope1", 4), "qs": ("rope2", 4), "v": ("v_ready", 2),
          "attT": ("attT_lo", 2), "fin": ("y_ready", 2)}


def read_by(n, use):
    kind = use[0]
    if kind == "s":
        _, g, u = use
        if u >= NS:
            return "maxrow_ready", 2 * NG * n + 2 * g + u - NS + 1
        return "scores_read", NS * (NG * n + g) + u + 1
    if kind == "o":
        return "att_ready", 2 * NG * n + 2 * use[1] + use[2] + 1
    name, per = READER[kind]
    return name, per * n + use[1] + (2 if kind in ("q", "qs") else 0) + 1


def position(n, use):
    if use[0] == "fin":
        return (LAST if isinstance(n, int) and n == B - 1 else CYCLE), n
    if isinstance(n, int) and n == 0:
        return BEFORE, None
    return CYCLE, n - 1


FEATURE = np.array([D * (G * g + h) + d for g in range(NG) for d in range(D) for h in range(G)])


def rope_tables():
    inv = 1.0 / 10000.0 ** (np.arange(0, D, 2, dtype=np.float32) / D)
    ang = np.outer(np.arange(T, dtype=np.float32), inv)
    d = FEATURE % D
    sign = np.where(d % 2 == 0, np.float32(-1), np.float32(1))[:, None]
    cos, sin = (f(ang).astype(np.float32).T[d // 2] for f in (np.cos, np.sin))
    return np.ascontiguousarray(cos), np.ascontiguousarray(sin * sign)


def fixed_rows():
    page = np.arange(T) // PAGE
    rows = np.arange(T // PAGE)[:, None]
    q, k = (np.zeros((n - FIXED_ROW, T), np.float16) for n in (MAX_ROW, ST_ROWS))
    at = slice(MASK_ROW - FIXED_ROW, MASK_ROW - FIXED_ROW + T // PAGE)
    q[at] = np.where(page[None] == rows, BIG, 0.0)
    k[at] = np.where(page[None] > rows, -BIG, 0.0)
    k[MAX_ROW - FIXED_ROW:] = 1.0
    return q, k


def build(nc, x, vecs, w0_in, w1_in, w1u_in, wf_in, k8, bias8, c_ident, c_cos, c_sin, c_maskq, c_maskk, out):
    with ExitStack() as ctx:
        def sb(name, shape, dt=F32):
            return ctx.enter_context(nc.sbuf_tensor(name, shape, dt))

        def ps(name, shape, dt=F32):
            return ctx.enter_context(nc.psum_tensor(name, shape, dt))

        sem = {}
        for name in (
            "vec_loaded ident_loaded w0_loaded w1_loaded k8_loaded rope_loaded masks_loaded x_loaded w_staged0 "
            "w_staged1 w_staged2 w_staged3 qk_loaded0 qk_loaded1 qk_loaded2 max_loaded0 max_loaded1 max_loaded2 "
            "handed_over stored batch_done "
            "half_made outs_made v_ones vec_steps w0_hi w0_lo w1_hi w1_lo kq_ready wf_hi wf_lo "
            "ring_full0 ring_full1 "
            "rows1 stats1 ln1_ready pool_steps xn_ready xr_ready xb_ready amax_ready sc_ready quant_steps rows_counted "
            "q_ready xrT_hi xrT_lo sz_ready sdt_ready a_ready b_ready h_ready h_hi h_lo yact_ready qT_ready y8_read "
            "y8_ready x_y8_ready yT_ready x1_ready rows2 stats2 r2_ready xr2_ready xr2T_hi xr2T_lo fcact_ready hid_ready "
            "hid_hi hid_lo oT_ready onat_read x2_ready rows3 stats3 ln2_ready xn2_ready xT_hi xT_lo lat_hi lat_lo "
            "rope1 rope2 rot_ready k_hi k_lo q_hi q_lo v_ready "
            "scores_read max_steps maxrow_ready st_full exp_done pv_done po_ready rden_ready att_ready attT_hi attT_lo "
            "gate_full up_full silu_ready h32_ready e_hi e_lo down_done fT_ready y_ready"
        ).split():
            sem[name] = ctx.enter_context(nc.semaphore(name))
        ring_full = [sem["ring_full0"], sem["ring_full1"]]
        qk_loaded = [sem[f"qk_loaded{i}"] for i in range(3)]
        max_loaded = [sem[f"max_loaded{i}"] for i in range(3)]
        w_staged = [sem[f"w_staged{i}"] for i in range(4)]

        wf = sb("wf", [P, 3 * NE, 2, 512], F16)
        w0 = sb("w0", [P, 2, NW0, P], F16)
        w1 = sb("w1", [P, 2, 448], F16)
        w1u = sb("w1u", [LAT, 2, 384], F16)
        WQ, WQS, WDN, WO = slice(0, 128), slice(128, 256), slice(256, 320), slice(320, 448)
        WK, WKS, WV = slice(0, 128), slice(128, 256), slice(256, 384)
        vec = sb("vec", [P, NV])
        ident = sb("ident", [P, P])
        ident16 = sb("ident16", [P, P], F16)
        neg_half, ln_eps, rms_eps = (sb(name, [P, NT]) for name in ("neg_half", "ln_eps", "rms_eps"))
        k8b = sb("k8b", [P, P], BF16)
        k8q = sb("k8q", [P, P], F16)
        bias_bc = sb("bias_bc", [P, P], BF16)
        cos = sb("cos", [P, T])
        sin = sb("sin", [P, T])

        probs = sb("probs", [P, 2, G, T])
        sz, sdt, a_dec, sy = (probs[:, 0, i, :] for i in range(4))
        hid = probs[:, 0, :, :].bitcast(F16)
        h32 = [probs[:, 1, 0, 0:512], probs[:, 1, 0, 512:1024], probs[:, 1, 1, 0:512], probs[:, 1, 1, 512:1024]]
        e_hi = [probs[:, 1, 2, :].bitcast(F16)[:, 512 * i:512 * i + 512] for i in range(4)]
        e_lo = [probs[:, 1, 3, :].bitcast(F16)[:, 512 * i:512 * i + 512] for i in range(4)]
        stage = [probs[:, 1, i // 2, 512 * (i % 2):512 * (i % 2) + 512] for i in range(4)]
        w0nat = probs[:, 0, 0:2, :].rearrange("p a b -> p (a b)")
        w1nat = probs[:, 1, 2, 0:448]
        w1unat = probs[0:LAT, 1, 3, 0:384]
        xr = probs[:, 0, 3, :].rearrange("p (t d) -> p t d", d=P)

        x_nat = sb("x_nat", [P, NT, P])
        xn = sb("xn", [P, NT, P])
        x1 = sb("x1", [P, NT, P])
        x2 = sb("x2", [P, NT, P])
        xrT = sb("xrT", [P, 2, T], F16)
        xT = sb("xT", [P, 2, T], F16)
        exT = sb("exT", [P, 2, T], F16)
        tmp = sb("tmp", [P, 2, 512])
        y8 = tmp[:, 0, 0:HT * P // 2].bitcast(BF16).rearrange("p (t d) -> p t d", d=P)
        misc = sb("misc", [P, 2, 512])
        xb = misc[:, 0, :].bitcast(BF16).rearrange("p (t d) -> p t d", d=P)
        qb = misc[:, 0, :].bitcast(F16).rearrange("p (t d) -> p t d", d=P)
        qT = misc[:, 1, :].bitcast(F16)
        hid32 = [misc[:, i, :] for i in range(2)]
        gated = sb("gated", [P, 2, 512])
        latT = gated[0:LAT].rearrange("p a b -> p (a b)").bitcast(F16).rearrange("p (s t) -> p s t", s=2)
        sg = sb("sg", [P, 2, 512])
        qh = sb("qh", [P, 2, T], F16)
        kh = sb("kh", [P, 2, T], F16)
        v1 = sb("v1", [P, NT, H, D + 1])
        QO = [sb(f"qo{i}", [P, G, T], F16) for i in range(3)]
        KO = [sb(f"ko{i}", [P, G, T], F16) for i in range(3)]
        mx = [sb(f"mx{i}", [P, G, 12]) for i in range(2)]
        mhl = sb("mhl", [P, 2, G * NT], F16)
        maxrow = sb("maxrow", [G * NT, 2, P], F16)
        rden = sb("rden", [P, 2, HT, G])
        raw6 = sb("raw6", [P, NT, 6])
        mv = sb("mv", [P, NT, 2])
        st = sb("st", [P, 6, NT])
        amax = sb("amax", [P, NT])
        sc_tok = sb("sc_tok", [P, NT])
        h_hl = xrT
        hT = sdt
        yT = a_dec
        att = x1
        attT = xrT
        y_out = x1
        po = xn[:, :, :].rearrange("p a b -> p (a b)")
        fT = po
        oT = po

        pair = [ps(f"pair{i}", [P, T]) for i in range(2)]
        acc = [ps(f"acc{i}", [P, HALF]) for i in range(2)]
        ring = [ps(f"ring{i}", [P, HALF]) for i in range(2)]
        ring16 = [r[:].bitcast(F16) for r in ring]

        HC = [slice(0, HALF), slice(HALF, T)]

        def tiles(c):
            return slice(HT * c, HT * c + HT)

        def index_and_before(n, use):
            order, cycle = position(n, use)
            i = order.index(use)
            before = i // 2
            if cycle is not None:
                before = before + len(BEFORE) // 2 + cycle * (len(CYCLE) // 2)
            return order, i, before

        def filled(b, g):
            return (2 if g % 3 == 0 else 1) * b + g // 3 + 1

        def s0_uses(s):
            first = sum(m for t, m in S0_SLOTS.items() if t < s)
            return range(first, first + S0_SLOTS.get(s, 0))

        def bank(n, use):
            return index_and_before(n, use)[1] % 2

        def wait_full(eng, n, use):
            _, i, before = index_and_before(n, use)
            eng.wait_ge(ring_full[i % 2], before + 1)

        def wait_free(eng, n, use):
            order, i, _ = index_and_before(n, use)
            if order is BEFORE and i < 2:
                return
            if i >= 2:
                last = order[i - 2]
                m = n if order is LAST else n + (use[0] == "fin") - (last[0] == "fin")
            else:
                last = CYCLE[len(CYCLE) - 2 + i]
                m = n if use[0] == "fin" else n - 1
            name, value = read_by(m, last)
            eng.wait_ge(sem[name], value)

        block = ctx.enter_context(nc.Block())

        @block.sync
        def _(sp):
            def load_x(n):
                sp.dma_start(x_nat[:], x[bass.ds(n, 1)].rearrange("b (t p) d -> p (b t) d", p=P)
                             ).then_inc(sem["x_loaded"], 16)

            sp.dma_start(vec[:, 0:NV_IN], vecs).then_inc(sem["vec_loaded"], 16)
            load_x(0)
            sp.dma_start(ident[:], c_ident).then_inc(sem["ident_loaded"], 16)
            for i in range(2):
                sp.dma_start(w0nat[:, T * i:T * i + T], w0_in[:, T * i:T * i + T]).then_inc(sem["w0_loaded"], 16)
            sp.dma_start(w1nat, w1_in).then_inc(sem["w1_loaded"], 16)
            sp.dma_start(w1unat, w1u_in).then_inc(sem["w1_loaded"], 16)
            sp.dma_start(k8b[:], k8).then_inc(sem["k8_loaded"], 16)
            sp.dma_start(bias_bc[:], bias8.rearrange("(o p) -> o p", o=1).to_broadcast([P, P])).then_inc(sem["k8_loaded"], 16)
            sp.dma_start(cos[:], c_cos).then_inc(sem["rope_loaded"], 16)
            sp.dma_start(sin[:], c_sin).then_inc(sem["rope_loaded"], 16)

            def stage_unit(u):
                if u >= 4:
                    sp.wait_ge(sem["wf_lo"], u - 3)
                sp.dma_start(stage[u % 4], wf_in[:, u, :]).then_inc(w_staged[u % 4], 16)

            for u in range(16):
                stage_unit(u)
            for i in range(3):
                for z, rows in ((QO[i], c_maskq), (KO[i], c_maskk)):
                    sp.dma_start(z[FIXED_ROW:FIXED_ROW + rows.shape[0], :, :],
                                 rows.rearrange("r (o t) -> r o t", o=1).to_broadcast([rows.shape[0], G, T])
                                 ).then_inc(sem["masks_loaded"], 16)
            for u in range(16, 3 * NE):
                stage_unit(u)

            def scatter(b, g, parts="kq"):
                i = g % 3
                rows = slice(D * G * g, D * G * (g + 1))
                for part in parts:
                    operand, rotated, order = (KO, kh, (0, 1, 0)) if part == "k" else (QO, qh, (0, 0, 1))
                    for at, which in enumerate(order):
                        sp.dma_start(operand[i][D * at:D * at + D, :, :], rotated[rows, which, :]).then_inc(qk_loaded[i], 16)

            def put_max(b, g):
                sp.wait_ge(sem["maxrow_ready"], 2 * NG * b + 2 * g + 2)
                for s in range(2):
                    sp.dma_start(QO[g % 3][MAX_ROW + s:MAX_ROW + s + 1, :, :], maxrow[:, s, :]).then_inc(max_loaded[g % 3], 16)

            def first_groups(n):
                for part in "kq":
                    for half in ("hi", "lo"):
                        sp.wait_ge(sem[f"{part}_{half}"], 2 * n + 2)
                    scatter(n, 0, part)
                for g in (1, 2):
                    scatter(n, g)

            def attention(b, fin):
                put_max(b, 0)
                for name in ("xT_hi", "xT_lo"):
                    sp.wait_ge(sem[name], 2 * b + 2)
                sp.dma_start(exT[:], xT[:]).then_inc(sem["handed_over"], 16)
                if fin:
                    store(b - 1)
                put_max(b, 1)
                sp.wait_ge(sem["st_full"], NPACK * (NG * b + 1))
                scatter(b, 3)
                put_max(b, 2)
                put_max(b, 3)

            def store(b):
                for c in range(2):
                    sp.wait_ge(sem["y_ready"], 2 * b + c + 1)
                    sp.dma_start(out[bass.ds(b, 1)].rearrange("b (t p) d -> p (b t) d", p=P)[:, tiles(c), :],
                                 y_out[:, tiles(c), :]).then_inc(sem["stored"], 16)

            first_groups(0)
            attention(0, False)
            with sp.Fori(0, B - 1) as b:
                sp.wait_ge(sem["x2_ready"], 2 * b + 2)
                load_x(b + 1)
                first_groups(b + 1)
                attention(b + 1, True)
                sp.sem_inc(sem["batch_done"], 1)
            store(B - 1)
            sp.wait_ge(sem["stored"], 32 * B)

        STEPS = 7

        @block.gpsimd
        def _(pool):
            nc.gpsimd.memset(ln_eps[:], LN_EPS)
            nc.gpsimd.memset(rms_eps[:], RMS_EPS)
            nc.gpsimd.memset(neg_half[:], -0.5).then_inc(sem["half_made"], 1)
            pool.wait_ge(sem["half_made"], 1)

            def weights(u):
                pool.wait_ge(sem["wf_hi"], u + 1)
                nc.gpsimd.tensor_tensor(wf[:, u, 1, :], stage[u % 4], wf[:, u, 0, :], ALU.subtract).then_inc(sem["wf_lo"], 1)

            def chain(n, first):
                count = [first]

                def link(ins):
                    ins.then_inc(sem["pool_steps"], 1)
                    count[0] += 1
                    pool.wait_ge(sem["pool_steps"], STEPS * n + count[0])
                return link

            MEAN, VAR = mv[:, :, 0], mv[:, :, 1]

            def rstd1(n):
                pool.wait_ge(sem["stats1"], n + 1)
                link = chain(n, 0)
                link(nc.gpsimd.tensor_tensor(st[:, 0, :], VAR, ln_eps[:], ALU.add))
                link(nc.gpsimd.tensor_tensor(st[:, 2, :], st[:, 0, :], rms_eps[:], ALU.mult))
                link(nc.gpsimd.tensor_tensor(st[:, 1, :], st[:, 2, :], VAR, ALU.add))
                nc.gpsimd.tensor_tensor(st[:, 3, :], st[:, 1, :], neg_half[:], ALU.pow).then_inc(sem["ln1_ready"], 1)

            def rstd2(n):
                pool.wait_ge(sem["stats2"], n + 1)
                link = chain(n, 3)
                link(nc.gpsimd.tensor_tensor(st[:, 0, :], MEAN, MEAN, ALU.mult))
                link(nc.gpsimd.tensor_tensor(st[:, 1, :], st[:, 0, :], VAR, ALU.add))
                link(nc.gpsimd.tensor_tensor(st[:, 0, :], st[:, 1, :], rms_eps[:], ALU.add))
                nc.gpsimd.tensor_tensor(st[:, 4, :], st[:, 0, :], neg_half[:], ALU.pow).then_inc(sem["r2_ready"], 1)

            def rstd3(n):
                pool.wait_ge(sem["stats3"], n + 1)
                link = chain(n, 6)
                link(nc.gpsimd.tensor_tensor(st[:, 0, :], VAR, ln_eps[:], ALU.add))
                nc.gpsimd.tensor_tensor(st[:, 5, :], st[:, 0, :], neg_half[:], ALU.pow).then_inc(sem["ln2_ready"], 1)

            def front(n, s):
                if s == RSTD1:
                    rstd1(n)
                if s == RSTD1 + 2:
                    nc.gpsimd.tensor_tensor(st[:, 2, :], st[:, 0, :], neg_half[:], ALU.pow).then_inc(sem["ln1_ready"], 1)
                if s == RSTD2:
                    rstd2(n)
                if s == RSTD3:
                    rstd3(n)
                for name, i in PE_USES.get(s - 1, ()):
                    if name in ("ks", "qs"):
                        hi, lo, dst = ("k_hi", "k_lo", kh) if name == "ks" else ("q_hi", "q_lo", qh)
                        pool.wait_ge(sem[hi], 2 * n + i + 1)
                        nc.gpsimd.tensor_tensor(dst[:, 1, HC[i]], misc[:, i, :], dst[:, 0, HC[i]], ALU.subtract
                                                ).then_inc(sem[lo], 1)
                    if name == "fc":
                        f, c = i // 2, i % 2
                        pool.wait_ge(sem["hid_hi"], 2 * FF0 * n + i + 1)
                        nc.gpsimd.tensor_tensor(hid[:, f, T + HALF * c:T + HALF * c + HALF], hid32[i % 2],
                                                hid[:, f, HALF * c:HALF * c + HALF], ALU.subtract).then_inc(sem["hid_lo"], 1)

            def expert_lo(b, s):
                pool.wait_ge(sem["e_hi"], SLOTS * b + s + 1)
                nc.gpsimd.tensor_tensor(e_lo[s % 4], h32[s % 4], e_hi[s % 4], ALU.subtract).then_inc(sem["e_lo"], 1)

            def experts(b, more):
                for s in range(SLOTS + 1):
                    if s:
                        expert_lo(b, s - 1)
                    if more and s < SLOTS:
                        front(b + 1, s)

            for s in range(SLOTS):
                front(0, s)
                for u in UNITS_BEHIND.get(s, ()):
                    weights(u)
            with pool.Fori(0, B - 1) as b:
                experts(b, True)
            experts(B - 1, False)

        @block.tensor
        def _(pe):
            def three(o, whi, wlo, xhi, xlo, start, stop, inc=None):
                nc.tensor.matmul(o, whi, xhi, start=start, stop=False)
                nc.tensor.matmul(o, whi, xlo, start=False, stop=False)
                mm = nc.tensor.matmul(o, wlo, xhi, start=False, stop=stop)
                if inc is not None:
                    mm.then_inc(inc, 1)

            def turn(n, use, src, idt, dst=None):
                wait_free(pe, n, use)
                i = bank(n, use)
                r = (dst or ring)[i]
                for t in range(HT):
                    mm = nc.tensor.transpose(r[:, P * t:P * t + P], src(HT * use[-1] + t), idt)
                mm.then_inc(ring_full[i], 1)

            def product(n, use, w, at, xs, c, rows=P, m=P):
                wait_free(pe, n, use)
                i = bank(n, use)
                three(ring[i][0:m, :], w[0:rows, 0, at], w[0:rows, 1, at], xs[0:rows, 0, HC[c]],
                      xs[0:rows, 1, HC[c]], True, True, ring_full[i])

            def w0block(at):
                return w0[:, :, at, :]

            def front_use(n, use):
                name, c = use
                i = bank(n, use)
                if name == "xrT":
                    pe.wait_ge(sem["xr_ready"], n + 1)
                    turn(n, use, lambda t: xr[:, t, :], ident[:])
                elif name in ("z", "dt", "yact"):
                    if isinstance(n, int) and name == "z" and c == 0:
                        pe.wait_ge(sem["w0_lo"], 2)
                    if name == "z":
                        pe.wait_ge(sem["xrT_lo"], 2 * n + c + 1)
                    product(n, use, w0block({"z": W_Z, "dt": W_DT, "yact": W_YACT}[name]), slice(0, P), xrT, c)
                elif name == "qT":
                    pe.wait_ge(sem["q_ready"], 2 * n + c + 1)
                    turn(n, use, lambda t: qb[:, t, :], ident16[:], ring16)
                elif name == "y8":
                    if isinstance(n, int) and c == 0:
                        pe.wait_ge(sem["kq_ready"], 1)
                    pe.wait_ge(sem["qT_ready"], 2 * n + c + 1)
                    wait_free(pe, n, use)
                    for t in range(HT):
                        at = HALF * c + P * t
                        mm = nc.tensor.matmul(ring[i][:, P * t:P * t + P], qT[:, at:at + P], k8q[:], start=True, stop=True)
                    mm.then_inc(ring_full[i], 1)
                elif name == "y":
                    if c == 0:
                        pe.wait_ge(sem["h_lo"], n + 1)
                    product(n, use, w0block(W_Y), slice(0, P), h_hl, c)
                elif name == "ynat":
                    pe.wait_ge(sem["yT_ready"], 2 * n + c + 1)
                    turn(n, use, lambda t: yT[:, P * t:P * t + P], ident[:])
                elif name == "xr2T":
                    pe.wait_ge(sem["xr2_ready"], n + 1)
                    turn(n, use, lambda t: xr[:, t, :], ident[:])
                elif name in ("fcact", "fc"):
                    if name == "fcact" and c < 2:
                        pe.wait_ge(sem["xr2T_lo"], 2 * n + c + 1)
                    product(n, use, w0block((W_FCACT if name == "fcact" else W_FC) + c // 2), slice(0, P), xrT, c % 2)
                elif name == "out":
                    pe.wait_ge(sem["hid_lo"], 2 * FF0 * n + 2 * FF0 - 1 + c)
                    wait_free(pe, n, use)
                    for f in range(FF0):
                        three(ring[i][:], w0[:, 0, W_OUT + f, :], w0[:, 1, W_OUT + f, :],
                              hid[:, f, HALF * c:HALF * c + HALF], hid[:, f, T + HALF * c:T + HALF * c + HALF],
                              f == 0, f == FF0 - 1, ring_full[i] if f == FF0 - 1 else None)
                elif name == "onat":
                    pe.wait_ge(sem["oT_ready"], 2 * n + c + 1)
                    turn(n, use, lambda t: oT[:, P * t:P * t + P], ident[:])
                elif name == "xT":
                    pe.wait_ge(sem["xn2_ready"], n + 1)
                    turn(n, use, lambda t: xr[:, t, :], ident[:])
                elif name == "lat":
                    if isinstance(n, int) and c == 0:
                        pe.wait_ge(sem["w1_lo"], 2)
                    pe.wait_ge(sem["xT_lo"], 2 * n + c + 1)
                    product(n, use, w1, WDN, xT, c, m=LAT)
                elif name in ("k", "ks"):
                    pe.wait_ge(sem["lat_lo"], 2 * n + c + 1)
                    product(n, use, w1u, WK if name == "k" else WKS, latT, c, rows=LAT)
                elif name in ("q", "qs"):
                    product(n, use, w1, WQ if name == "q" else WQS, xT, c)
                elif name == "v":
                    wait_free(pe, n, use)
                    for t in range(HT):
                        at = slice(HALF * c + P * t, HALF * c + P * t + P)
                        three(ring[i][:, P * t:P * t + P], latT[:, 0, at], latT[:, 1, at], w1u[:, 0, WV], w1u[:, 1, WV],
                              True, True, ring_full[i] if t == HT - 1 else None)

            def scores(b, g, u):
                use = ("s", g, u)
                h, pieces = u // len(S_USES), S_USES[u % len(S_USES)]
                if u == 0:
                    pe.wait_ge(qk_loaded[g % 3], 16 * 6 * filled(b, g))
                    if isinstance(b, int) and b == 0 and g == 0:
                        pe.wait_ge(sem["masks_loaded"], 16 * 6)
                wait_free(pe, b, use)
                i = bank(b, use)
                for q, k0, kn, col in pieces:
                    mm = nc.tensor.matmul(ring[i][:, col:col + kn], QO[g % 3][0:S_ROWS, h, P * q:P * q + P],
                                          KO[g % 3][0:S_ROWS, h, k0:k0 + kn], start=True, stop=True)
                mm.then_inc(ring_full[i], 1)

            def maxima(b, g):
                pe.wait_ge(sem["max_steps"], 3 * (NG * b + g + 1))
                for s in range(2):
                    use = ("s", g, NS + s)
                    wait_free(pe, b, use)
                    i = bank(b, use)
                    nc.tensor.transpose(ring16[i][0:G * NT, 0:P], mhl[:, s, :], ident16[:]).then_inc(ring_full[i], 1)

            def front(n, s):
                for use in PE_USES.get(s, ()):
                    front_use(n, use)
                for u in s0_uses(s):
                    scores(n, 0, u)

            def pack(b, g, k):
                no = NPACK * (NG * b + g) + k
                if k == 0:
                    pe.wait_ge(max_loaded[g % 3], 32 * filled(b, g))
                if g > 0 or k >= 2:
                    pe.wait_ge(sem["exp_done"], no - 1)
                for h, j, col in PACKS[k][2]:
                    q0 = P * j
                    while q0 < T:
                        at = col + q0 - P * j
                        n = min(T - q0, HALF - at % HALF)
                        mm = nc.tensor.matmul(pair[k % 2][:, at:at + n], KO[g % 3][0:ST_ROWS, h, P * j:P * j + P],
                                              QO[g % 3][0:ST_ROWS, h, q0:q0 + n], start=True, stop=True)
                        q0 += n
                mm.then_inc(sem["st_full"], 1)

            def times_v(b, g, p, i):
                if i == 0:
                    last = max(k for k in range(NPACK) if PACKS[k][0] == p)
                    pe.wait_ge(sem["exp_done"], NPACK * (NG * b + g) + last + 1)
                if i == 0 and p == 0:
                    if g > 0:
                        pe.wait_ge(sem["po_ready"], 2 * (NG * b + g))
                    else:
                        pe.wait_ge(sem["v_ready"], 2 * b + 2)
                buf = (len(SETS) * g + p) % 2
                j, c = PIECES[p][i]
                q0 = max(HALF * c, P * j)
                n = HALF * c + HALF - q0
                for h in range(G):
                    place, col = WHERE[h, j]
                    at = col + q0 - P * j
                    mm = nc.tensor.matmul(acc[c][32 * h:32 * h + D + 1, q0 - HALF * c:HALF],
                                          v1[:, j, G * g + h, :], probs[:, buf, place, at:at + n],
                                          start=(j == 0), stop=(j == (3 if c == 0 else 4)))
                if i == len(PIECES[p]) - 1:
                    mm.then_inc(sem["pv_done"], 1)

            def output(b, g):
                for c in range(2):
                    pe.wait_ge(sem["po_ready"], 2 * (NG * b + g) + c + 1)
                    turn(b, ("o", g, c), lambda t: po[:, P * t:P * t + P], ident[:])

            def finish(b):
                for c in range(2):
                    pe.wait_ge(sem["fT_ready"], 2 * b + c + 1)
                    turn(b, ("fin", c), lambda t: fT[:, P * t:P * t + P], ident[:])

            def attention(b, fin):
                for g in range(NG):
                    u = 0
                    for k in range(NPACK):
                        if k == 0 and g + 1 < NG:
                            for u in range(S_BEFORE):
                                scores(b, g + 1, u)
                            u = S_BEFORE
                        pieces = [(g - back, p, i) for back, p, i in PV_BEHIND.get(k, ()) if g >= back]
                        n = S_BEHIND[k] if g + 1 < NG else 0
                        for step in range(max(n, 1 + len(pieces))):
                            if step < n:
                                scores(b, g + 1, u)
                                u += 1
                            if step == 0:
                                pack(b, g, k)
                            elif step <= len(pieces):
                                times_v(b, *pieces[step - 1])
                        if k == OUT_BEHIND and g > 0:
                            output(b, g - 1)
                        if k == FIN_BEHIND and g == 0 and fin:
                            finish(b - 1)
                        if k == MAX_BEHIND and g + 1 < NG:
                            maxima(b, g + 1)
                times_v(b, NG - 1, len(SETS) - 1, 0)
                gate_up(b, 0)
                output(b, NG - 1)
                gate_up(b, 1)
                pe.wait_ge(sem["att_ready"], 2 * NG * (b + 1))
                for c in range(2):
                    turn(b, ("attT", c), lambda t: att[:, t, :], ident[:])
                for c in range(2):
                    pe.wait_ge(sem["attT_lo"], 2 * b + c + 1)
                    three(acc[c][:], w1[:, 0, WO], w1[:, 1, WO], attT[:, 0, HC[c]], attT[:, 1, HC[c]], True, False)
                    for t in range(HT):
                        nc.tensor.matmul(acc[c][:, P * t:P * t + P], x2[:, HT * c + t, :], ident[:], start=False, stop=False)

            def unit(s):
                return s // (2 * FE), s // 2 % FE, s % 2

            def gate_up(b, s):
                e, f, c = unit(s)
                if s == 0:
                    pe.wait_ge(sem["handed_over"], 16 * (b + 1))
                    pe.wait_ge(sem["wf_lo"], 3 * NE)
                ws = slice(P * f, P * f + P)
                for k, (name, freed) in enumerate((("gate_full", "silu_ready"), ("up_full", "h32_ready"))):
                    if s >= 2:
                        pe.wait_ge(sem[freed], SLOTS * b + s - 1)
                    if s < 2:
                        pe.wait_ge(sem["exp_done"], NPACK * NG * (b + 1))
                    three(pair[k][:, HC[s % 2]], wf[:, 3 * e + k, 0, ws], wf[:, 3 * e + k, 1, ws],
                          exT[:, 0, HC[c]], exT[:, 1, HC[c]], True, True, sem[name])

            def down(b, s):
                e, f, c = unit(s)
                pe.wait_ge(sem["e_lo"], SLOTS * b + s + 1)
                ws = slice(P * f, P * f + P)
                three(acc[c][:], wf[:, 3 * e + 2, 0, ws], wf[:, 3 * e + 2, 1, ws], e_hi[s % 4], e_lo[s % 4],
                      False, s >= SLOTS - 2, sem["down_done"])

            def experts(b, more):
                for s in range(SLOTS + LAG):
                    if s < SLOTS:
                        if s >= EARLY:
                            gate_up(b, s)
                        if more:
                            front(b + 1, s)
                    if more and s == SLOTS:
                        maxima(b + 1, 0)
                    if s >= LAG:
                        down(b, s - LAG)


            pe.wait_ge(sem["ident_loaded"], 16)
            pe.wait_ge(sem["v_ones"], 1)
            pe.wait_ge(sem["outs_made"], 1)
            pe.wait_ge(sem["vec_steps"], 1)
            for s in range(SLOTS):
                front(0, s)
            maxima(0, 0)
            attention(0, False)
            with pe.Fori(0, B - 1) as b:
                experts(b, True)
                attention(b + 1, True)
            experts(B - 1, False)
            finish(B - 1)

        @block.scalar
        def _(act):
            act.wait_ge(sem["w0_loaded"], 2 * 16)
            for i in range(2):
                nc.scalar.activation(w0[:, 0, 8 * i:8 * i + 8, :].rearrange("p a b -> p (a b)"), w0nat[:, T * i:T * i + T],
                                     ACT.Copy).then_inc(sem["w0_hi"], 1)
            act.wait_ge(sem["w1_loaded"], 2 * 16)
            nc.scalar.activation(w1[:, 0, :], w1nat, ACT.Copy).then_inc(sem["w1_hi"], 1)
            nc.scalar.activation(w1u[:, 0, :], w1unat, ACT.Copy).then_inc(sem["w1_hi"], 1)
            act.wait_ge(sem["vec_loaded"], 16)
            act.wait_ge(sem["vec_steps"], 1)

            def vcol(i):
                return vec[:, i:i + 1]

            def hi_of(n, use, dst, name, scale=1.0, rows=P):
                wait_full(act, n, use)
                nc.scalar.activation(dst[0:rows, 0, HC[use[1]]], ring[bank(n, use)][0:rows, :], ACT.Copy,
                                     scale=scale).then_inc(sem[name], 1)

            def front_use(n, use):
                name, c = use
                r = ring[bank(n, use)]
                if name == "xrT":
                    hi_of(n, use, xrT, "xrT_hi", vcol(V_GSIO))
                elif name == "z":
                    if isinstance(n, int) and c == 0:
                        act.wait_ge(sem["w0_lo"], 2)
                    wait_full(act, n, use)
                    nc.scalar.activation(sz[:, HC[c]], r[:], ACT.Sigmoid, bias=vcol(V_BZ)).then_inc(sem["sz_ready"], 1)
                elif name == "dt":
                    wait_full(act, n, use)
                    nc.scalar.activation(sdt[:, HC[c]], r[:], ACT.Sigmoid, bias=vcol(V_BDT)).then_inc(sem["sdt_ready"], 1)
                    nc.scalar.activation(a_dec[:, HC[c]], r[:], ACT.Sigmoid, scale=-1.0,
                                         bias=vcol(V_NBDT)).then_inc(sem["a_ready"], 1)
                elif name == "yact":
                    wait_full(act, n, use)
                    nc.scalar.activation(sy[:, HC[c]], r[:], ACT.Silu, bias=vcol(V_BYACT)).then_inc(sem["yact_ready"], 1)
                elif name == "qT":
                    wait_full(act, n, use)
                    nc.scalar.activation(qT[:, HC[c]], ring16[bank(n, use)][:, 0:HALF], ACT.Copy).then_inc(sem["qT_ready"], 1)
                elif name == "xr2T":
                    hi_of(n, use, xrT, "xr2T_hi", vcol(V_GFFN))
                elif name == "fcact":
                    if c >= 2:
                        act.wait_ge(sem["hid_ready"], 2 * FF0 * n + c - 1)
                    wait_full(act, n, use)
                    nc.scalar.activation(gated[:, c % 2, :], r[:], ACT.Silu,
                                         bias=vcol(V_BFCACT + c // 2)).then_inc(sem["fcact_ready"], 1)
                elif name == "out":
                    wait_full(act, n, use)
                    nc.scalar.activation(oT[:, HC[c]], r[:], ACT.Identity, bias=vcol(V_BOUT)).then_inc(sem["oT_ready"], 1)
                elif name == "xT":
                    hi_of(n, use, xT, "xT_hi")
                elif name == "lat":
                    hi_of(n, use, latT, "lat_hi", rows=LAT)
                elif name == "v":
                    wait_full(act, n, use)
                    nc.scalar.activation(v1[:, tiles(c), :, 0:D], r[:].rearrange("p (t h d) -> p t h d", t=HT, h=H),
                                         ACT.Copy).then_inc(sem["v_ready"], 1)

            def front_hi(n, use):
                name, c = use
                if name == "fc":
                    act.wait_ge(sem["hid_ready"], 2 * FF0 * n + c + 1)
                    nc.scalar.activation(hid[:, c // 2, HALF * (c % 2):HALF * (c % 2) + HALF], hid32[c % 2],
                                         ACT.Copy).then_inc(sem["hid_hi"], 1)
                elif name in ("ks", "qs"):
                    which, dst = ("k_hi", kh) if name == "ks" else ("q_hi", qh)
                    act.wait_ge(sem["rot_ready"], 4 * n + (0 if name == "ks" else 2) + c + 1)
                    nc.scalar.activation(dst[:, 0, HC[c]], misc[:, c, :], ACT.Copy).then_inc(sem[which], 1)

            def front(n, s):
                for use in PE_USES.get(s - 1, ()):
                    front_hi(n, use)
                for use in PE_USES.get(s, ()):
                    front_use(n, use)
                if s == SCAN + 1:
                    act.wait_ge(sem["h_ready"], n + 1)
                    nc.scalar.activation(h_hl[:, 0, :], hT, ACT.Copy).then_inc(sem["h_hi"], 1)

            def weights(u):
                act.wait_ge(w_staged[u % 4], 16 * (u // 4 + 1))
                nc.scalar.activation(wf[:, u, 0, :], stage[u % 4], ACT.Copy).then_inc(sem["wf_hi"], 1)

            def copy_out(b, g):
                act.wait_ge(sem["pv_done"], len(SETS) * (NG * b + g + 1))
                for c in range(2):
                    nc.scalar.activation(po[:, HC[c]], acc[c][:], ACT.Copy).then_inc(sem["po_ready"], 1)

            def finish(b):
                for c in range(2):
                    act.wait_ge(sem["down_done"], SLOTS * b + SLOTS - 1 + c)
                    nc.scalar.activation(fT[:, HC[c]], acc[c][:], ACT.Copy).then_inc(sem["fT_ready"], 1)

            def attention(b, fin):
                if fin:
                    finish(b - 1)
                for g in range(NG):
                    for k in range(NPACK):
                        p, place, items = PACKS[k]
                        n = sum(columns(j) for _, j, _ in items)
                        buf = (len(SETS) * g + p) % 2
                        if place == 0 and (g > 0 or p >= 2):
                            act.wait_ge(sem["pv_done"], len(SETS) * (NG * b + g) + p - 1)
                        act.wait_ge(sem["st_full"], NPACK * (NG * b + g) + k + 1)
                        nc.scalar.activation(probs[:, buf, place, 0:n], pair[k % 2][:, 0:n], ACT.Exp,
                                             scale=SCALE).then_inc(sem["exp_done"], 1)
                        if k == PO_BEHIND and g > 0:
                            copy_out(b, g - 1)
                copy_out(b, NG - 1)
                expert_silu(b, 0)
                for c in range(2):
                    use = ("attT", c)
                    wait_full(act, b, use)
                    nc.scalar.activation(attT[:, 0, HC[c]], ring[bank(b, use)][:], ACT.Copy).then_inc(sem["attT_hi"], 1)

            def expert_silu(b, s):
                if s >= 2:
                    act.wait_ge(sem["h32_ready"], SLOTS * b + s - 1)
                act.wait_ge(sem["gate_full"], SLOTS * b + s + 1)
                nc.scalar.activation(sg[:, s % 2, :], pair[0][:, HC[s % 2]], ACT.Silu).then_inc(sem["silu_ready"], 1)

            def expert_hi(b, s):
                if s >= 4:
                    act.wait_ge(sem["down_done"], SLOTS * b + s - 3)
                act.wait_ge(sem["h32_ready"], SLOTS * b + s + 1)
                nc.scalar.activation(e_hi[s % 4], h32[s % 4], ACT.Copy).then_inc(sem["e_hi"], 1)

            def experts(b, more):
                for s in range(SLOTS + 1):
                    if 1 <= s < SLOTS:
                        expert_silu(b, s)
                    if s:
                        expert_hi(b, s - 1)
                    if more and s < SLOTS:
                        front(b + 1, s)

            for s in range(SLOTS):
                front(0, s)
                for u in UNITS_BEHIND.get(s, ()):
                    weights(u)
            attention(0, False)
            with act.Fori(0, B - 1) as b:
                experts(b, True)
                attention(b + 1, True)
            experts(B - 1, False)
            finish(B - 1)

        @block.vector
        def _(dve):
            def col(i):
                return vec[:, i:i + 1]

            nc.vector.memset(v1[:, :, :, D:D + 1], 1.0).then_inc(sem["v_ones"], 1)
            for z in acc:
                ins = nc.vector.memset(z[:], 0.0)
            ins.then_inc(sem["outs_made"], 1)
            dve.wait_ge(sem["vec_loaded"], 16)
            dve.wait_ge(sem["ident_loaded"], 16)
            nc.vector.tensor_copy(ident16[:], ident[:])
            nc.vector.tensor_scalar(col(V_NBDT), col(V_BDT), -1.0, None, ALU.mult)
            nc.vector.reciprocal(col(V_RIN), col(V_SIN))
            nc.vector.reciprocal(col(V_RK), col(V_SK))
            nc.vector.tensor_tensor(col(V_SC), col(V_SIN), col(V_SK), ALU.mult).then_inc(sem["vec_steps"], 1)
            dve.wait_ge(sem["vec_steps"], 1)

            def quantise(dst, src, rcp, shape, step, parts=(0, 1)):
                v, m = (tmp[:, i, 0:shape[0] * shape[1]] for i in range(2))
                v3 = v.rearrange("p (a b) -> p a b", b=shape[1])
                m3 = m.rearrange("p (a b) -> p a b", b=shape[1])
                if 0 in parts:
                    step(nc.vector.tensor_scalar(v3, src, rcp, None, ALU.mult))
                    step(nc.vector.tensor_scalar(m.bitcast(U32), v.bitcast(U32), 0x7F800000, None, ALU.bitwise_and))
                    step(nc.vector.tensor_scalar(m, m, 2.0 ** -6, 1.5 * 2.0 ** 20, ALU.max, ALU.mult))
                if 1 in parts:
                    step(nc.vector.tensor_tensor(v, v, m, ALU.add))
                    return nc.vector.tensor_tensor(dst, v3, m3, ALU.subtract)

            def weights_lo():
                for i in range(2):
                    dve.wait_ge(sem["w0_hi"], i + 1)
                    nc.vector.tensor_tensor(w0[:, 1, 8 * i:8 * i + 8, :].rearrange("p a b -> p (a b)"),
                                            w0nat[:, T * i:T * i + T],
                                            w0[:, 0, 8 * i:8 * i + 8, :].rearrange("p a b -> p (a b)"),
                                            ALU.subtract).then_inc(sem["w0_lo"], 1)
                dve.wait_ge(sem["w1_hi"], 2)
                nc.vector.tensor_tensor(w1[:, 1, :], w1nat, w1[:, 0, :], ALU.subtract).then_inc(sem["w1_lo"], 1)
                nc.vector.tensor_tensor(w1u[:, 1, :], w1unat, w1u[:, 0, :], ALU.subtract).then_inc(sem["w1_lo"], 1)

            def quantise_kernel():
                count = [1]

                def link(ins):
                    ins.then_inc(sem["vec_steps"], 1)
                    count[0] += 1
                    dve.wait_ge(sem["vec_steps"], count[0])
                dve.wait_ge(sem["k8_loaded"], 2 * 16)
                big = tmp[:, 1, 256:384]
                link(nc.vector.tensor_scalar(big, k8b[:], col(V_RK), None, ALU.mult))
                link(nc.vector.tensor_scalar(tmp[:, 1, 384:512].bitcast(U32), big.bitcast(U32), 0x7FFFFFFF, None, ALU.bitwise_and))
                link(nc.vector.tensor_scalar(big, tmp[:, 1, 384:512], 464.0, 3e38, ALU.is_gt, ALU.mult))
                link(nc.vector.tensor_scalar(big, big, 3e38, 0.0, ALU.mult, ALU.mult))
                link(quantise(k8q[:].rearrange("p (a b) -> p a b", a=1), k8b[:].rearrange("p (a b) -> p a b", a=1),
                              col(V_RK), (1, P), link))
                nc.vector.tensor_tensor(k8q[:], k8q[:], big, ALU.add).then_inc(sem["kq_ready"], 1)
                dve.wait_ge(sem["kq_ready"], 1)

            def lo_of(n, use, dst, hi, name, scale=1.0, rows=P):
                c = use[1]
                dve.wait_ge(sem[hi], 2 * n + c + 1)
                nc.vector.scalar_tensor_tensor(dst[0:rows, 1, HC[c]], ring[bank(n, use)][0:rows, :], scale,
                                               dst[0:rows, 0, HC[c]], ALU.mult, ALU.subtract).then_inc(sem[name], 1)

            def row_stats(src, name):
                for t in range(NT):
                    ins = nc.vector.bn_stats(raw6[:, t, :], src[:, t, :])
                ins.then_inc(sem[name], 1)

            def aggregate(rows, name, n):
                dve.wait_ge(sem[rows], n + 1)
                dve.sem_inc(sem["rows_counted"], 1)
                for t in range(NT):
                    ins = nc.vector.bn_aggr(mv[:, t, :], raw6[:, t, :])
                ins.then_inc(sem[name], 1)

            QSTEPS = 8

            def centred(dst, src, scale_row):
                for t in range(NT):
                    ins = nc.vector.tensor_scalar(dst[:, t, :], src[:, t, :], mv[:, t, 0:1], st[:, scale_row, t:t + 1],
                                                  ALU.subtract, ALU.mult)
                return ins

            def quantise_half(n, half, part):
                k = [4 * half + 3 * part]

                def step(ins):
                    ins.then_inc(sem["quant_steps"], 1)
                    k[0] += 1
                    dve.wait_ge(sem["quant_steps"], QSTEPS * n + k[0])
                last = quantise(qb[:, tiles(half), :], xb[:, tiles(half), :], col(V_RIN), (HT, P), step, (part,))
                if part:
                    last.then_inc(sem["q_ready"], 1)

            def scale_of_tokens(n):
                dve.wait_ge(sem["amax_ready"], n + 1)
                nc.vector.tensor_scalar(amax[:], amax[:], col(V_RIN), 464.0, ALU.mult, ALU.is_gt).then_inc(sem["sc_ready"], 1)
                dve.wait_ge(sem["sc_ready"], 3 * n + 1)
                nc.vector.tensor_scalar(amax[:], amax[:], 3e38, 3e38, ALU.mult, ALU.mult).then_inc(sem["sc_ready"], 1)
                dve.wait_ge(sem["sc_ready"], 3 * n + 2)
                nc.vector.tensor_scalar(sc_tok[:], amax[:], 0.0, col(V_SC), ALU.mult, ALU.add).then_inc(sem["sc_ready"], 1)

            def front_use(n, use):
                name, c = use
                r = ring[bank(n, use)]
                r3 = r[:].rearrange("p (t d) -> p t d", d=P)
                if name == "xrT":
                    lo_of(n, use, xrT, "xrT_hi", "xrT_lo", col(V_GSIO))
                elif name == "y8":
                    wait_full(dve, n, use)
                    dve.wait_ge(sem["sc_ready"], 3 * n + 3)
                    if c == 1:
                        dve.wait_ge(sem["x_y8_ready"], 2 * n + 1)
                    for t in range(HT):
                        ins = nc.vector.tensor_scalar(y8[:, t, :], r[:, P * t:P * t + P],
                                                      sc_tok[:, HT * c + t:HT * c + t + 1], None, ALU.mult)
                    ins.then_inc(sem["y8_read"], 1)
                    dve.wait_ge(sem["y8_read"], 2 * n + c + 1)
                    nc.vector.tensor_tensor(y8, y8, bias_bc[:].rearrange("p (o d) -> p o d", o=1).to_broadcast([P, HT, P]),
                                            ALU.add).then_inc(sem["y8_ready"], 1)
                    dve.wait_ge(sem["y8_ready"], 2 * n + c + 1)
                    nc.vector.tensor_tensor(x_nat[:, tiles(c), :], x_nat[:, tiles(c), :], y8, ALU.add
                                            ).then_inc(sem["x_y8_ready"], 1)
                elif name == "y":
                    wait_full(dve, n, use)
                    dve.wait_ge(sem["yact_ready"], 2 * n + c + 1)
                    nc.vector.scalar_tensor_tensor(yT[:, HC[c]], r[:], col(V_BY), sy[:, HC[c]],
                                                   ALU.add, ALU.mult).then_inc(sem["yT_ready"], 1)
                elif name == "ynat":
                    wait_full(dve, n, use)
                    nc.vector.tensor_tensor(x1[:, tiles(c), :], r3, xn[:, tiles(c), :], ALU.add).then_inc(sem["x1_ready"], 1)
                elif name == "xr2T":
                    lo_of(n, use, xrT, "xr2T_hi", "xr2T_lo", col(V_GFFN))
                elif name == "fc":
                    if c >= 2:
                        dve.wait_ge(sem["hid_lo"], 2 * FF0 * n + c - 1)
                    dve.wait_ge(sem["fcact_ready"], 2 * FF0 * n + c + 1)
                    wait_full(dve, n, use)
                    nc.vector.scalar_tensor_tensor(hid32[c % 2], r[:], col(V_BFC + c // 2), gated[:, c % 2, :],
                                                   ALU.add, ALU.mult).then_inc(sem["hid_ready"], 1)
                elif name == "onat":
                    wait_full(dve, n, use)
                    nc.vector.tensor_tensor(x2[:, tiles(c), :], r3, x1[:, tiles(c), :], ALU.add).then_inc(sem["onat_read"], 1)
                    dve.wait_ge(sem["onat_read"], 2 * n + c + 1)
                    dve.wait_ge(sem["x_y8_ready"], 2 * n + c + 1)
                    nc.vector.tensor_tensor(x2[:, tiles(c), :], x2[:, tiles(c), :], x_nat[:, tiles(c), :],
                                            ALU.add).then_inc(sem["x2_ready"], 1)
                elif name == "xT":
                    lo_of(n, use, xT, "xT_hi", "xT_lo")
                elif name == "lat":
                    lo_of(n, use, latT, "lat_hi", "lat_lo", rows=LAT)
                elif name in ("k", "q"):
                    before = (0 if name == "k" else 2) + c
                    if before:
                        dve.wait_ge(sem["rot_ready"], 4 * n + before)
                    wait_full(dve, n, use)
                    nc.vector.tensor_tensor(tmp[:, 0, :], r[:], cos[:, HC[c]], ALU.mult).then_inc(sem["rope1"], 1)
                elif name in ("ks", "qs"):
                    j = 4 * n + (0 if name == "ks" else 2) + c
                    wait_full(dve, n, use)
                    nc.vector.tensor_tensor(tmp[:, 1, :], r[:], sin[:, HC[c]], ALU.mult).then_inc(sem["rope2"], 1)
                    if name == "qs":
                        dve.wait_ge(sem["k_lo"], 2 * n + c + 1)
                    dve.wait_ge(sem["rope1"], j + 1)
                    dve.wait_ge(sem["rope2"], j + 1)
                    nc.vector.tensor_tensor(misc[:, c, :], tmp[:, 0, :], tmp[:, 1, :], ALU.add).then_inc(sem["rot_ready"], 1)

            def front(n, s):
                if s == STATS1:
                    dve.wait_ge(sem["x_loaded"], 16 * n + 16)
                    row_stats(x_nat, "rows1")
                if s == RSTD1:
                    aggregate("rows1", "stats1", n)
                if s == XR:
                    dve.wait_ge(sem["ln1_ready"], 2 * n + 1)
                    centred(xr, x_nat, 3).then_inc(sem["xr_ready"], 1)
                if s == H_LO:
                    dve.wait_ge(sem["h_hi"], n + 1)
                    nc.vector.tensor_tensor(h_hl[:, 1, :], hT, h_hl[:, 0, :], ALU.subtract).then_inc(sem["h_lo"], 1)
                if s == B_IN:
                    for c in range(2):
                        dve.wait_ge(sem["sdt_ready"], 2 * n + c + 1)
                        nc.vector.tensor_tensor(sz[:, HC[c]], sz[:, HC[c]], sdt[:, HC[c]], ALU.mult).then_inc(sem["b_ready"], 1)
                if s == SCAN:
                    dve.wait_ge(sem["b_ready"], 2 * n + 2)
                    dve.wait_ge(sem["a_ready"], 2 * n + 2)
                    nc.vector.tensor_tensor_scan(hT, a_dec, sz, col(V_H0), ALU.mult, ALU.add).then_inc(sem["h_ready"], 1)
                if s == XR2:
                    dve.wait_ge(sem["r2_ready"], n + 1)
                    for t in range(NT):
                        ins = nc.vector.tensor_scalar(xr[:, t, :], x1[:, t, :], st[:, 4, t:t + 1], None, ALU.mult)
                    ins.then_inc(sem["xr2_ready"], 1)
                if s == XN2:
                    dve.wait_ge(sem["ln2_ready"], n + 1)
                    centred(xr, x2, 5).then_inc(sem["xn2_ready"], 1)
                for use in PE_USES.get(s, ()):
                    front_use(n, use)
                if s == XN:
                    dve.wait_ge(sem["ln1_ready"], 2 * n + 2)
                    centred(xn, x_nat, 2).then_inc(sem["xn_ready"], 1)
                if s == XB:
                    dve.wait_ge(sem["xn_ready"], n + 1)
                    nc.vector.tensor_copy(xb, xn[:]).then_inc(sem["xb_ready"], 1)
                if s == AMAX:
                    dve.wait_ge(sem["xb_ready"], n + 1)
                    nc.vector.tensor_reduce(amax[:], xb, AX.X, ALU.max, apply_absolute_value=True).then_inc(sem["amax_ready"], 1)
                if s in (QUANT0, QUANT0 + 1):
                    quantise_half(n, 0, s - QUANT0)
                if s == SCALES:
                    scale_of_tokens(n)
                if s == STATS2:
                    dve.wait_ge(sem["x1_ready"], 2 * n + 2)
                    row_stats(x1, "rows2")
                if s == RSTD2:
                    aggregate("rows2", "stats2", n)
                if s in (QUANT1, QUANT1 + 1):
                    dve.wait_ge(sem["x_y8_ready"], 2 * n + 1)
                    quantise_half(n, 1, s - QUANT1)
                if s == STATS3:
                    dve.wait_ge(sem["x2_ready"], 2 * n + 2)
                    row_stats(x2, "rows3")
                if s == RSTD3:
                    aggregate("rows3", "stats3", n)
                for u in s0_uses(s):
                    scores(n, 0, u)

            def scores(b, g, u):
                use = ("s", g, u)
                r = ring[bank(b, use)]
                h, m = u // len(S_USES), mx[g % 2]
                pieces = S_USES[u % len(S_USES)]
                wait_full(dve, b, use)
                if len(pieces) == 2 and pieces[0][2] == pieces[1][2]:
                    (i0, _, n, _), (i1, k1, _, _) = pieces
                    cols = (i0, i1 + (4 if k1 else 0))
                    ins = nc.vector.tensor_reduce(m[:, h, cols[0]:cols[1] + 1:cols[1] - cols[0]],
                                                  r[:].rearrange("p (a k) -> p a k", k=n), AX.X, ALU.max)
                else:
                    for i, k0, n, at in pieces:
                        to = i + (4 if k0 else 0)
                        ins = nc.vector.tensor_reduce(m[:, h, to:to + 1], r[:, at:at + n], AX.X, ALU.max)
                ins.then_inc(sem["scores_read"], 1)

            def maxima_steps(b, g):
                m = mx[g % 2]
                done = 3 * (NG * b + g)
                dve.wait_ge(sem["scores_read"], NS * (NG * b + g + 1))
                nc.vector.tensor_tensor(m[:, :, 4:8], m[:, :, 4:8], m[:, :, 8:12], ALU.max).then_inc(sem["max_steps"], 1)
                dve.wait_ge(sem["max_steps"], done + 1)
                parts = [mhl[:, s, :].rearrange("p (h i) -> p h i", h=G) for s in range(2)]
                nc.vector.tensor_scalar(parts[0], m[:, :, 0:8], -1.0, None, ALU.mult).then_inc(sem["max_steps"], 1)
                dve.wait_ge(sem["max_steps"], done + 2)
                nc.vector.scalar_tensor_tensor(parts[1], m[:, :, 0:8], -1.0, parts[0], ALU.mult, ALU.subtract
                                               ).then_inc(sem["max_steps"], 1)

            def maxima_rows(b, g):
                for s in range(2):
                    use = ("s", g, NS + s)
                    wait_full(dve, b, use)
                    if s == 0 and not (isinstance(b, int) and b == 0 and g == 0):
                        before = (g - 1) % NG
                        dve.wait_ge(max_loaded[before % 3], 32 * (filled(b, before) if g else 2 * b))
                    nc.vector.tensor_copy(maxrow[:, s, :], ring16[bank(b, use)][0:G * NT, 0:P]).then_inc(sem["maxrow_ready"], 1)

            def output(b, g):
                if g == 0 and not isinstance(b, int):
                    dve.wait_ge(sem["stored"], 32 * b)
                for c in range(2):
                    use = ("o", g, c)
                    no = 2 * (NG * b + g) + c
                    r = ring[bank(b, use)][:].rearrange("p (t h r) -> p t h r", t=HT, h=G)
                    wait_full(dve, b, use)
                    nc.vector.reciprocal(rden[:, c], r[:, :, :, D]).then_inc(sem["rden_ready"], 1)
                    dve.wait_ge(sem["rden_ready"], no + 1)
                    nc.vector.tensor_tensor(att[:, tiles(c), 32 * g:32 * g + 32].rearrange("p t (h d) -> p t h d", h=G),
                                            r[:, :, :, 0:D],
                                            rden[:, c].rearrange("p t (h o) -> p t h o", o=1).to_broadcast([P, HT, G, D]),
                                            ALU.mult).then_inc(sem["att_ready"], 1)

            def finish(b):
                for c in range(2):
                    use = ("fin", c)
                    wait_full(dve, b, use)
                    nc.vector.tensor_copy(y_out[:, tiles(c), :], ring[bank(b, use)][:].rearrange("p (t d) -> p t d", d=P)
                                          ).then_inc(sem["y_ready"], 1)

            def attention(b, fin):
                for g in range(NG):
                    u = S_BEFORE
                    if g + 1 < NG:
                        for v in range(u):
                            scores(b, g + 1, v)
                    for k in range(NPACK):
                        if g + 1 < NG:
                            for _ in range(S_BEHIND[k]):
                                scores(b, g + 1, u)
                                u += 1
                                if u == NS:
                                    maxima_steps(b, g + 1)
                        if k == OUT_BEHIND and g > 0:
                            output(b, g - 1)
                        if k == FIN_BEHIND and g == 0 and fin:
                            finish(b - 1)
                    if g + 1 < NG:
                        maxima_rows(b, g + 1)
                output(b, NG - 1)
                for c in range(2):
                    dve.wait_ge(sem["attT_hi"], 2 * b + c + 1)
                    nc.vector.tensor_tensor(attT[:, 1, HC[c]], ring[bank(b, ("attT", c))][:], attT[:, 0, HC[c]], ALU.subtract
                                            ).then_inc(sem["attT_lo"], 1)

            def expert_gated(b, s):
                if s >= 4:
                    dve.wait_ge(sem["e_lo"], SLOTS * b + s - 3)
                dve.wait_ge(sem["silu_ready"], SLOTS * b + s + 1)
                dve.wait_ge(sem["up_full"], SLOTS * b + s + 1)
                nc.vector.tensor_tensor(h32[s % 4], pair[1][:, HC[s % 2]], sg[:, s % 2, :], ALU.mult).then_inc(sem["h32_ready"], 1)

            def experts(b, more):
                for s in range(SLOTS):
                    expert_gated(b, s)
                    if more:
                        front(b + 1, s)
                if more:
                    maxima_steps(b + 1, 0)
                    maxima_rows(b + 1, 0)

            for s in range(SLOTS):
                front(0, s)
                if s == 1:
                    weights_lo()
                if s == 3:
                    quantise_kernel()
            maxima_steps(0, 0)
            maxima_rows(0, 0)
            attention(0, False)
            with dve.Fori(0, B - 1) as b:
                experts(b, True)
                attention(b + 1, True)
            experts(B - 1, False)
            finish(B - 1)


def stacked(blocks):
    return np.ascontiguousarray(np.concatenate(blocks, axis=1))


def kernel(**inputs):
    import concourse.bacc as bacc
    from concourse.bass_utils import run_bass_kernel_spmd

    nc = bacc.Bacc("TRN2", target_bir_lowering=False, num_devices=1)
    a = {name: np.asarray(v) for name, v in inputs.items()}
    cos, sin = rope_tables()
    maskq, maskk = fixed_rows()

    def att0(name):
        return a[f"L0_attn_{name}"]

    def spread(v):
        return np.broadcast_to(v, (P,))

    vectors = [att0(n) for n in ("b_ln_z", "b_dt", "b_y", "b_yact", "h0", "g_sio", "g_ffn", "b_out")]
    vectors += [spread(a["L0_ffn_input_scale"]), spread(a["L0_ffn_kernel_scale"])]
    vectors += list(att0("b_fc").reshape(FF0, P)) + list(att0("b_fcact").reshape(FF0, P))
    w0 = [att0(n).T for n in ("w_ln_z", "w_dt", "w_y", "w_yact")]
    w0 += [att0(n)[P * f:P * f + P].T for n in ("w_fc", "w_fcact") for f in range(FF0)]
    w0 += [att0("w_out")[:, P * f:P * f + P].T for f in range(FF0)]
    partner = FEATURE ^ 1
    wq, wk = a["L1_attn_wq"], a["L1_attn_wk_up"]
    experts = np.stack([a["L1_ffn_Wg"], a["L1_ffn_Wu"],
                        a["L1_ffn_Wd"].reshape(NE, FE, P, P).transpose(0, 2, 1, 3).reshape(NE, P, FE * P)], axis=1)
    arrays = {
        "x": a["L0_attn_x"], "vecs": np.stack(vectors, axis=1), "w0_in": stacked(w0),
        "w1_in": stacked([wq[:, FEATURE], wq[:, partner], a["L1_attn_w_down"], a["L1_attn_wo"]]),
        "w1u_in": stacked([wk[:, FEATURE], wk[:, partner], a["L1_attn_wv_up"]]),
        "wf_in": experts.reshape(3 * NE, P, FE * P).transpose(1, 0, 2),
        "k8": a["L0_ffn_kernel"], "bias8": a["L0_ffn_bias"],
        "c_ident": np.eye(P, dtype=np.float32), "c_cos": cos, "c_sin": sin, "c_maskq": maskq, "c_maskk": maskk}
    arrays = {name: np.ascontiguousarray(v) for name, v in arrays.items()}
    args = [nc.dram_tensor(n, v.shape, mybir.dt.from_np(v.dtype), kind="ExternalInput").ap() for n, v in arrays.items()]
    y = nc.dram_tensor("y", (B, T, P), F32, kind="ExternalOutput").ap()
    build(nc, *args, y)
    r = run_bass_kernel_spmd(nc, [arrays], core_ids=[0])
    return r.results[0]["y"]
```

```python
from contextlib import ExitStack

import numpy as np

import concourse.bass as bass
from concourse import mybir

F32 = mybir.dt.float32
F16 = mybir.dt.float16
BF16 = mybir.dt.bfloat16
U32 = mybir.dt.uint32
ALU = mybir.AluOpType
ACT = mybir.ActivationFunctionType
AX = mybir.AxisListType

P = 128
B, T = 4, 1024
NT = T // P
HT = NT // 2
HALF = T // 2
FF0 = 4
NE, FE = 8, 4
SLOTS = NE * FE * 2
LAT = 64
H, D = 16, 8
G = 4
NG = H // G
PAGE = 32
LN_EPS, RMS_EPS = 1e-5, 1e-6
SCALE = float(1.0 / np.sqrt(np.float32(D)))

FIXED_ROW, MASK_ROW, MAX_ROW = 3 * D, 32, 96
S_ROWS, ST_ROWS = 96, 98
BIG = 60000.0

W_Z, W_DT, W_Y, W_YACT, W_FC, W_FCACT, W_OUT, NW0 = 0, 1, 2, 3, 4, 8, 12, 16
(V_BZ, V_BDT, V_BY, V_BYACT, V_H0, V_GSIO, V_GFFN, V_BOUT, V_SIN, V_SK, V_BFC) = range(11)
V_BFCACT, NV_IN = V_BFC + FF0, V_BFC + 2 * FF0
V_NBDT, V_RIN, V_RK, V_SC, NV = (NV_IN + i for i in range(5))

STATS1, RSTD1, XR, XN, XB, AMAX, QUANT0 = 0, 0, 2, 4, 5, 7, 7
B_IN, SCAN, SCALES, H_LO = 9, 10, 11, 11
STATS2, RSTD2, QUANT1, XR2, FC = 14, 15, 16, 18, 20
STATS3, RSTD3, XN2 = 32, 33, 34
FIRST_S0 = 46
KERNEL8, W1_LO = 10, 28
USES = [(4, "xrT0 xrT1"), (5, "z0 z1"), (8, "dt0 dt1"), (9, "yact0 yact1"), (11, "qT0"), (12, "y80"), (13, "y0 y1"),
        (14, "ynat0 ynat1"), (19, "qT1"), (19, "xr2T0 xr2T1"), (19, "y81")]
USES += [(FC + i, f"fcact{i} fc{i}") for i in range(2 * FF0)]
USES += [(29, "out0"), (30, "out1"), (30, "onat0"), (32, "onat1"), (37, "xT0 xT1"), (38, "lat0 lat1"),
         (39, "k0 ks0"), (40, "k1 ks1"), (41, "q0 qs0"), (41, "q1 qs1"), (44, "v0"), (44, "v1")]
PE_USES = {}
for _slot, _uses in USES:
    PE_USES.setdefault(_slot, []).extend((use[:-1], int(use[-1])) for use in _uses.split())
S0_SLOTS = {s: n for s, n in enumerate([2, 1, 2, 1, 2, 3, 2, 3, 3, 3, 2, 3, 3, 2, 1, 3], FIRST_S0)}
S_USES = [[(0, 0, 128, 0), (2, 0, 384, 128)], [(1, 0, 256, 0), (5, 512, 256, 256)],
          [(4, 512, 128, 0), (6, 512, 384, 128)], [(3, 0, 512, 0)], [(4, 0, 512, 0)], [(5, 0, 512, 0)],
          [(6, 0, 512, 0)], [(7, 0, 512, 0)], [(7, 512, 512, 0)]]
NS = G * len(S_USES)
assert sum(S0_SLOTS.values()) == NS
SETS = [[0], [1, 7], [2, 6], [3, 5], [4]]


def columns(j):
    return T - P * j


PACKS = []
for _p, _js in enumerate(SETS):
    if _p < 4:
        for _h in range(G):
            PACKS.append((_p, _h, [(_h, j, sum(columns(i) for i in _js[:n])) for n, j in enumerate(_js)]))
    else:
        for _h in range(0, G, 2):
            PACKS.append((_p, _h // 2, [(_h, 4, 0), (_h + 1, 4, columns(4))]))
NPACK = len(PACKS)
WHERE = {(h, j): (place, col) for _, place, items in PACKS for h, j, col in items}
PIECES = [[(j, c) for j in js for c in range(2) if P * j < HALF * (c + 1)] for js in SETS]
PV_BEHIND = {1: [(1, 4, 0)], 5: [(0, 0, 0)], 6: [(0, 0, 1)], 9: [(0, 1, 0)], 10: [(0, 1, 1)], 11: [(0, 1, 2)],
             13: [(0, 2, 0)], 14: [(0, 2, 1)], 16: [(0, 2, 2), (0, 3, 0)], 17: [(0, 3, 1), (0, 3, 2)]}
assert [len(pieces) for pieces in PIECES] == [2, 3, 3, 3, 1]

MAX0_SLOT = 62
S_TAIL = [3, 2, 2, 2]
S_BEFORE = 1
S_BEHIND0 = [3, 0, 3, 1, 2, 2, 2, 2, 2, 2, 1, 2, 1, 2, 1, 1, 0, 0]
S_BEHIND = [2, 2, 3, 1, 3, 2, 3, 1, 2, 2, 3, 2, 2, 3, 3, 1, 0, 0]
OUT_BEHIND, MAX_BEHIND, PO_BEHIND, FIN_BEHIND = 3, 16, 2, 0
EARLY = 2
LAG = 4
UNITS = [2, 2, 2, 4, 4, 5, 12, 13, 13, 14, 14, 15, 15, 16, 17, 34, 34, 36, 37, 37, 39, 39, 40, 41]
UNITS_BEHIND = {}
for _u, _slot in enumerate(sorted(UNITS)):
    UNITS_BEHIND.setdefault(_slot, []).append(_u)
assert S_BEFORE + sum(S_BEHIND) == NS and sum(S_TAIL) + sum(S_BEHIND0) == NS

FRONT = [use for s in sorted(PE_USES) for use in PE_USES[s]]
S0 = [("s", 0, u) for u in range(NS)]
MAX0 = [("s", 0, NS)]
S1 = [("s", 1, u) for u in range(sum(S_TAIL))]
FIN = [("fin", 0), ("fin", 1)]


def s_uses(g, k):
    before, behind = (sum(S_TAIL), S_BEHIND0) if g == 0 else (S_BEFORE, S_BEHIND)
    first = before + sum(behind[:k])
    return range(0 if k == 0 and g > 0 else first, first + behind[k])


def attention_order(fin):
    order = []
    for g in range(NG):
        for k in range(NPACK):
            if g + 1 < NG:
                order += [("s", g + 1, v) for v in s_uses(g, k)]
            if k == OUT_BEHIND and g > 0:
                order += [("o", g - 1, 0), ("o", g - 1, 1)]
            if k == FIN_BEHIND and g == 0 and fin:
                order += FIN
            if k == MAX_BEHIND and g + 1 < NG:
                order += [("s", g + 1, NS)]
    return order + [("o", NG - 1, 0), ("o", NG - 1, 1), ("attT", 0), ("attT", 1)]


BEFORE = FRONT + S0 + MAX0 + S1 + attention_order(False)
CYCLE = FRONT + S0 + MAX0 + S1 + attention_order(True)
LAST = FIN
assert len(BEFORE) % 2 == 0 and len(CYCLE) % 2 == 0
READER = {"xrT": ("xrT_lo", 2), "z": ("sz_ready", 2), "dt": ("a_ready", 2), "yact": ("yact_ready", 2),
          "qT": ("qT_ready", 2), "y8": ("y8_read", 2), "y": ("yT_ready", 2), "ynat": ("x1_ready", 2),
          "xr2T": ("xr2T_lo", 2), "fcact": ("fcact_ready", 2 * FF0), "fc": ("hid_ready", 2 * FF0),
          "out": ("oT_ready", 2), "onat": ("onat_read", 2), "xT": ("xT_lo", 2), "lat": ("lat_lo", 2),
          "k": ("rope1", 4), "ks": ("rope2", 4), "q": ("rope1", 4), "qs": ("rope2", 4), "v": ("v_ready", 2),
          "attT": ("attT_lo", 2), "fin": ("y_ready", 2)}


def read_by(n, use):
    kind = use[0]
    if kind == "s":
        _, g, u = use
        if u >= NS:
            return "maxrow_ready", NG * n + g + 1
        return "scores_read", NS * (NG * n + g) + u + 1
    if kind == "o":
        return "att_ready", 2 * NG * n + 2 * use[1] + use[2] + 1
    name, per = READER[kind]
    return name, per * n + use[1] + (2 if kind in ("q", "qs") else 0) + 1


def position(n, use):
    if use[0] == "fin":
        return (LAST if isinstance(n, int) and n == B - 1 else CYCLE), n
    if isinstance(n, int) and n == 0:
        return BEFORE, None
    return CYCLE, n - 1


FEATURE = np.array([D * (G * g + h) + d for g in range(NG) for d in range(D) for h in range(G)])


def rope_tables():
    inv = 1.0 / 10000.0 ** (np.arange(0, D, 2, dtype=np.float32) / D)
    ang = np.outer(np.arange(T, dtype=np.float32), inv)
    d = FEATURE % D
    sign = np.where(d % 2 == 0, np.float32(-1), np.float32(1))[:, None]
    cos, sin = (f(ang).astype(np.float32).T[d // 2] for f in (np.cos, np.sin))
    return np.ascontiguousarray(cos), np.ascontiguousarray(sin * sign)


def fixed_rows():
    page = np.arange(T) // PAGE
    rows = np.arange(T // PAGE)[:, None]
    q, k = (np.zeros((n - FIXED_ROW, T), np.float16) for n in (MAX_ROW, ST_ROWS))
    at = slice(MASK_ROW - FIXED_ROW, MASK_ROW - FIXED_ROW + T // PAGE)
    q[at] = np.where(page[None] == rows, BIG, 0.0)
    k[at] = np.where(page[None] > rows, -BIG, 0.0)
    k[MAX_ROW - FIXED_ROW:] = 1.0
    return q, k


def build(nc, x, vecs, w0_in, w1_in, w1u_in, wf_in, k8, bias8, c_ident, c_cos, c_sin, c_maskq, c_maskk, out):
    with ExitStack() as ctx:
        def sb(name, shape, dt=F32):
            return ctx.enter_context(nc.sbuf_tensor(name, shape, dt))

        def ps(name, shape, dt=F32):
            return ctx.enter_context(nc.psum_tensor(name, shape, dt))

        sem = {}
        for name in (
            "vec_loaded ident_loaded w0_loaded w1_loaded k8_loaded rope_loaded masks_loaded x_loaded w_staged0 "
            "w_staged1 w_staged2 w_staged3 qk_loaded0 qk_loaded1 qk_loaded2 max_loaded0 max_loaded1 max_loaded2 "
            "handed_over stored batch_done "
            "half_made outs_made v_ones vec_steps w0_hi w0_lo w1_hi w1_lo kq_ready wf_hi wf_lo "
            "ring_full0 ring_full1 "
            "rows1 stats1 ln1_ready pool_steps xn_ready xr_ready xb_ready amax_ready sc_ready quant_steps rows_counted "
            "q_ready xrT_hi xrT_lo sz_ready sdt_ready a_ready b_ready h_ready h_hi h_lo yact_ready qT_ready y8_read "
            "y8_ready x_y8_ready yT_ready x1_ready rows2 stats2 r2_ready xr2_ready xr2T_hi xr2T_lo fcact_ready hid_ready "
            "hid_hi hid_lo oT_ready onat_read x2_ready rows3 stats3 ln2_ready xn2_ready xT_hi xT_lo lat_hi lat_lo "
            "rope1 rope2 rot_ready k_hi k_lo q_hi q_lo v_ready "
            "scores_read max_steps maxrow_ready st_full exp_done pv_done po_ready rden_ready att_ready attT_hi attT_lo "
            "gate_full up_full silu_ready h32_ready e_hi e_lo down_done fT_ready y_ready"
        ).split():
            sem[name] = ctx.enter_context(nc.semaphore(name))
        ring_full = [sem["ring_full0"], sem["ring_full1"]]
        qk_loaded = [sem[f"qk_loaded{i}"] for i in range(3)]
        max_loaded = [sem[f"max_loaded{i}"] for i in range(3)]
        w_staged = [sem[f"w_staged{i}"] for i in range(4)]

        wf = sb("wf", [P, 3 * NE, 2, 512], F16)
        w0 = sb("w0", [P, 2, NW0, P], F16)
        w1 = sb("w1", [P, 2, 448], F16)
        w1u = sb("w1u", [LAT, 2, 384], F16)
        WQ, WQS, WDN, WO = slice(0, 128), slice(128, 256), slice(256, 320), slice(320, 448)
        WK, WKS, WV = slice(0, 128), slice(128, 256), slice(256, 384)
        vec = sb("vec", [P, NV])
        ident = sb("ident", [P, P])
        ident16 = sb("ident16", [P, P], F16)
        neg_half, ln_eps, rms_eps = (sb(name, [P, NT]) for name in ("neg_half", "ln_eps", "rms_eps"))
        k8b = sb("k8b", [P, P], BF16)
        k8q = sb("k8q", [P, P], F16)
        bias_bc = sb("bias_bc", [P, P], BF16)
        cos = sb("cos", [P, T])
        sin = sb("sin", [P, T])

        probs = sb("probs", [P, 2, G, T])
        sz, sdt, a_dec, sy = (probs[:, 0, i, :] for i in range(4))
        hid = probs[:, 0, :, :].bitcast(F16)
        h32 = [probs[:, 1, i // 2, 512 * (i % 2):512 * (i % 2) + 512] for i in range(3)]
        e_parts = [probs[:, 1, 2 + i // 4, :].bitcast(F16)[:, 512 * (i % 4):512 * (i % 4) + 512] for i in range(8)]
        e_parts += [probs[:, 1, 1, :].bitcast(F16)[:, 512 * i:512 * i + 512] for i in (2, 3)]
        e_hi, e_lo = e_parts[0::2], e_parts[1::2]
        stage = [probs[:, 1, i // 2, 512 * (i % 2):512 * (i % 2) + 512] for i in range(4)]
        w0nat = probs[:, 0, 0:2, :].rearrange("p a b -> p (a b)")
        w1nat = probs[:, 1, 2, 0:448]
        w1unat = probs[0:LAT, 1, 3, 0:384]
        xr = probs[:, 0, 3, :].rearrange("p (t d) -> p t d", d=P)

        x_nat = sb("x_nat", [P, NT, P])
        xn = sb("xn", [P, NT, P])
        x1 = sb("x1", [P, NT, P])
        x2 = sb("x2", [P, NT, P])
        xrT = sb("xrT", [P, 2, T], F16)
        xT = sb("xT", [P, 2, T], F16)
        exT = sb("exT", [P, 2, T], F16)
        tmp = sb("tmp", [P, 2, 512])
        y8 = tmp[:, 0, 0:HT * P // 2].bitcast(BF16).rearrange("p (t d) -> p t d", d=P)
        misc = sb("misc", [P, 2, 512])
        xb = misc[:, 0, :].bitcast(BF16).rearrange("p (t d) -> p t d", d=P)
        qb = misc[:, 0, :].bitcast(F16).rearrange("p (t d) -> p t d", d=P)
        qT = misc[:, 1, :].bitcast(F16)
        hid32 = [misc[:, i, :] for i in range(2)]
        gated = sb("gated", [P, 2, 512])
        latT = gated[0:LAT].rearrange("p a b -> p (a b)").bitcast(F16).rearrange("p (s t) -> p s t", s=2)
        sg = sb("sg", [P, 2, 512])
        qh = sb("qh", [P, 2, T], F16)
        kh = sb("kh", [P, 2, T], F16)
        v1 = sb("v1", [P, NT, H, D + 1])
        QO = [sb(f"qo{i}", [P, G, T], F16) for i in range(3)]
        KO = [sb(f"ko{i}", [P, G, T], F16) for i in range(3)]
        mx = [sb(f"mx{i}", [P, G, 12]) for i in range(2)]
        mhl = sb("mhl", [P, 2, G * NT], F16)
        maxrow = sb("maxrow", [2 * G * NT, P], F16)
        rden = sb("rden", [P, 2, HT, G])
        raw6 = sb("raw6", [P, NT, 6])
        mv = sb("mv", [P, NT, 2])
        st = sb("st", [P, 6, NT])
        amax = sb("amax", [P, NT])
        sc_tok = sb("sc_tok", [P, NT])
        h_hl = xrT
        hT = sdt
        yT = a_dec
        att = x1
        attT = xrT
        y_out = x1
        po = xn[:, :, :].rearrange("p a b -> p (a b)")
        fT = po
        oT = po

        pair = [ps(f"pair{i}", [P, T]) for i in range(2)]
        acc = [ps(f"acc{i}", [P, HALF]) for i in range(2)]
        ring = [ps(f"ring{i}", [P, HALF]) for i in range(2)]
        ring16 = [r[:].bitcast(F16) for r in ring]

        HC = [slice(0, HALF), slice(HALF, T)]

        def tiles(c):
            return slice(HT * c, HT * c + HT)

        def index_and_before(n, use):
            order, cycle = position(n, use)
            i = order.index(use)
            before = i // 2
            if cycle is not None:
                before = before + len(BEFORE) // 2 + cycle * (len(CYCLE) // 2)
            return order, i, before

        def tail_uses(i):
            return range(sum(S_TAIL[:i]), sum(S_TAIL[:i + 1]))

        def filled(b, g):
            return (2 if g % 3 == 0 else 1) * b + g // 3 + 1

        def s0_uses(s):
            first = sum(m for t, m in S0_SLOTS.items() if t < s)
            return range(first, first + S0_SLOTS.get(s, 0))

        def bank(n, use):
            return index_and_before(n, use)[1] % 2

        def wait_full(eng, n, use):
            _, i, before = index_and_before(n, use)
            eng.wait_ge(ring_full[i % 2], before + 1)

        def wait_free(eng, n, use):
            order, i, _ = index_and_before(n, use)
            if order is BEFORE and i < 2:
                return
            if i >= 2:
                last = order[i - 2]
                m = n if order is LAST else n + (use[0] == "fin") - (last[0] == "fin")
            else:
                last = CYCLE[len(CYCLE) - 2 + i]
                m = n if use[0] == "fin" else n - 1
            name, value = read_by(m, last)
            eng.wait_ge(sem[name], value)

        block = ctx.enter_context(nc.Block())

        @block.sync
        def _(sp):
            def load_x(n):
                sp.dma_start(x_nat[:], x[bass.ds(n, 1)].rearrange("b (t p) d -> p (b t) d", p=P)
                             ).then_inc(sem["x_loaded"], 16)

            sp.dma_start(vec[:, 0:NV_IN], vecs).then_inc(sem["vec_loaded"], 16)
            load_x(0)
            sp.dma_start(ident[:], c_ident).then_inc(sem["ident_loaded"], 16)
            for i in range(2):
                sp.dma_start(w0nat[:, T * i:T * i + T], w0_in[:, T * i:T * i + T]).then_inc(sem["w0_loaded"], 16)
            sp.dma_start(w1nat, w1_in).then_inc(sem["w1_loaded"], 16)
            sp.dma_start(w1unat, w1u_in).then_inc(sem["w1_loaded"], 16)
            sp.dma_start(k8b[:], k8).then_inc(sem["k8_loaded"], 16)
            sp.dma_start(bias_bc[:], bias8.rearrange("(o p) -> o p", o=1).to_broadcast([P, P])).then_inc(sem["k8_loaded"], 16)
            sp.dma_start(cos[:], c_cos).then_inc(sem["rope_loaded"], 16)
            sp.dma_start(sin[:], c_sin).then_inc(sem["rope_loaded"], 16)

            def stage_unit(u):
                if u >= 4:
                    sp.wait_ge(sem["wf_lo"], u - 3)
                sp.dma_start(stage[u % 4], wf_in[:, u, :]).then_inc(w_staged[u % 4], 16)

            for u in range(3 * NE):
                stage_unit(u)
            for i in range(3):
                for z, rows in ((QO[i], c_maskq), (KO[i], c_maskk)):
                    sp.dma_start(z[FIXED_ROW:FIXED_ROW + rows.shape[0], :, :],
                                 rows.rearrange("r (o t) -> r o t", o=1).to_broadcast([rows.shape[0], G, T])
                                 ).then_inc(sem["masks_loaded"], 16)

            def scatter(b, g, parts="kq"):
                i = g % 3
                rows = slice(D * G * g, D * G * (g + 1))
                for part in parts:
                    operand, rotated, order = (KO, kh, (0, 1, 0)) if part == "k" else (QO, qh, (0, 0, 1))
                    for at, which in enumerate(order):
                        sp.dma_start(operand[i][D * at:D * at + D, :, :], rotated[rows, which, :]).then_inc(qk_loaded[i], 16)

            def put_max(b, g):
                sp.wait_ge(sem["maxrow_ready"], NG * b + g + 1)
                sp.dma_start(QO[g % 3][MAX_ROW:MAX_ROW + 2, :, :], maxrow[:]).then_inc(max_loaded[g % 3], 16)

            def first_groups(n):
                for part in "kq":
                    for half in ("hi", "lo"):
                        sp.wait_ge(sem[f"{part}_{half}"], 2 * n + 2)
                    scatter(n, 0, part)
                for g in (1, 2):
                    scatter(n, g)

            def attention(b, fin):
                put_max(b, 0)
                if fin:
                    sp.wait_ge(sem["up_full"], SLOTS * b)
                for name in ("xT_hi", "xT_lo"):
                    sp.wait_ge(sem[name], 2 * b + 2)
                sp.dma_start(exT[:], xT[:]).then_inc(sem["handed_over"], 16)
                if fin:
                    store(b - 1)
                put_max(b, 1)
                sp.wait_ge(sem["st_full"], NPACK * (NG * b + 1))
                scatter(b, 3)
                put_max(b, 2)
                put_max(b, 3)

            def store(b):
                for c in range(2):
                    sp.wait_ge(sem["y_ready"], 2 * b + c + 1)
                    sp.dma_start(out[bass.ds(b, 1)].rearrange("b (t p) d -> p (b t) d", p=P)[:, tiles(c), :],
                                 y_out[:, tiles(c), :]).then_inc(sem["stored"], 16)

            first_groups(0)
            attention(0, False)
            with sp.Fori(0, B - 1) as b:
                sp.wait_ge(sem["x2_ready"], 2 * b + 2)
                load_x(b + 1)
                first_groups(b + 1)
                attention(b + 1, True)
                sp.sem_inc(sem["batch_done"], 1)
            store(B - 1)
            sp.wait_ge(sem["stored"], 32 * B)

        STEPS = 7

        @block.gpsimd
        def _(pool):
            nc.gpsimd.memset(ln_eps[:], LN_EPS)
            nc.gpsimd.memset(rms_eps[:], RMS_EPS)
            nc.gpsimd.memset(neg_half[:], -0.5).then_inc(sem["half_made"], 1)
            pool.wait_ge(sem["half_made"], 1)

            def weights(u):
                pool.wait_ge(sem["wf_hi"], u + 1)
                nc.gpsimd.tensor_tensor(wf[:, u, 1, :], stage[u % 4], wf[:, u, 0, :], ALU.subtract).then_inc(sem["wf_lo"], 1)

            def chain(n, first):
                count = [first]

                def link(ins):
                    ins.then_inc(sem["pool_steps"], 1)
                    count[0] += 1
                    pool.wait_ge(sem["pool_steps"], STEPS * n + count[0])
                return link

            MEAN, VAR = mv[:, :, 0], mv[:, :, 1]

            def rstd1(n):
                pool.wait_ge(sem["stats1"], n + 1)
                link = chain(n, 0)
                link(nc.gpsimd.tensor_tensor(st[:, 0, :], VAR, ln_eps[:], ALU.add))
                link(nc.gpsimd.tensor_tensor(st[:, 2, :], st[:, 0, :], rms_eps[:], ALU.mult))
                link(nc.gpsimd.tensor_tensor(st[:, 1, :], st[:, 2, :], VAR, ALU.add))
                nc.gpsimd.tensor_tensor(st[:, 3, :], st[:, 1, :], neg_half[:], ALU.pow).then_inc(sem["ln1_ready"], 1)

            def rstd2(n):
                pool.wait_ge(sem["stats2"], n + 1)
                link = chain(n, 3)
                link(nc.gpsimd.tensor_tensor(st[:, 0, :], MEAN, MEAN, ALU.mult))
                link(nc.gpsimd.tensor_tensor(st[:, 1, :], st[:, 0, :], VAR, ALU.add))
                link(nc.gpsimd.tensor_tensor(st[:, 0, :], st[:, 1, :], rms_eps[:], ALU.add))
                nc.gpsimd.tensor_tensor(st[:, 4, :], st[:, 0, :], neg_half[:], ALU.pow).then_inc(sem["r2_ready"], 1)

            def rstd3(n):
                pool.wait_ge(sem["stats3"], n + 1)
                link = chain(n, 6)
                link(nc.gpsimd.tensor_tensor(st[:, 0, :], VAR, ln_eps[:], ALU.add))
                nc.gpsimd.tensor_tensor(st[:, 5, :], st[:, 0, :], neg_half[:], ALU.pow).then_inc(sem["ln2_ready"], 1)

            def front(n, s):
                if s == RSTD1:
                    rstd1(n)
                if s == RSTD1 + 2:
                    nc.gpsimd.tensor_tensor(st[:, 2, :], st[:, 0, :], neg_half[:], ALU.pow).then_inc(sem["ln1_ready"], 1)
                if s == RSTD2:
                    rstd2(n)
                if s == RSTD3:
                    rstd3(n)
                for name, i in PE_USES.get(s - 1, ()):
                    if name == "y8":
                        pool.wait_ge(sem["y8_ready"], 2 * n + i + 1)
                        nc.gpsimd.tensor_tensor(x_nat[:, tiles(i), :], x_nat[:, tiles(i), :], y8, ALU.add
                                                ).then_inc(sem["x_y8_ready"], 1)
                    if name in ("ks", "qs"):
                        hi, lo, dst = ("k_hi", "k_lo", kh) if name == "ks" else ("q_hi", "q_lo", qh)
                        pool.wait_ge(sem[hi], 2 * n + i + 1)
                        nc.gpsimd.tensor_tensor(dst[:, 1, HC[i]], misc[:, i, :], dst[:, 0, HC[i]], ALU.subtract
                                                ).then_inc(sem[lo], 1)
                    if name == "fc":
                        f, c = i // 2, i % 2
                        pool.wait_ge(sem["hid_hi"], 2 * FF0 * n + i + 1)
                        nc.gpsimd.tensor_tensor(hid[:, f, T + HALF * c:T + HALF * c + HALF], hid32[i % 2],
                                                hid[:, f, HALF * c:HALF * c + HALF], ALU.subtract).then_inc(sem["hid_lo"], 1)

            def expert_lo(b, s):
                pool.wait_ge(sem["e_hi"], SLOTS * b + s + 1)
                nc.gpsimd.tensor_tensor(e_lo[s % 5], h32[s % 3], e_hi[s % 5], ALU.subtract).then_inc(sem["e_lo"], 1)

            def experts(b, more):
                for s in range(SLOTS + 1):
                    if s:
                        expert_lo(b, s - 1)
                    if more and s < SLOTS:
                        front(b + 1, s)

            for s in range(SLOTS):
                front(0, s)
                for u in UNITS_BEHIND.get(s, ()):
                    weights(u)
                if s == W1_LO:
                    pool.wait_ge(sem["w1_hi"], 2)
                    nc.gpsimd.tensor_tensor(w1[:, 1, :], w1nat, w1[:, 0, :], ALU.subtract).then_inc(sem["w1_lo"], 1)
                    nc.gpsimd.tensor_tensor(w1u[:, 1, :], w1unat, w1u[:, 0, :], ALU.subtract).then_inc(sem["w1_lo"], 1)
            with pool.Fori(0, B - 1) as b:
                experts(b, True)
            experts(B - 1, False)

        @block.tensor
        def _(pe):
            def three(o, whi, wlo, xhi, xlo, start, stop, inc=None):
                nc.tensor.matmul(o, whi, xhi, start=start, stop=False)
                nc.tensor.matmul(o, whi, xlo, start=False, stop=False)
                mm = nc.tensor.matmul(o, wlo, xhi, start=False, stop=stop)
                if inc is not None:
                    mm.then_inc(inc, 1)

            def turn(n, use, src, idt, dst=None):
                wait_free(pe, n, use)
                i = bank(n, use)
                r = (dst or ring)[i]
                for t in range(HT):
                    mm = nc.tensor.transpose(r[:, P * t:P * t + P], src(HT * use[-1] + t), idt)
                mm.then_inc(ring_full[i], 1)

            def product(n, use, w, at, xs, c, rows=P, m=P):
                wait_free(pe, n, use)
                i = bank(n, use)
                three(ring[i][0:m, :], w[0:rows, 0, at], w[0:rows, 1, at], xs[0:rows, 0, HC[c]],
                      xs[0:rows, 1, HC[c]], True, True, ring_full[i])

            def w0block(at):
                return w0[:, :, at, :]

            def front_use(n, use):
                name, c = use
                i = bank(n, use)
                if name == "xrT":
                    pe.wait_ge(sem["xr_ready"], 2 * n + c + 1)
                    turn(n, use, lambda t: xr[:, t, :], ident[:])
                elif name in ("z", "dt", "yact"):
                    if isinstance(n, int) and name == "z" and c == 0:
                        pe.wait_ge(sem["w0_lo"], 2)
                    if name == "z":
                        pe.wait_ge(sem["xrT_lo"], 2 * n + c + 1)
                    product(n, use, w0block({"z": W_Z, "dt": W_DT, "yact": W_YACT}[name]), slice(0, P), xrT, c)
                elif name == "qT":
                    pe.wait_ge(sem["q_ready"], 2 * n + c + 1)
                    turn(n, use, lambda t: qb[:, t, :], ident16[:], ring16)
                elif name == "y8":
                    if isinstance(n, int) and c == 0:
                        pe.wait_ge(sem["kq_ready"], 1)
                    pe.wait_ge(sem["qT_ready"], 2 * n + c + 1)
                    wait_free(pe, n, use)
                    for t in range(HT):
                        at = HALF * c + P * t
                        mm = nc.tensor.matmul(ring[i][:, P * t:P * t + P], qT[:, at:at + P], k8q[:], start=True, stop=True)
                    mm.then_inc(ring_full[i], 1)
                elif name == "y":
                    if c == 0:
                        pe.wait_ge(sem["h_lo"], n + 1)
                    product(n, use, w0block(W_Y), slice(0, P), h_hl, c)
                elif name == "ynat":
                    pe.wait_ge(sem["yT_ready"], 2 * n + c + 1)
                    turn(n, use, lambda t: yT[:, P * t:P * t + P], ident[:])
                elif name == "xr2T":
                    pe.wait_ge(sem["xr2_ready"], 2 * n + c + 1)
                    turn(n, use, lambda t: xr[:, t, :], ident[:])
                elif name in ("fcact", "fc"):
                    if name == "fcact" and c < 2:
                        pe.wait_ge(sem["xr2T_lo"], 2 * n + c + 1)
                    product(n, use, w0block((W_FCACT if name == "fcact" else W_FC) + c // 2), slice(0, P), xrT, c % 2)
                elif name == "out":
                    pe.wait_ge(sem["hid_lo"], 2 * FF0 * n + 2 * FF0 - 1 + c)
                    wait_free(pe, n, use)
                    for f in range(FF0):
                        three(ring[i][:], w0[:, 0, W_OUT + f, :], w0[:, 1, W_OUT + f, :],
                              hid[:, f, HALF * c:HALF * c + HALF], hid[:, f, T + HALF * c:T + HALF * c + HALF],
                              f == 0, f == FF0 - 1, ring_full[i] if f == FF0 - 1 else None)
                elif name == "onat":
                    pe.wait_ge(sem["oT_ready"], 2 * n + c + 1)
                    turn(n, use, lambda t: oT[:, P * t:P * t + P], ident[:])
                elif name == "xT":
                    pe.wait_ge(sem["xn2_ready"], 2 * n + c + 1)
                    turn(n, use, lambda t: xr[:, t, :], ident[:])
                elif name == "lat":
                    if isinstance(n, int) and c == 0:
                        pe.wait_ge(sem["w1_lo"], 2)
                    pe.wait_ge(sem["xT_lo"], 2 * n + c + 1)
                    product(n, use, w1, WDN, xT, c, m=LAT)
                elif name in ("k", "ks"):
                    pe.wait_ge(sem["lat_lo"], 2 * n + c + 1)
                    product(n, use, w1u, WK if name == "k" else WKS, latT, c, rows=LAT)
                elif name in ("q", "qs"):
                    product(n, use, w1, WQ if name == "q" else WQS, xT, c)
                elif name == "v":
                    wait_free(pe, n, use)
                    for t in range(HT):
                        at = slice(HALF * c + P * t, HALF * c + P * t + P)
                        three(ring[i][:, P * t:P * t + P], latT[:, 0, at], latT[:, 1, at], w1u[:, 0, WV], w1u[:, 1, WV],
                              True, True, ring_full[i] if t == HT - 1 else None)

            def scores(b, g, u):
                use = ("s", g, u)
                h, pieces = u // len(S_USES), S_USES[u % len(S_USES)]
                if u == 0:
                    pe.wait_ge(qk_loaded[g % 3], 16 * 6 * filled(b, g))
                    if isinstance(b, int) and b == 0 and g == 0:
                        pe.wait_ge(sem["masks_loaded"], 16 * 6)
                wait_free(pe, b, use)
                i = bank(b, use)
                for q, k0, kn, col in pieces:
                    mm = nc.tensor.matmul(ring[i][:, col:col + kn], QO[g % 3][0:S_ROWS, h, P * q:P * q + P],
                                          KO[g % 3][0:S_ROWS, h, k0:k0 + kn], start=True, stop=True)
                mm.then_inc(ring_full[i], 1)

            def maxima(b, g):
                pe.wait_ge(sem["max_steps"], 3 * (NG * b + g + 1))
                use = ("s", g, NS)
                wait_free(pe, b, use)
                i = bank(b, use)
                nc.tensor.matmul(ring[i][0:2 * G * NT, 0:P], mhl[:].rearrange("p s n -> p (s n)"), ident16[:],
                                 start=True, stop=True).then_inc(ring_full[i], 1)

            def front(n, s):
                for use in PE_USES.get(s, ()):
                    front_use(n, use)

            def first_scores(n, s, i):
                for u in s0_uses(s)[i:i + 1]:
                    scores(n, 0, u)

            def first_maxima(n, s):
                if s == MAX0_SLOT:
                    maxima(n, 0)

            def pack(b, g, k):
                no = NPACK * (NG * b + g) + k
                if k == 0:
                    pe.wait_ge(max_loaded[g % 3], 16 * filled(b, g))
                if g > 0 or k >= 2:
                    pe.wait_ge(sem["exp_done"], no - 1)
                for h, j, col in PACKS[k][2]:
                    q0 = P * j
                    while q0 < T:
                        at = col + q0 - P * j
                        n = min(T - q0, HALF - at % HALF)
                        mm = nc.tensor.matmul(pair[k % 2][:, at:at + n], KO[g % 3][0:ST_ROWS, h, P * j:P * j + P],
                                              QO[g % 3][0:ST_ROWS, h, q0:q0 + n], start=True, stop=True)
                        q0 += n
                mm.then_inc(sem["st_full"], 1)

            def times_v(b, g, p, i):
                if i == 0:
                    last = max(k for k in range(NPACK) if PACKS[k][0] == p)
                    pe.wait_ge(sem["exp_done"], NPACK * (NG * b + g) + last + 1)
                if i == 0 and p == 0:
                    if g > 0:
                        pe.wait_ge(sem["po_ready"], 2 * (NG * b + g))
                    else:
                        pe.wait_ge(sem["v_ready"], 2 * b + 2)
                buf = (len(SETS) * g + p) % 2
                j, c = PIECES[p][i]
                q0 = max(HALF * c, P * j)
                n = HALF * c + HALF - q0
                for h in range(G):
                    place, col = WHERE[h, j]
                    at = col + q0 - P * j
                    mm = nc.tensor.matmul(acc[c][32 * h:32 * h + D + 1, q0 - HALF * c:HALF],
                                          v1[:, j, G * g + h, :], probs[:, buf, place, at:at + n],
                                          start=(j == 0), stop=(j == (3 if c == 0 else 4)))
                if i == len(PIECES[p]) - 1:
                    mm.then_inc(sem["pv_done"], 1)

            def output(b, g):
                for c in range(2):
                    pe.wait_ge(sem["po_ready"], 2 * (NG * b + g) + c + 1)
                    turn(b, ("o", g, c), lambda t: po[:, P * t:P * t + P], ident[:])

            def finish(b):
                for c in range(2):
                    pe.wait_ge(sem["fT_ready"], 2 * b + c + 1)
                    turn(b, ("fin", c), lambda t: fT[:, P * t:P * t + P], ident[:])

            def attention(b, fin):
                for g in range(NG):
                    for k in range(NPACK):
                        pieces = [(g - back, p, i) for back, p, i in PV_BEHIND.get(k, ()) if g >= back]
                        uses = list(s_uses(g, k)) if g + 1 < NG else []
                        if k == 0 and g > 0:
                            for u in uses[:S_BEFORE]:
                                scores(b, g + 1, u)
                            uses = uses[S_BEFORE:]
                        for step in range(max(len(uses), 1 + len(pieces))):
                            if step < len(uses):
                                scores(b, g + 1, uses[step])
                            if step == 0:
                                pack(b, g, k)
                            elif step <= len(pieces):
                                times_v(b, *pieces[step - 1])
                        if k == OUT_BEHIND and g > 0:
                            output(b, g - 1)
                        if k == FIN_BEHIND and g == 0 and fin:
                            finish(b - 1)
                        if k == MAX_BEHIND and g + 1 < NG:
                            maxima(b, g + 1)
                times_v(b, NG - 1, len(SETS) - 1, 0)
                gate_up(b, 0)
                output(b, NG - 1)
                for c in range(2):
                    for t in range(HT):
                        nc.tensor.matmul(acc[c][:, P * t:P * t + P], x2[:, HT * c + t, :], ident[:], start=t == 0, stop=False)
                pe.wait_ge(sem["att_ready"], 2 * NG * (b + 1))
                for c in range(2):
                    turn(b, ("attT", c), lambda t: att[:, t, :], ident[:])
                gate_up(b, 1)
                for c in range(2):
                    pe.wait_ge(sem["attT_lo"], 2 * b + c + 1)
                    three(acc[c][:], w1[:, 0, WO], w1[:, 1, WO], attT[:, 0, HC[c]], attT[:, 1, HC[c]], False, False)

            def unit(s):
                return s // (2 * FE), s // 2 % FE, s % 2

            def gate_up(b, s, between=None):
                e, f, c = unit(s)
                if s == 0:
                    pe.wait_ge(sem["handed_over"], 16 * (b + 1))
                    pe.wait_ge(sem["wf_lo"], 3 * NE)
                ws = slice(P * f, P * f + P)
                for k, (name, freed) in enumerate((("gate_full", "silu_ready"), ("up_full", "h32_ready"))):
                    if s >= 2:
                        pe.wait_ge(sem[freed], SLOTS * b + s - 1)
                    else:
                        pe.wait_ge(sem["exp_done"], NPACK * NG * (b + 1))
                    three(pair[k][:, HC[s % 2]], wf[:, 3 * e + k, 0, ws], wf[:, 3 * e + k, 1, ws],
                          exT[:, 0, HC[c]], exT[:, 1, HC[c]], True, True, sem[name])
                    if k == 0 and between is not None:
                        first_scores(between, s, 0)

            def down(b, s):
                e, f, c = unit(s)
                pe.wait_ge(sem["e_lo"], SLOTS * b + s + 1)
                ws = slice(P * f, P * f + P)
                three(acc[c][:], wf[:, 3 * e + 2, 0, ws], wf[:, 3 * e + 2, 1, ws], e_hi[s % 5], e_lo[s % 5],
                      False, s >= SLOTS - 2, sem["down_done"])

            def experts(b, more):
                for s in range(SLOTS + LAG):
                    if s < SLOTS:
                        if s >= EARLY:
                            gate_up(b, s, b + 1 if more else None)
                        if more:
                            front(b + 1, s)
                            first_scores(b + 1, s, 1)
                    if s >= LAG:
                        down(b, s - LAG)
                    if more and s < SLOTS:
                        first_scores(b + 1, s, 2)
                        first_maxima(b + 1, s)
                    if more and s >= SLOTS:
                        for u in tail_uses(s - SLOTS):
                            scores(b + 1, 1, u)

            pe.wait_ge(sem["ident_loaded"], 16)
            pe.wait_ge(sem["v_ones"], 1)
            pe.wait_ge(sem["outs_made"], 1)
            pe.wait_ge(sem["vec_steps"], 1)
            for s in range(SLOTS):
                front(0, s)
                for i in range(3):
                    first_scores(0, s, i)
                first_maxima(0, s)
            for u in range(sum(S_TAIL)):
                scores(0, 1, u)
            attention(0, False)
            with pe.Fori(0, B - 1) as b:
                experts(b, True)
                attention(b + 1, True)
            experts(B - 1, False)
            finish(B - 1)

        @block.scalar
        def _(act):
            act.wait_ge(sem["w0_loaded"], 2 * 16)
            for i in range(2):
                nc.scalar.activation(w0[:, 0, 8 * i:8 * i + 8, :].rearrange("p a b -> p (a b)"), w0nat[:, T * i:T * i + T],
                                     ACT.Copy).then_inc(sem["w0_hi"], 1)
            act.wait_ge(sem["w1_loaded"], 2 * 16)
            nc.scalar.activation(w1[:, 0, :], w1nat, ACT.Copy).then_inc(sem["w1_hi"], 1)
            nc.scalar.activation(w1u[:, 0, :], w1unat, ACT.Copy).then_inc(sem["w1_hi"], 1)
            act.wait_ge(sem["vec_loaded"], 16)
            act.wait_ge(sem["vec_steps"], 1)

            def vcol(i):
                return vec[:, i:i + 1]

            def hi_of(n, use, dst, name, scale=1.0, rows=P):
                wait_full(act, n, use)
                nc.scalar.activation(dst[0:rows, 0, HC[use[1]]], ring[bank(n, use)][0:rows, :], ACT.Copy,
                                     scale=scale).then_inc(sem[name], 1)

            def front_use(n, use):
                name, c = use
                r = ring[bank(n, use)]
                if name == "xrT":
                    hi_of(n, use, xrT, "xrT_hi", vcol(V_GSIO))
                elif name == "z":
                    if isinstance(n, int) and c == 0:
                        act.wait_ge(sem["w0_lo"], 2)
                    wait_full(act, n, use)
                    nc.scalar.activation(sz[:, HC[c]], r[:], ACT.Sigmoid, bias=vcol(V_BZ)).then_inc(sem["sz_ready"], 1)
                elif name == "dt":
                    wait_full(act, n, use)
                    nc.scalar.activation(sdt[:, HC[c]], r[:], ACT.Sigmoid, bias=vcol(V_BDT)).then_inc(sem["sdt_ready"], 1)
                    nc.scalar.activation(a_dec[:, HC[c]], r[:], ACT.Sigmoid, scale=-1.0,
                                         bias=vcol(V_NBDT)).then_inc(sem["a_ready"], 1)
                elif name == "yact":
                    wait_full(act, n, use)
                    nc.scalar.activation(sy[:, HC[c]], r[:], ACT.Silu, bias=vcol(V_BYACT)).then_inc(sem["yact_ready"], 1)
                elif name == "qT":
                    wait_full(act, n, use)
                    nc.scalar.activation(qT[:, HC[c]], ring16[bank(n, use)][:, 0:HALF], ACT.Copy).then_inc(sem["qT_ready"], 1)
                elif name == "xr2T":
                    hi_of(n, use, xrT, "xr2T_hi", vcol(V_GFFN))
                elif name == "fcact":
                    if c >= 2:
                        act.wait_ge(sem["hid_ready"], 2 * FF0 * n + c - 1)
                    wait_full(act, n, use)
                    nc.scalar.activation(gated[:, c % 2, :], r[:], ACT.Silu,
                                         bias=vcol(V_BFCACT + c // 2)).then_inc(sem["fcact_ready"], 1)
                elif name == "out":
                    wait_full(act, n, use)
                    nc.scalar.activation(oT[:, HC[c]], r[:], ACT.Identity, bias=vcol(V_BOUT)).then_inc(sem["oT_ready"], 1)
                elif name == "xT":
                    hi_of(n, use, xT, "xT_hi")
                elif name == "lat":
                    hi_of(n, use, latT, "lat_hi", rows=LAT)
                elif name == "v":
                    wait_full(act, n, use)
                    nc.scalar.activation(v1[:, tiles(c), :, 0:D], r[:].rearrange("p (t h d) -> p t h d", t=HT, h=H),
                                         ACT.Copy).then_inc(sem["v_ready"], 1)

            def front_hi(n, use):
                name, c = use
                if name == "fc":
                    act.wait_ge(sem["hid_ready"], 2 * FF0 * n + c + 1)
                    nc.scalar.activation(hid[:, c // 2, HALF * (c % 2):HALF * (c % 2) + HALF], hid32[c % 2],
                                         ACT.Copy).then_inc(sem["hid_hi"], 1)
                elif name in ("ks", "qs"):
                    which, dst = ("k_hi", kh) if name == "ks" else ("q_hi", qh)
                    act.wait_ge(sem["rot_ready"], 4 * n + (0 if name == "ks" else 2) + c + 1)
                    nc.scalar.activation(dst[:, 0, HC[c]], misc[:, c, :], ACT.Copy).then_inc(sem[which], 1)

            def front(n, s):
                for use in PE_USES.get(s, ()):
                    front_use(n, use)
                for use in PE_USES.get(s - 1, ()):
                    front_hi(n, use)
                if s == SCAN + 1:
                    act.wait_ge(sem["h_ready"], n + 1)
                    nc.scalar.activation(h_hl[:, 0, :], hT, ACT.Copy).then_inc(sem["h_hi"], 1)

            def weights(u):
                act.wait_ge(w_staged[u % 4], 16 * (u // 4 + 1))
                nc.scalar.activation(wf[:, u, 0, :], stage[u % 4], ACT.Copy).then_inc(sem["wf_hi"], 1)

            def copy_out(b, g):
                act.wait_ge(sem["pv_done"], len(SETS) * (NG * b + g + 1))
                for c in range(2):
                    nc.scalar.activation(po[:, HC[c]], acc[c][:], ACT.Copy).then_inc(sem["po_ready"], 1)

            def result(b):
                for c in range(2):
                    use = ("fin", c)
                    wait_full(act, b, use)
                    nc.scalar.activation(y_out[:, tiles(c), :], ring[bank(b, use)][:].rearrange("p (t d) -> p t d", d=P),
                                         ACT.Copy).then_inc(sem["y_ready"], 1)

            def finish(b):
                for c in range(2):
                    act.wait_ge(sem["down_done"], SLOTS * b + SLOTS - 1 + c)
                    nc.scalar.activation(fT[:, HC[c]], acc[c][:], ACT.Copy).then_inc(sem["fT_ready"], 1)

            def attention(b, fin):
                if fin:
                    finish(b - 1)
                for g in range(NG):
                    for k in range(NPACK):
                        p, place, items = PACKS[k]
                        n = sum(columns(j) for _, j, _ in items)
                        buf = (len(SETS) * g + p) % 2
                        if place == 0 and (g > 0 or p >= 2):
                            act.wait_ge(sem["pv_done"], len(SETS) * (NG * b + g) + p - 1)
                        act.wait_ge(sem["st_full"], NPACK * (NG * b + g) + k + 1)
                        nc.scalar.activation(probs[:, buf, place, 0:n], pair[k % 2][:, 0:n], ACT.Exp,
                                             scale=SCALE).then_inc(sem["exp_done"], 1)
                        if k == PO_BEHIND and g > 0:
                            copy_out(b, g - 1)
                        if k == FIN_BEHIND and g == 0 and fin:
                            result(b - 1)
                copy_out(b, NG - 1)
                expert_silu(b, 0)
                for c in range(2):
                    use = ("attT", c)
                    wait_full(act, b, use)
                    nc.scalar.activation(attT[:, 0, HC[c]], ring[bank(b, use)][:], ACT.Copy).then_inc(sem["attT_hi"], 1)

            def expert_silu(b, s):
                if s >= 2:
                    act.wait_ge(sem["h32_ready"], SLOTS * b + s - 1)
                act.wait_ge(sem["gate_full"], SLOTS * b + s + 1)
                nc.scalar.activation(sg[:, s % 2, :], pair[0][:, HC[s % 2]], ACT.Silu).then_inc(sem["silu_ready"], 1)

            def expert_hi(b, s):
                if s >= 5:
                    act.wait_ge(sem["down_done"], SLOTS * b + s - 4)
                act.wait_ge(sem["h32_ready"], SLOTS * b + s + 1)
                nc.scalar.activation(e_hi[s % 5], h32[s % 3], ACT.Copy).then_inc(sem["e_hi"], 1)

            def experts(b, more):
                for s in range(SLOTS + 1):
                    if 1 <= s < SLOTS:
                        expert_silu(b, s)
                    if s:
                        expert_hi(b, s - 1)
                    if more and s < SLOTS:
                        front(b + 1, s)

            for s in range(SLOTS):
                front(0, s)
                for u in UNITS_BEHIND.get(s, ()):
                    weights(u)
            attention(0, False)
            with act.Fori(0, B - 1) as b:
                experts(b, True)
                attention(b + 1, True)
            experts(B - 1, False)
            finish(B - 1)
            result(B - 1)

        @block.vector
        def _(dve):
            def col(i):
                return vec[:, i:i + 1]

            nc.vector.memset(v1[:, :, :, D:D + 1], 1.0).then_inc(sem["v_ones"], 1)
            for z in acc:
                ins = nc.vector.memset(z[:], 0.0)
            ins.then_inc(sem["outs_made"], 1)
            dve.wait_ge(sem["vec_loaded"], 16)
            dve.wait_ge(sem["ident_loaded"], 16)
            nc.vector.tensor_copy(ident16[:], ident[:])
            nc.vector.tensor_scalar(col(V_NBDT), col(V_BDT), -1.0, None, ALU.mult)
            nc.vector.reciprocal(col(V_RIN), col(V_SIN))
            nc.vector.reciprocal(col(V_RK), col(V_SK))
            nc.vector.tensor_tensor(col(V_SC), col(V_SIN), col(V_SK), ALU.mult).then_inc(sem["vec_steps"], 1)
            dve.wait_ge(sem["vec_steps"], 1)

            def quantise(dst, src, rcp, shape, step, parts=(0, 1)):
                v, m = (tmp[:, i, 0:shape[0] * shape[1]] for i in range(2))
                v3 = v.rearrange("p (a b) -> p a b", b=shape[1])
                m3 = m.rearrange("p (a b) -> p a b", b=shape[1])
                if 0 in parts:
                    step(nc.vector.tensor_scalar(v3, src, rcp, None, ALU.mult))
                    step(nc.vector.tensor_scalar(m.bitcast(U32), v.bitcast(U32), 0x7F800000, None, ALU.bitwise_and))
                    step(nc.vector.tensor_scalar(m, m, 2.0 ** -6, 1.5 * 2.0 ** 20, ALU.max, ALU.mult))
                if 1 in parts:
                    step(nc.vector.tensor_tensor(v, v, m, ALU.add))
                    return nc.vector.tensor_tensor(dst, v3, m3, ALU.subtract)

            def weights_lo():
                for i in range(2):
                    dve.wait_ge(sem["w0_hi"], i + 1)
                    nc.vector.tensor_tensor(w0[:, 1, 8 * i:8 * i + 8, :].rearrange("p a b -> p (a b)"),
                                            w0nat[:, T * i:T * i + T],
                                            w0[:, 0, 8 * i:8 * i + 8, :].rearrange("p a b -> p (a b)"),
                                            ALU.subtract).then_inc(sem["w0_lo"], 1)

            def quantise_kernel():
                count = [1]

                def link(ins):
                    ins.then_inc(sem["vec_steps"], 1)
                    count[0] += 1
                    dve.wait_ge(sem["vec_steps"], count[0])
                dve.wait_ge(sem["k8_loaded"], 2 * 16)
                big = tmp[:, 1, 256:384]
                link(nc.vector.tensor_scalar(big, k8b[:], col(V_RK), None, ALU.mult))
                link(nc.vector.tensor_scalar(tmp[:, 1, 384:512].bitcast(U32), big.bitcast(U32), 0x7FFFFFFF, None, ALU.bitwise_and))
                link(nc.vector.tensor_scalar(big, tmp[:, 1, 384:512], 464.0, 3e38, ALU.is_gt, ALU.mult))
                link(nc.vector.tensor_scalar(big, big, 3e38, 0.0, ALU.mult, ALU.mult))
                link(quantise(k8q[:].rearrange("p (a b) -> p a b", a=1), k8b[:].rearrange("p (a b) -> p a b", a=1),
                              col(V_RK), (1, P), link))
                nc.vector.tensor_tensor(k8q[:], k8q[:], big, ALU.add).then_inc(sem["kq_ready"], 1)
                dve.wait_ge(sem["kq_ready"], 1)

            def lo_of(n, use, dst, hi, name, scale=1.0, rows=P):
                c = use[1]
                dve.wait_ge(sem[hi], 2 * n + c + 1)
                nc.vector.scalar_tensor_tensor(dst[0:rows, 1, HC[c]], ring[bank(n, use)][0:rows, :], scale,
                                               dst[0:rows, 0, HC[c]], ALU.mult, ALU.subtract).then_inc(sem[name], 1)

            def row_stats(src, half):
                for t in range(HT * half, HT * half + HT):
                    ins = nc.vector.bn_stats(raw6[:, t, :], src[:, t, :])
                return ins

            def aggregate(rows, name, n):
                dve.wait_ge(sem[rows], n + 1)
                dve.sem_inc(sem["rows_counted"], 1)
                for t in range(NT):
                    ins = nc.vector.bn_aggr(mv[:, t, :], raw6[:, t, :])
                ins.then_inc(sem[name], 1)

            QSTEPS = 8

            def centred(dst, src, scale_row, half):
                for t in range(HT * half, HT * half + HT):
                    ins = nc.vector.tensor_scalar(dst[:, t, :], src[:, t, :], mv[:, t, 0:1], st[:, scale_row, t:t + 1],
                                                  ALU.subtract, ALU.mult)
                return ins

            def quantise_half(n, half, part):
                k = [4 * half + 3 * part]

                def step(ins):
                    ins.then_inc(sem["quant_steps"], 1)
                    k[0] += 1
                    dve.wait_ge(sem["quant_steps"], QSTEPS * n + k[0])
                last = quantise(qb[:, tiles(half), :], xb[:, tiles(half), :], col(V_RIN), (HT, P), step, (part,))
                if part:
                    last.then_inc(sem["q_ready"], 1)

            def scale_of_tokens(n):
                dve.wait_ge(sem["amax_ready"], n + 1)
                nc.vector.tensor_scalar(amax[:], amax[:], col(V_RIN), 464.0, ALU.mult, ALU.is_gt).then_inc(sem["sc_ready"], 1)
                dve.wait_ge(sem["sc_ready"], 3 * n + 1)
                nc.vector.tensor_scalar(amax[:], amax[:], 3e38, 3e38, ALU.mult, ALU.mult).then_inc(sem["sc_ready"], 1)
                dve.wait_ge(sem["sc_ready"], 3 * n + 2)
                nc.vector.tensor_scalar(sc_tok[:], amax[:], 0.0, col(V_SC), ALU.mult, ALU.add).then_inc(sem["sc_ready"], 1)

            def front_use(n, use):
                name, c = use
                r = ring[bank(n, use)]
                r3 = r[:].rearrange("p (t d) -> p t d", d=P)
                if name == "xrT":
                    lo_of(n, use, xrT, "xrT_hi", "xrT_lo", col(V_GSIO))
                elif name == "y8":
                    wait_full(dve, n, use)
                    dve.wait_ge(sem["sc_ready"], 3 * n + 3)
                    if c == 1:
                        dve.wait_ge(sem["x_y8_ready"], 2 * n + 1)
                    for t in range(HT):
                        ins = nc.vector.tensor_scalar(y8[:, t, :], r[:, P * t:P * t + P],
                                                      sc_tok[:, HT * c + t:HT * c + t + 1], None, ALU.mult)
                    ins.then_inc(sem["y8_read"], 1)
                    dve.wait_ge(sem["y8_read"], 2 * n + c + 1)
                    nc.vector.tensor_tensor(y8, y8, bias_bc[:].rearrange("p (o d) -> p o d", o=1).to_broadcast([P, HT, P]),
                                            ALU.add).then_inc(sem["y8_ready"], 1)
                elif name == "y":
                    wait_full(dve, n, use)
                    dve.wait_ge(sem["yact_ready"], 2 * n + c + 1)
                    nc.vector.scalar_tensor_tensor(yT[:, HC[c]], r[:], col(V_BY), sy[:, HC[c]],
                                                   ALU.add, ALU.mult).then_inc(sem["yT_ready"], 1)
                elif name == "ynat":
                    wait_full(dve, n, use)
                    nc.vector.tensor_tensor(x1[:, tiles(c), :], r3, xn[:, tiles(c), :], ALU.add).then_inc(sem["x1_ready"], 1)
                elif name == "xr2T":
                    lo_of(n, use, xrT, "xr2T_hi", "xr2T_lo", col(V_GFFN))
                elif name == "fc":
                    if c >= 2:
                        dve.wait_ge(sem["hid_lo"], 2 * FF0 * n + c - 1)
                    dve.wait_ge(sem["fcact_ready"], 2 * FF0 * n + c + 1)
                    wait_full(dve, n, use)
                    nc.vector.scalar_tensor_tensor(hid32[c % 2], r[:], col(V_BFC + c // 2), gated[:, c % 2, :],
                                                   ALU.add, ALU.mult).then_inc(sem["hid_ready"], 1)
                elif name == "onat":
                    wait_full(dve, n, use)
                    nc.vector.tensor_tensor(x2[:, tiles(c), :], r3, x1[:, tiles(c), :], ALU.add).then_inc(sem["onat_read"], 1)
                    dve.wait_ge(sem["onat_read"], 2 * n + c + 1)
                    dve.wait_ge(sem["x_y8_ready"], 2 * n + c + 1)
                    nc.vector.tensor_tensor(x2[:, tiles(c), :], x2[:, tiles(c), :], x_nat[:, tiles(c), :],
                                            ALU.add).then_inc(sem["x2_ready"], 1)
                elif name == "xT":
                    lo_of(n, use, xT, "xT_hi", "xT_lo")
                elif name == "lat":
                    lo_of(n, use, latT, "lat_hi", "lat_lo", rows=LAT)
                elif name in ("k", "q"):
                    before = (0 if name == "k" else 2) + c
                    if isinstance(n, int) and before == 0:
                        dve.wait_ge(sem["rope_loaded"], 2 * 16)
                    if before:
                        dve.wait_ge(sem["rot_ready"], 4 * n + before)
                    wait_full(dve, n, use)
                    nc.vector.tensor_tensor(tmp[:, 0, :], r[:], cos[:, HC[c]], ALU.mult).then_inc(sem["rope1"], 1)
                elif name in ("ks", "qs"):
                    j = 4 * n + (0 if name == "ks" else 2) + c
                    wait_full(dve, n, use)
                    nc.vector.tensor_tensor(tmp[:, 1, :], r[:], sin[:, HC[c]], ALU.mult).then_inc(sem["rope2"], 1)
                    if name == "qs":
                        dve.wait_ge(sem["k_lo"], 2 * n + c + 1)
                    dve.wait_ge(sem["rope1"], j + 1)
                    dve.wait_ge(sem["rope2"], j + 1)
                    nc.vector.tensor_tensor(misc[:, c, :], tmp[:, 0, :], tmp[:, 1, :], ALU.add).then_inc(sem["rot_ready"], 1)

            def half_of(s, first):
                return s - first if s in (first, first + 1) else None

            def front(n, s):
                if s == STATS1:
                    dve.wait_ge(sem["x_loaded"], 16 * n + 16)
                    row_stats(x_nat, 0)
                    row_stats(x_nat, 1).then_inc(sem["rows1"], 1)
                if s == RSTD1:
                    aggregate("rows1", "stats1", n)
                if (half := half_of(s, XR)) is not None:
                    dve.wait_ge(sem["ln1_ready"], 2 * n + 1)
                    centred(xr, x_nat, 3, half).then_inc(sem["xr_ready"], 1)
                if s == H_LO:
                    dve.wait_ge(sem["h_hi"], n + 1)
                    nc.vector.tensor_tensor(h_hl[:, 1, :], hT, h_hl[:, 0, :], ALU.subtract).then_inc(sem["h_lo"], 1)
                if s == B_IN:
                    for c in range(2):
                        dve.wait_ge(sem["sdt_ready"], 2 * n + c + 1)
                        nc.vector.tensor_tensor(sz[:, HC[c]], sz[:, HC[c]], sdt[:, HC[c]], ALU.mult).then_inc(sem["b_ready"], 1)
                if s == SCAN:
                    dve.wait_ge(sem["b_ready"], 2 * n + 2)
                    dve.wait_ge(sem["a_ready"], 2 * n + 2)
                    nc.vector.tensor_tensor_scan(hT, a_dec, sz, col(V_H0), ALU.mult, ALU.add).then_inc(sem["h_ready"], 1)
                if (half := half_of(s, XR2)) is not None:
                    dve.wait_ge(sem["r2_ready"], n + 1)
                    for t in range(HT * half, HT * half + HT):
                        ins = nc.vector.tensor_scalar(xr[:, t, :], x1[:, t, :], st[:, 4, t:t + 1], None, ALU.mult)
                    ins.then_inc(sem["xr2_ready"], 1)
                if (half := half_of(s, XN2)) is not None:
                    dve.wait_ge(sem["ln2_ready"], n + 1)
                    centred(xr, x2, 5, half).then_inc(sem["xn2_ready"], 1)
                for use in PE_USES.get(s, ()):
                    front_use(n, use)
                if (half := half_of(s, XN)) is not None:
                    dve.wait_ge(sem["ln1_ready"], 2 * n + 2)
                    centred(xn, x_nat, 2, half).then_inc(sem["xn_ready"], 1)
                if s == XB:
                    dve.wait_ge(sem["xn_ready"], 2 * n + 2)
                    nc.vector.tensor_copy(xb, xn[:]).then_inc(sem["xb_ready"], 1)
                if s == AMAX:
                    dve.wait_ge(sem["xb_ready"], n + 1)
                    nc.vector.tensor_reduce(amax[:], xb, AX.X, ALU.max, apply_absolute_value=True).then_inc(sem["amax_ready"], 1)
                if (part := half_of(s, QUANT0)) is not None:
                    quantise_half(n, 0, part)
                if s == SCALES:
                    scale_of_tokens(n)
                if (half := half_of(s, STATS2)) is not None:
                    dve.wait_ge(sem["x1_ready"], 2 * n + half + 1)
                    ins = row_stats(x1, half)
                    if half:
                        ins.then_inc(sem["rows2"], 1)
                if s == RSTD2:
                    aggregate("rows2", "stats2", n)
                if (part := half_of(s, QUANT1)) is not None:
                    dve.wait_ge(sem["x_y8_ready"], 2 * n + 1)
                    quantise_half(n, 1, part)
                if (half := half_of(s, STATS3)) is not None:
                    dve.wait_ge(sem["x2_ready"], 2 * n + half + 1)
                    ins = row_stats(x2, half)
                    if half:
                        ins.then_inc(sem["rows3"], 1)
                if s == RSTD3:
                    aggregate("rows3", "stats3", n)

            def first_scores(n, s, places):
                for u in s0_uses(s)[places]:
                    scores(n, 0, u)
                    if u == NS - 1:
                        maxima_steps(n, 0)
                if s == MAX0_SLOT and places.stop is None:
                    maxima_rows(n, 0)

            def scores(b, g, u):
                use = ("s", g, u)
                r = ring[bank(b, use)]
                h, m = u // len(S_USES), mx[g % 2]
                pieces = S_USES[u % len(S_USES)]
                wait_full(dve, b, use)
                if len(pieces) == 2 and pieces[0][2] == pieces[1][2]:
                    (i0, _, n, _), (i1, k1, _, _) = pieces
                    cols = (i0, i1 + (4 if k1 else 0))
                    ins = nc.vector.tensor_reduce(m[:, h, cols[0]:cols[1] + 1:cols[1] - cols[0]],
                                                  r[:].rearrange("p (a k) -> p a k", k=n), AX.X, ALU.max)
                else:
                    for i, k0, n, at in pieces:
                        to = i + (4 if k0 else 0)
                        ins = nc.vector.tensor_reduce(m[:, h, to:to + 1], r[:, at:at + n], AX.X, ALU.max)
                ins.then_inc(sem["scores_read"], 1)

            def maxima_steps(b, g):
                m = mx[g % 2]
                done = 3 * (NG * b + g)
                dve.wait_ge(sem["scores_read"], NS * (NG * b + g + 1))
                nc.vector.tensor_tensor(m[:, :, 4:8], m[:, :, 4:8], m[:, :, 8:12], ALU.max).then_inc(sem["max_steps"], 1)
                dve.wait_ge(sem["max_steps"], done + 1)
                parts = [mhl[:, s, :].rearrange("p (h i) -> p h i", h=G) for s in range(2)]
                nc.vector.tensor_scalar(parts[0], m[:, :, 0:8], -1.0, None, ALU.mult).then_inc(sem["max_steps"], 1)
                dve.wait_ge(sem["max_steps"], done + 2)
                nc.vector.scalar_tensor_tensor(parts[1], m[:, :, 0:8], -1.0, parts[0], ALU.mult, ALU.subtract
                                               ).then_inc(sem["max_steps"], 1)

            def maxima_rows(b, g):
                use = ("s", g, NS)
                wait_full(dve, b, use)
                if not (isinstance(b, int) and b == 0 and g == 0):
                    before = (g - 1) % NG
                    dve.wait_ge(max_loaded[before % 3], 16 * (filled(b, before) if g else 2 * b))
                nc.vector.tensor_copy(maxrow[:], ring[bank(b, use)][0:2 * G * NT, 0:P]).then_inc(sem["maxrow_ready"], 1)

            def output(b, g):
                if g == 0 and not (isinstance(b, int) and b == 0):
                    dve.wait_ge(sem["stored"], 32 * b)
                parts = [ring[bank(b, ("o", g, c))][:].rearrange("p (t h r) -> p t h r", t=HT, h=G) for c in range(2)]
                for c in range(2):
                    wait_full(dve, b, ("o", g, c))
                    nc.vector.reciprocal(rden[:, c], parts[c][:, :, :, D]).then_inc(sem["rden_ready"], 1)
                for c in range(2):
                    dve.wait_ge(sem["rden_ready"], 2 * (NG * b + g) + c + 1)
                    nc.vector.tensor_tensor(att[:, tiles(c), 32 * g:32 * g + 32].rearrange("p t (h d) -> p t h d", h=G),
                                            parts[c][:, :, :, 0:D],
                                            rden[:, c].rearrange("p t (h o) -> p t h o", o=1).to_broadcast([P, HT, G, D]),
                                            ALU.mult).then_inc(sem["att_ready"], 1)

            def attention(b, fin):
                for g in range(NG):
                    for k in range(NPACK):
                        if g + 1 < NG:
                            for u in s_uses(g, k):
                                scores(b, g + 1, u)
                                if u == NS - 1:
                                    maxima_steps(b, g + 1)
                        if k == OUT_BEHIND and g > 0:
                            output(b, g - 1)
                    if g + 1 < NG:
                        maxima_rows(b, g + 1)
                output(b, NG - 1)
                for c in range(2):
                    dve.wait_ge(sem["attT_hi"], 2 * b + c + 1)
                    nc.vector.tensor_tensor(attT[:, 1, HC[c]], ring[bank(b, ("attT", c))][:], attT[:, 0, HC[c]], ALU.subtract
                                            ).then_inc(sem["attT_lo"], 1)

            def expert_gated(b, s):
                if s >= 3:
                    dve.wait_ge(sem["e_lo"], SLOTS * b + s - 2)
                dve.wait_ge(sem["silu_ready"], SLOTS * b + s + 1)
                dve.wait_ge(sem["up_full"], SLOTS * b + s + 1)
                nc.vector.tensor_tensor(h32[s % 3], pair[1][:, HC[s % 2]], sg[:, s % 2, :], ALU.mult).then_inc(sem["h32_ready"], 1)

            def experts(b, more):
                for s in range(SLOTS):
                    if more:
                        first_scores(b + 1, s, slice(0, 1))
                    expert_gated(b, s)
                    if more:
                        front(b + 1, s)
                        first_scores(b + 1, s, slice(1, None))
                if more:
                    for u in range(sum(S_TAIL)):
                        scores(b + 1, 1, u)

            for s in range(SLOTS):
                front(0, s)
                first_scores(0, s, slice(0, None))
                if s == 1:
                    weights_lo()
                if s == KERNEL8:
                    if KERNEL8 > QUANT0:
                        dve.wait_ge(sem["q_ready"], 1)
                    quantise_kernel()
            for u in range(sum(S_TAIL)):
                scores(0, 1, u)
            attention(0, False)
            with dve.Fori(0, B - 1) as b:
                experts(b, True)
                attention(b + 1, True)
            experts(B - 1, False)


def stacked(blocks):
    return np.ascontiguousarray(np.concatenate(blocks, axis=1))


def kernel(**inputs):
    import concourse.bacc as bacc
    from concourse.bass_utils import run_bass_kernel_spmd

    nc = bacc.Bacc("TRN2", target_bir_lowering=False, num_devices=1)
    a = {name: np.asarray(v) for name, v in inputs.items()}
    cos, sin = rope_tables()
    maskq, maskk = fixed_rows()

    def att0(name):
        return a[f"L0_attn_{name}"]

    def spread(v):
        return np.broadcast_to(v, (P,))

    vectors = [att0(n) for n in ("b_ln_z", "b_dt", "b_y", "b_yact", "h0", "g_sio", "g_ffn", "b_out")]
    vectors += [spread(a["L0_ffn_input_scale"]), spread(a["L0_ffn_kernel_scale"])]
    vectors += list(att0("b_fc").reshape(FF0, P)) + list(att0("b_fcact").reshape(FF0, P))
    w0 = [att0(n).T for n in ("w_ln_z", "w_dt", "w_y", "w_yact")]
    w0 += [att0(n)[P * f:P * f + P].T for n in ("w_fc", "w_fcact") for f in range(FF0)]
    w0 += [att0("w_out")[:, P * f:P * f + P].T for f in range(FF0)]
    partner = FEATURE ^ 1
    wq, wk = a["L1_attn_wq"], a["L1_attn_wk_up"]
    experts = np.stack([a["L1_ffn_Wg"], a["L1_ffn_Wu"],
                        a["L1_ffn_Wd"].reshape(NE, FE, P, P).transpose(0, 2, 1, 3).reshape(NE, P, FE * P)], axis=1)
    arrays = {
        "x": a["L0_attn_x"], "vecs": np.stack(vectors, axis=1), "w0_in": stacked(w0),
        "w1_in": stacked([wq[:, FEATURE], wq[:, partner], a["L1_attn_w_down"], a["L1_attn_wo"]]),
        "w1u_in": stacked([wk[:, FEATURE], wk[:, partner], a["L1_attn_wv_up"]]),
        "wf_in": experts.reshape(3 * NE, P, FE * P).transpose(1, 0, 2),
        "k8": a["L0_ffn_kernel"], "bias8": a["L0_ffn_bias"],
        "c_ident": np.eye(P, dtype=np.float32), "c_cos": cos, "c_sin": sin, "c_maskq": maskq, "c_maskk": maskk}
    arrays = {name: np.ascontiguousarray(v) for name, v in arrays.items()}
    args = [nc.dram_tensor(n, v.shape, mybir.dt.from_np(v.dtype), kind="ExternalInput").ap() for n, v in arrays.items()]
    y = nc.dram_tensor("y", (B, T, P), F32, kind="ExternalOutput").ap()
    build(nc, *args, y)
    r = run_bass_kernel_spmd(nc, [arrays], core_ids=[0])
    return r.results[0]["y"]
```
